# Optimizing a Trainium2 kernel written in Bass

```python
import numpy as np
import jax
import jax.numpy as jnp

def _softmax(x, axis=-1):
    return jax.nn.softmax(x, axis=axis)

def _gelu(x):
    return jax.nn.gelu(x, approximate=True)

def _silu(x):
    return jax.nn.silu(x)

def _sigmoid(x):
    return jax.nn.sigmoid(x)

def _layernorm(x, axis=-1, eps=1e-05):
    m = jnp.mean(x, axis=axis, keepdims=True)
    v = jnp.var(x, axis=axis, keepdims=True)
    return (x - m) / jnp.sqrt(v + eps)

def _scatter_add(tgt, idx, src, axis=0):
    return tgt.at[idx].add(src)

def _segment_sum(src, seg, n):
    return jax.ops.segment_sum(src, seg, n)
kernel_name = 'mk_macaron_d1_jaxref_r8_ae5a44'

def setup_inputs(seed: int=0):
    np.random.seed(seed)
    _w = jnp.asarray

    def _L0_attn_setup():
        import jax, jax.numpy as jnp
        import numpy as np
        B, T, D = (2, 256, 128)
        H = 16
        HD = D // H
        DL = 64
        NR = 64
        EPS = 1.1920929e-07

        def _rms_norm(x, w):
            ms = jnp.mean(jnp.square(x), axis=-1, keepdims=True)
            return x * jax.lax.rsqrt(ms + EPS) * w
        key = jax.random.key(seed)
        ks = jax.random.split(key, 10)
        s = 0.02
        return {'x': jax.random.normal(ks[0], (B, T, D), dtype=jnp.float32), 'W_DQ': jax.random.normal(ks[1], (DL, HD), dtype=jnp.float32) * s, 'W_UQ': jax.random.normal(ks[2], (HD, DL), dtype=jnp.float32) * s, 'W_DKV': jax.random.normal(ks[3], (2 * DL, HD), dtype=jnp.float32) * s, 'W_UKV': jax.random.normal(ks[4], (2 * HD, 2 * DL), dtype=jnp.float32) * s, 'W_QR': jax.random.normal(ks[5], (NR, HD), dtype=jnp.float32) * s, 'W_KR': jax.random.normal(ks[6], (NR, HD), dtype=jnp.float32) * s, 'W_O': jax.random.normal(ks[7], (HD, HD), dtype=jnp.float32) * s, 'q_norm_w': jnp.ones((HD,), dtype=jnp.float32), 'k_norm_w': jnp.ones((HD,), dtype=jnp.float32)}
    _L0_attn_in = _L0_attn_setup()

    def _L0_ffn_setup():
        import jax, jax.numpy as jnp
        import numpy as np
        DIM = 128
        DEPTH = 2
        HEADS = 8
        DIM_HEAD = 64
        WINDOW = 64
        INNER = HEADS * DIM_HEAD
        HID = int(DIM * 4 * 2 / 3)
        B, N = (2, 1024)
        QK_SCALE = 8.0

        def shift_token(t):
            t1, t2 = jnp.split(t, 2, axis=-1)
            t2 = jnp.pad(t2, ((0, 0), (1, 0), (0, 0)))[:, :-1]
            return jnp.concatenate([t1, t2], axis=-1)

        def l2norm(t):
            return t / jnp.clip(jnp.linalg.norm(t, axis=-1, keepdims=True), 1e-12)

        def rotate_half(x):
            x1, x2 = jnp.split(x, 2, axis=-1)
            return jnp.concatenate([-x2, x1], axis=-1)

        def rotary_xpos(q, k):
            n = q.shape[-2]
            half_idx = jnp.arange(0, DIM_HEAD, 2, dtype=jnp.float32)
            inv_freq = 1.0 / 10000.0 ** (half_idx / DIM_HEAD)
            t = jnp.arange(n, dtype=jnp.float32)
            freqs = t[:, None] * inv_freq[None, :]
            freqs = jnp.concatenate([freqs, freqs], axis=-1)
            base = (half_idx + 0.4 * DIM_HEAD) / (1.4 * DIM_HEAD)
            power = (t - n // 2) / float(WINDOW // 2)
            scale = base[None, :] ** power[:, None]
            scale = jnp.concatenate([scale, scale], axis=-1)
            cos, sin = (jnp.cos(freqs), jnp.sin(freqs))
            q = q * cos * scale + rotate_half(q) * sin * scale
            k = k * cos / scale + rotate_half(k) * sin / scale
            return (q, k)

        def local_attention(q, k, v):
            b, h, n, d = q.shape
            w = n // WINDOW
            bq = q.reshape(b, h, w, WINDOW, d) * QK_SCALE
            bk = k.reshape(b, h, w, WINDOW, d)
            bv = v.reshape(b, h, w, WINDOW, d)

            def look_around(t):
                p = jnp.pad(t, ((0, 0), (0, 0), (1, 0), (0, 0), (0, 0)))
                return jnp.concatenate([p[:, :, :w], p[:, :, 1:]], axis=3)
            bk, bv = (look_around(bk), look_around(bv))
            bt = jnp.arange(n).reshape(w, WINDOW)
            btp = jnp.pad(bt, ((1, 0), (0, 0)), constant_values=-1)
            btk = jnp.concatenate([btp[:w], btp[1:]], axis=1)
            sim = jnp.einsum('bhwid,bhwjd->bhwij', bq, bk)
            i = bt[:, :, None]
            j = btk[:, None, :]
            mask = (i < j) | (i > j + WINDOW) | (j == -1)
            sim = jnp.where(mask, -jnp.finfo(sim.dtype).max, sim)
            attn = jax.nn.softmax(sim, axis=-1)
            out = jnp.einsum('bhwij,bhwjd->bhwid', attn, bv)
            return out.reshape(b, h, n, d)

        def _layer(x, wqkv, qs, ksc, wo, lg, lb, w1, b1, w2, b2):
            b, n, _ = x.shape
            h = shift_token(x)
            qkv = h @ wqkv
            q, k, v = jnp.split(qkv, 3, axis=-1)
            to_heads = lambda t: t.reshape(b, n, HEADS, DIM_HEAD).transpose(0, 2, 1, 3)
            q, k, v = (to_heads(q), to_heads(k), to_heads(v))
            q = l2norm(q) * qs
            k = l2norm(k) * ksc
            q, k = rotary_xpos(q, k)
            o = local_attention(q, k, v)
            o = o.transpose(0, 2, 1, 3).reshape(b, n, INNER)
            x = x + o @ wo
            h = shift_token(x)
            mu = h.mean(-1, keepdims=True)
            var = h.var(-1, keepdims=True)
            h = (h - mu) / jnp.sqrt(var + 1e-05) * lg + lb
            h = h @ w1 + b1
            a, g = jnp.split(h, 2, axis=-1)
            h = a * jax.nn.gelu(g, approximate=False)
            x = x + h @ w2 + b2
            return x
        key = jax.random.key(seed)
        ks = jax.random.split(key, 6)
        return {'x': jax.random.normal(ks[0], (B, N, DIM), jnp.float32), 'wqkv': jax.random.normal(ks[1], (DEPTH, DIM, 3 * INNER), jnp.float32) * 0.02, 'q_scale': jnp.ones((DEPTH, DIM_HEAD), jnp.float32), 'k_scale': jnp.ones((DEPTH, DIM_HEAD), jnp.float32), 'wo': jax.random.normal(ks[2], (DEPTH, INNER, DIM), jnp.float32) * 0.02, 'ln_g': jnp.ones((DEPTH, DIM), jnp.float32), 'ln_b': jnp.zeros((DEPTH, DIM), jnp.float32), 'w1': jax.random.normal(ks[3], (DEPTH, DIM, 2 * HID), jnp.float32) * 0.02, 'b1': jnp.zeros((DEPTH, 2 * HID), jnp.float32), 'w2': jax.random.normal(ks[4], (DEPTH, HID, DIM), jnp.float32) * 0.02, 'b2': jnp.zeros((DEPTH, DIM), jnp.float32)}
    _L0_ffn_in = _L0_ffn_setup()
    _d = {'L0_attn_x': _L0_attn_in['x'], 'L0_attn_W_DQ': _L0_attn_in['W_DQ'], 'L0_attn_W_UQ': _L0_attn_in['W_UQ'], 'L0_attn_W_DKV': _L0_attn_in['W_DKV'], 'L0_attn_W_UKV': _L0_attn_in['W_UKV'], 'L0_attn_W_QR': _L0_attn_in['W_QR'], 'L0_attn_W_KR': _L0_attn_in['W_KR'], 'L0_attn_W_O': _L0_attn_in['W_O'], 'L0_attn_q_norm_w': _L0_attn_in['q_norm_w'], 'L0_attn_k_norm_w': _L0_attn_in['k_norm_w'], 'L0_ffn_wqkv': _L0_ffn_in['wqkv'], 'L0_ffn_q_scale': _L0_ffn_in['q_scale'], 'L0_ffn_k_scale': _L0_ffn_in['k_scale'], 'L0_ffn_wo': _L0_ffn_in['wo'], 'L0_ffn_ln_g': _L0_ffn_in['ln_g'], 'L0_ffn_ln_b': _L0_ffn_in['ln_b'], 'L0_ffn_w1': _L0_ffn_in['w1'], 'L0_ffn_b1': _L0_ffn_in['b1'], 'L0_ffn_w2': _L0_ffn_in['w2'], 'L0_ffn_b2': _L0_ffn_in['b2']}
    _x0 = _d['L0_attn_x']
    _d['L0_attn_x'] = jax.random.normal(jax.random.fold_in(jax.random.key(seed), 1), (1, 2048, 128), dtype=_x0.dtype)
    del _x0
    return _d

def reference(L0_attn_x, L0_attn_W_DQ, L0_attn_W_UQ, L0_attn_W_DKV, L0_attn_W_UKV, L0_attn_W_QR, L0_attn_W_KR, L0_attn_W_O, L0_attn_q_norm_w, L0_attn_k_norm_w, L0_ffn_wqkv, L0_ffn_q_scale, L0_ffn_k_scale, L0_ffn_wo, L0_ffn_ln_g, L0_ffn_ln_b, L0_ffn_w1, L0_ffn_b1, L0_ffn_w2, L0_ffn_b2):

    def _L0_attn_ref(x, W_DQ, W_UQ, W_DKV, W_UKV, W_QR, W_KR, W_O, q_norm_w, k_norm_w):
        import jax, jax.numpy as jnp
        import numpy as np
        B, T, D = (2, 256, 128)
        H = 16
        HD = D // H
        DL = 64
        NR = 64
        EPS = 1.1920929e-07

        def _rms_norm(x, w):
            ms = jnp.mean(jnp.square(x), axis=-1, keepdims=True)
            return x * jax.lax.rsqrt(ms + EPS) * w
        b, t, d = x.shape
        scale = HD ** (-0.5)
        xh = x.reshape(b, t, H, HD).transpose(0, 2, 1, 3)
        c_q = jnp.einsum('bhtd,ld->bhtl', xh, W_DQ)
        q_c = jnp.einsum('bhtl,dl->bhtd', c_q, W_UQ)
        q_c_norm = _rms_norm(q_c, q_norm_w)
        q_r = jnp.einsum('bhtd,rd->bhtr', q_c_norm, W_QR)
        q = jnp.concatenate([q_c_norm, q_r], axis=-1)
        c_kv = jnp.einsum('bhtd,ld->bhtl', xh, W_DKV)
        kv = jnp.einsum('bhtl,dl->bhtd', c_kv, W_UKV)
        k_c, v_c = (kv[..., :HD], kv[..., HD:])
        k_c_norm = _rms_norm(k_c, k_norm_w)
        k_r = jnp.einsum('bhtd,rd->bhtr', xh, W_KR)
        k = jnp.concatenate([k_c_norm, k_r], axis=-1)
        scores = jnp.einsum('bhqd,bhkd->bhqk', q, k) * scale
        causal = jnp.triu(jnp.full((t, t), -jnp.inf, dtype=scores.dtype), k=1)
        attn = jax.nn.softmax(scores + causal, axis=-1)
        ctx = jnp.einsum('bhqk,bhkd->bhqd', attn, v_c)
        out = jnp.einsum('bhtd,od->bhto', ctx, W_O)
        return out.transpose(0, 2, 1, 3).reshape(b, t, d)

    def _L0_ffn_ref(x, wqkv, q_scale, k_scale, wo, ln_g, ln_b, w1, b1, w2, b2):
        import jax, jax.numpy as jnp
        import numpy as np
        DIM = 128
        DEPTH = 2
        HEADS = 8
        DIM_HEAD = 64
        WINDOW = 64
        INNER = HEADS * DIM_HEAD
        HID = int(DIM * 4 * 2 / 3)
        B, N = (2, 1024)
        QK_SCALE = 8.0

        def shift_token(t):
            t1, t2 = jnp.split(t, 2, axis=-1)
            t2 = jnp.pad(t2, ((0, 0), (1, 0), (0, 0)))[:, :-1]
            return jnp.concatenate([t1, t2], axis=-1)

        def l2norm(t):
            return t / jnp.clip(jnp.linalg.norm(t, axis=-1, keepdims=True), 1e-12)

        def rotate_half(x):
            x1, x2 = jnp.split(x, 2, axis=-1)
            return jnp.concatenate([-x2, x1], axis=-1)

        def rotary_xpos(q, k):
            n = q.shape[-2]
            half_idx = jnp.arange(0, DIM_HEAD, 2, dtype=jnp.float32)
            inv_freq = 1.0 / 10000.0 ** (half_idx / DIM_HEAD)
            t = jnp.arange(n, dtype=jnp.float32)
            freqs = t[:, None] * inv_freq[None, :]
            freqs = jnp.concatenate([freqs, freqs], axis=-1)
            base = (half_idx + 0.4 * DIM_HEAD) / (1.4 * DIM_HEAD)
            power = (t - n // 2) / float(WINDOW // 2)
            scale = base[None, :] ** power[:, None]
            scale = jnp.concatenate([scale, scale], axis=-1)
            cos, sin = (jnp.cos(freqs), jnp.sin(freqs))
            q = q * cos * scale + rotate_half(q) * sin * scale
            k = k * cos / scale + rotate_half(k) * sin / scale
            return (q, k)

        def local_attention(q, k, v):
            b, h, n, d = q.shape
            w = n // WINDOW
            bq = q.reshape(b, h, w, WINDOW, d) * QK_SCALE
            bk = k.reshape(b, h, w, WINDOW, d)
            bv = v.reshape(b, h, w, WINDOW, d)

            def look_around(t):
                p = jnp.pad(t, ((0, 0), (0, 0), (1, 0), (0, 0), (0, 0)))
                return jnp.concatenate([p[:, :, :w], p[:, :, 1:]], axis=3)
            bk, bv = (look_around(bk), look_around(bv))
            bt = jnp.arange(n).reshape(w, WINDOW)
            btp = jnp.pad(bt, ((1, 0), (0, 0)), constant_values=-1)
            btk = jnp.concatenate([btp[:w], btp[1:]], axis=1)
            sim = jnp.einsum('bhwid,bhwjd->bhwij', bq, bk)
            i = bt[:, :, None]
            j = btk[:, None, :]
            mask = (i < j) | (i > j + WINDOW) | (j == -1)
            sim = jnp.where(mask, -jnp.finfo(sim.dtype).max, sim)
            attn = jax.nn.softmax(sim, axis=-1)
            out = jnp.einsum('bhwij,bhwjd->bhwid', attn, bv)
            return out.reshape(b, h, n, d)

        def _layer(x, wqkv, qs, ksc, wo, lg, lb, w1, b1, w2, b2):
            b, n, _ = x.shape
            h = shift_token(x)
            qkv = h @ wqkv
            q, k, v = jnp.split(qkv, 3, axis=-1)
            to_heads = lambda t: t.reshape(b, n, HEADS, DIM_HEAD).transpose(0, 2, 1, 3)
            q, k, v = (to_heads(q), to_heads(k), to_heads(v))
            q = l2norm(q) * qs
            k = l2norm(k) * ksc
            q, k = rotary_xpos(q, k)
            o = local_attention(q, k, v)
            o = o.transpose(0, 2, 1, 3).reshape(b, n, INNER)
            x = x + o @ wo
            h = shift_token(x)
            mu = h.mean(-1, keepdims=True)
            var = h.var(-1, keepdims=True)
            h = (h - mu) / jnp.sqrt(var + 1e-05) * lg + lb
            h = h @ w1 + b1
            a, g = jnp.split(h, 2, axis=-1)
            h = a * jax.nn.gelu(g, approximate=False)
            x = x + h @ w2 + b2
            return x
        for l in range(DEPTH):
            x = _layer(x, wqkv[l], q_scale[l], k_scale[l], wo[l], ln_g[l], ln_b[l], w1[l], b1[l], w2[l], b2[l])
        return x
    x = L0_attn_x
    x = x + 0.5 * _L0_ffn_ref(_layernorm(x, axis=-1), L0_ffn_wqkv, L0_ffn_q_scale, L0_ffn_k_scale, L0_ffn_wo, L0_ffn_ln_g, L0_ffn_ln_b, L0_ffn_w1, L0_ffn_b1, L0_ffn_w2, L0_ffn_b2)
    x = x + _L0_attn_ref(_layernorm(x, axis=-1), L0_attn_W_DQ, L0_attn_W_UQ, L0_attn_W_DKV, L0_attn_W_UKV, L0_attn_W_QR, L0_attn_W_KR, L0_attn_W_O, L0_attn_q_norm_w, L0_attn_k_norm_w)
    x = x + 0.5 * _L0_ffn_ref(_layernorm(x, axis=-1), L0_ffn_wqkv, L0_ffn_q_scale, L0_ffn_k_scale, L0_ffn_wo, L0_ffn_ln_g, L0_ffn_ln_b, L0_ffn_w1, L0_ffn_b1, L0_ffn_w2, L0_ffn_b2)
    return x

_drawn_inputs = setup_inputs


def setup_inputs(seed=0):
    import zlib

    import numpy as np

    out = dict(_drawn_inputs(seed))
    spreads = {'L0_attn_q_norm_w': (1.0, 0.6),
     'L0_attn_k_norm_w': (1.0, 0.6),
     'L0_ffn_q_scale': (1.0, 0.6),
     'L0_ffn_k_scale': (1.0, 0.6),
     'L0_ffn_ln_g': (1.0, 0.6),
     'L0_ffn_ln_b': (0.0, 0.8),
     'L0_ffn_b1': (0.0, 0.8),
     'L0_ffn_b2': (0.0, 0.1)}
    factors = {'L0_attn_W_DQ': 8.0,
     'L0_attn_W_UQ': 26.204,
     'L0_attn_W_DKV': 8.0,
     'L0_attn_W_UKV': 8.0,
     'L0_attn_W_QR': 25.323,
     'L0_attn_W_KR': 8.0,
     'L0_attn_W_O': 8.0,
     'L0_ffn_wqkv': 3.463,
     'L0_ffn_wo': 3.438,
     'L0_ffn_w1': 5.293,
     'L0_ffn_w2': 5.209}
    for name, (base, spread) in spreads.items():
        noise = np.random.default_rng([zlib.crc32(name.encode()), seed]).standard_normal(out[name].shape)
        drawn = base * np.exp(spread * noise) if base else spread * noise
        out[name] = jnp.asarray(drawn.astype(out[name].dtype))
    for name, factor in factors.items():
        out[name] = (out[name] * factor).astype(out[name].dtype)
    return out
```

```python
import numpy as np
from contextlib import ExitStack

import concourse.bass as bass
from concourse import mybir


def macaron_kernel(nc: bass.Bass, I: dict, out: bass.AP):
    f32 = mybir.dt.float32
    bf16 = mybir.dt.bfloat16
    ALU = mybir.AluOpType
    ACT = mybir.ActivationFunctionType
    AX = mybir.AxisListType

    P = 128
    NTOK, DIM = I["L0_attn_x"].shape[1:]
    T = NTOK // P
    DEPTH = I["L0_ffn_wqkv"].shape[0]
    HEADS, DH, WIN = 8, 64, 64
    INNER = HEADS * DH
    PAIRS = HEADS // 2
    HID = I["L0_ffn_w2"].shape[1]
    HC = -(-HID // P)
    HT_ = HC * P
    G = 4
    NG = T // G
    MH, HD = 16, 8
    MG = MH // 4
    VW = 16
    LN_EPS = 1e-5
    RMS_EPS = 1.1920929e-07
    MSCALE = HD ** -0.5

    with ExitStack() as ctx:
        def sb(name, shape, dt=f32):
            return ctx.enter_context(nc.sbuf_tensor(name, shape, dt))

        def sem(name):
            return ctx.enter_context(nc.semaphore(name))

        s_mla_done = sem("mla_done")
        s_fin = sem("fin")
        s_w_zero = sem("w_zero")
        s_ln_var = sem("ln_var")
        s_layer_free = sem("layer_free")
        s_p_rsum = sem("p_rsum")
        s_ssum = sem("ssum")
        s_qk_scaled = sem("qk_scaled")
        s_rope_terms = sem("rope_terms")
        s_x_T = sem("x_T")
        s_attn_add = sem("attn_add")
        s_h_stats = sem("h_stats")
        s_h_norm = sem("h_norm")
        s_ff_out = sem("ff_out")
        s_mla_free = sem("mla_free")
        s_m_zero = sem("m_zero")
        s_m_ms = sem("m_ms")
        s_m_scaled = sem("m_scaled")
        s_qk_T = sem("qk_T")
        s_score = sem("score")
        s_kz0 = sem("kz0")
        s_score_max = sem("score_max")
        s_prob_T = sem("prob_T")
        s_qkv = sem("qkv")
        s_h_T = sem("h_T")
        s_pv = sem("pv")
        s_h_shift = sem("h_shift")
        s_hn_T = sem("hn_T")
        s_ff_up = sem("ff_up")
        s_ff_hid = sem("ff_hid")
        s_bd_u = sem("bd_u")
        s_all_in = sem("all_in")
        s_m_yT = sem("m_yT")
        s_m_proj = sem("m_proj")
        s_m_split = sem("m_split")
        s_m_QKT = sem("m_QKT")
        s_m_mT = sem("m_mT")
        s_b_score = sem("b_score")
        s_b_pv = sem("b_pv")
        s_c_T = sem("c_T")
        s_ln_rstd = sem("ln_rstd")
        s_rot_in = sem("rot_in")
        s_proj = sem("proj")
        s_p_exp = sem("p_exp")
        s_p_norm = sem("p_norm")
        s_qk_sq = sem("qk_sq")
        s_qk_rnorm = sem("qk_rnorm")
        s_rope_sum = sem("rope_sum")
        s_h_left = sem("h_left")
        s_h_right = sem("h_right")
        s_h_rstd = sem("h_rstd")
        s_ff_gelu = sem("ff_gelu")
        s_ff_down = sem("ff_down")
        s_x_bias = sem("x_bias")
        s_x_in = sem("x_in")
        s_const_in = sem("const_in")
        s_weights_in = sem("weights_in")
        s_const2 = sem("const2")
        s_bd_prod = sem("bd_prod")
        s_wqk_in = sem("wqk_in")
        s_m_sq = sem("m_sq")
        s_m_rms = sem("m_rms")
        s_m_stk = sem("m_stk")
        s_a_score = sem("a_score")
        s_o_ev = sem("o_ev")
        s_q_Tev = sem("q_Tev")
        s_k_Tev = sem("k_Tev")
        s_prob_Tev = sem("prob_Tev")
        s_v_ev = sem("v_ev")
        s_x_copy = sem("x_copy")
        s_ln_done = sem("ln_done")
        s_hn_Tev = sem("hn_Tev")
        s_bd_uev = sem("bd_uev")
        s_bd_ready = sem("bd_ready")
        s_m_yTev = sem("m_yTev")
        s_m_qst = sem("m_qst")
        s_m_kz = sem("m_kz")
        s_a_max = sem("a_max")
        s_m_parts = sem("m_parts")
        s_c_out = sem("c_out")
        s_m_mrow = sem("m_mrow")
        s_b_exp = sem("b_exp")
        s_c_ev = sem("c_ev")
        s_c_zero = sem("c_zero")
        s_stored = sem("stored")
        s_q_Tev0 = sem("q_Tev0")
        s_dve_link = sem("dve_link")

        xm = sb("xm", [P, T, DIM])
        xa = [sb("xa0", [P, T + 1, DIM]), sb("xa1", [P, T + 1, DIM])]
        wqkv = sb("wqkv", [P, DEPTH, 3 * INNER])
        wo = sb("wo", [P, DEPTH, PAIRS, DIM])
        w1 = sb("w1", [P, DEPTH, 2 * HT_])
        w2 = sb("w2", [P, DEPTH, HC, DIM])
        b1 = sb("b1", [P, DEPTH, 2 * HC])
        b2 = sb("b2", [P, DEPTH, DIM])
        lg = sb("lg", [P, DEPTH])
        lb = sb("lb", [P, DEPTH])
        qks = sb("qks", [P, DEPTH, 2, DH])
        ident = sb("ident", [P, P])
        identb = sb("identb", [P, P], bf16)
        shift = sb("shift", [P, 2, P])
        masks = sb("masks", [P, 5, P], bf16)
        wmask, cmask = masks[:, 0:3], masks[:, 3:5]
        nhalf = sb("nhalf", [P, 32])
        bd = sb("bd", [P, 4 * P])
        stat = sb("stat", [P, T, 6])
        mv = sb("mv", [P, T, 2])
        rstd = sb("rstd", [P, T])

        banks = ctx.enter_context(nc.psum_tensor("banks", [P, 8, 512], f32))
        psum = [banks[:, i, :] for i in range(8)]
        psA = [0, 1]
        BM, BC = 2, 3
        psB = [4, 6]

        ARENA = 37700
        arena = sb("arena", [P, ARENA])
        at = [0]

        def view(shape, dt=f32):
            n = int(np.prod(shape[1:])) * (4 if dt == f32 else 2) // 4
            v = arena[:, at[0]:at[0] + n]
            at[0] += n
            assert at[0] <= ARENA
            if dt != f32:
                v = v.bitcast(dt)
            names = "abcd"[:len(shape) - 1]
            if len(shape) > 2:
                v = v.rearrange(f"p ({' '.join(names)}) -> p {' '.join(names)}", **{c: s for c, s in zip(names, shape[1:])})
            return v

        rot = view([P, T, 2, 2, DH])
        rts = view([P, T, 2, 2, DH])
        xs = view([P, 2, DIM])
        hT = view([P, 2, P + 1])
        sqb = view([P, 2 * INNER])
        ss = view([P, 2, 16])
        rn = view([P, 2, 16])
        ra = view([P, 2 * INNER])
        rb = view([P, 2 * INNER])
        qk = view([P, 2 * INNER])
        va = view([P, 2, INNER])
        vm = view([P, 2, INNER])
        qbd = view([P, PAIRS, 2, P])
        kring = view([P, PAIRS, 2, 2, WIN])
        nm = view([P, 2, PAIRS])
        sm = view([P, 2, PAIRS])
        rs = view([P, 2, PAIRS])
        prob = view([P, 2, PAIRS, P])
        pT = view([P, 2, PAIRS, P])
        oT = view([P, 2, PAIRS, P])
        hb = view([P, 2, G, DIM])
        xb2 = view([P, 2, G, DIM])
        hn = view([P, 2, G, DIM])
        hnT = view([P, 2, G * P])
        gl = view([P, HC, G * P])
        hid = view([P, HC, G * P])
        fst = view([P, 2, G, 6])
        fmv = view([P, 2, G, 2])
        fve = view([P, 2, G])
        frs = view([P, 2, G])
        ffn_words = at[0]
        spare = xa[1][:, 1:, :].rearrange("p t d -> p (t d)")
        bdw = spare[:, 0:8 * P].rearrange("p (n c) -> p n c", n=8)
        bdu = spare[:, 8 * P:9 * P]
        mask_in = spare[:, 9 * P:14 * P].rearrange("p (n c) -> p n c", n=5)
        mst = spare.bitcast(bf16).rearrange("p (t c r) -> p t c r", t=T, c=2)
        at[0] = 0
        kz = view([P, MH, NTOK], bf16)
        qst = view([P, MH // 2, NTOK], bf16)
        vv = view([P, T, MH, VW])
        yT = view([P, 2, P])
        msq = view([P, 2 * P])
        mss = view([P, 2, 2 * MH])
        mrn = view([P, 2, 2 * MH])
        nb = view([P, 2 * P])
        r1 = view([P, 2 * P])
        c1 = view([P, 2 * P], bf16)
        c2 = view([P, 2 * P], bf16)
        stk = view([P, 2, MH, 8, HD], bf16)
        wqk = view([P, 2, P])
        mpart = view([P, MH, T, 4])
        nmx = view([P, MH, T])
        mr1 = view([P, 2, T, 2])
        pb = view([P, 4, 2, 512])
        cT = view([P, 512])
        rden = view([P, G, 4])
        cO = view([P, G * 4 * HD])
        mla_words = at[0]

        tick = sb("tick", [P, 1])
        bdm = sb("bdm", [P, P])

        block = ctx.enter_context(nc.Block())

        NL = 2 * DEPTH
        QS = ((0, 1, 5), (2, 3), (6,))
        KS = ((3, 5, 6), (1, 2), (0,))
        MS = 4
        NKZ = []
        for L in range(NL):
            NKZ.append((NKZ[-1] if NKZ else 0) + 1 + 2 * (L % DEPTH == 0))

        NQ = NTOK // 512
        sched = []
        s_units, v_units = [], []
        for g in range(MG + 1):
            a_list = [("A", g, k, h, c) for k in range(T) for h in range(4) for c in range(k // 4 + 1)] if g < MG else []
            b_list = []
            if g > 0:
                for q in range(NQ):
                    m = NQ * (g - 1) + q
                    b_list.append(("M", m))
                    for j in range(4 * q + 4):
                        for hp in range(2):
                            b_list.append(("S", len(s_units)))
                            s_units.append((m, j, hp))
                        if j:
                            b_list.append(("V", len(v_units)))
                            v_units.append((m, j - 1))
                    b_list.append(("V", len(v_units)))
                    v_units.append((m, 4 * q + 3))
                    b_list.append(("C", m))
            na, nb_ = len(a_list), len(b_list)
            ia = 0
            for ib, ev in enumerate(b_list):
                want = na * (ib + 1) // nb_
                sched += a_list[ia:want]
                ia = want
                sched.append(ev)
            sched += a_list[ia:]
            if g < MG:
                sched.append(("P", g))

        v_last = {m: n for n, (m, j) in enumerate(v_units)}

        @block.sync
        def _(sp):
            x_v = I["L0_attn_x"].rearrange("b (t p) d -> p (b t) d", p=P)
            for h in range(2):
                sp.dma_start(xm[:, h * T // 2:(h + 1) * T // 2, :], x_v[:, h * T // 2:(h + 1) * T // 2, :]).then_inc(s_x_in, 16)
            sp.dma_start(ident[:], I["c_ident"]).then_inc(s_const_in, 16)
            sp.dma_start(shift[:], I["c_shift"]).then_inc(s_const_in, 16)
            sp.dma_start(mask_in, I["c_masks"]).then_inc(s_const_in, 16)
            sp.dma_start(bdm[:], I["c_bdmask"]).then_inc(s_const_in, 16)
            sp.dma_start(wqkv[:], I["L0_ffn_wqkv"].rearrange("l k n -> k l n")).then_inc(s_const_in, 16)
            for l in range(DEPTH):
                sp.dma_start(wo[:, l], I["L0_ffn_wo"][l].rearrange("(c k) n -> k c n", k=P)).then_inc(s_const_in, 16)
            for f in range(2):
                if f:
                    sp.wait_ge(s_mla_done, 1)
                sp.dma_start(rot[:], I["c_rot"]).then_inc(s_rot_in, 16)
            sp.wait_ge(s_fin, 1)
            sp.dma_start(out.rearrange("b (t p) d -> p (b t) d", p=P), xm[:]).then_inc(s_stored, 16)
            sp.wait_ge(s_stored, 16)

        NCONST = 16 * 7

        @block.gpsimd
        def _(pool):
            w_tail = HID - (HC - 1) * P
            nc.gpsimd.memset(w1[:], 0.0).then_inc(s_w_zero, 1)
            nc.gpsimd.memset(w2[:], 0.0).then_inc(s_w_zero, 1)
            nc.gpsimd.memset(b1[:], 0.0).then_inc(s_w_zero, 1)
            nc.gpsimd.memset(nhalf[:], -0.5).then_inc(s_w_zero, 1)
            nc.gpsimd.memset(xa[0][:, 0, :], 0.0).then_inc(s_w_zero, 1)
            nc.gpsimd.memset(xa[1][:, 0, :], 0.0).then_inc(s_w_zero, 1)
            pool.wait_ge(s_w_zero, 6)
            c = s_weights_in
            for a in range(2):
                pool.dma_start(w1[:, :, a * HT_:a * HT_ + HID], I["L0_ffn_w1"][:, :, a * HID:(a + 1) * HID].rearrange("l k n -> k l n")).then_inc(c, 16)
            for l in range(DEPTH):
                pool.dma_start(w2[:, l, 0:HC - 1, :], I["L0_ffn_w2"][l, 0:(HC - 1) * P, :].rearrange("(c k) n -> k c n", k=P)).then_inc(c, 16)
            pool.dma_start(w2[0:w_tail, :, HC - 1, :], I["L0_ffn_w2"][:, (HC - 1) * P:HID, :].rearrange("l k n -> k l n")).then_inc(c, 16)
            with nc.allow_non_contiguous_dma(reason="bias and scale vectors, a few hundred words"):
                for a in range(2):
                    for l in range(DEPTH):
                        pool.dma_start(b1[:, l, a * HC:a * HC + HC - 1],
                                       I["L0_ffn_b1"][l, a * HID:a * HID + (HC - 1) * P].rearrange("(c k) -> k c", k=P)).then_inc(c, 16)
                        pool.dma_start(b1[0:w_tail, l, a * HC + HC - 1:a * HC + HC],
                                       I["L0_ffn_b1"][l, a * HID + (HC - 1) * P:(a + 1) * HID].rearrange("(k o) -> k o", o=1)).then_inc(c, 16)
                pool.dma_start(lg[:], I["L0_ffn_ln_g"].rearrange("l k -> k l")).then_inc(c, 16)
                pool.dma_start(lb[:], I["L0_ffn_ln_b"].rearrange("l k -> k l")).then_inc(c, 16)
            pool.dma_start(b2[:], I["L0_ffn_b2"].partition_broadcast(P)).then_inc(s_const2, 16)
            pool.dma_start(qks[:, :, 0, :], I["L0_ffn_q_scale"].partition_broadcast(P)).then_inc(s_const2, 16)
            pool.dma_start(qks[:, :, 1, :], I["L0_ffn_k_scale"].partition_broadcast(P)).then_inc(s_const2, 16)
            pool.dma_start(bdw[:], I["m_factors"].rearrange("n k c -> k n c")).then_inc(s_const2, 16)

            def ln_rstd(n):
                pool.wait_ge(s_ln_var, n)
                nc.gpsimd.tensor_tensor(rstd[:], mv[:, :, 1], nhalf[:, 0:T], ALU.pow).then_inc(s_ln_rstd, 1)

            def layer(L):
                x_in = xa[L % 2]
                pool.wait_ge(s_layer_free, L + 1)
                nc.gpsimd.memset(kring[:, :, 1, 1, :], 0.0).then_inc(s_kz0, 1)
                if L % DEPTH == 0:
                    nc.gpsimd.memset(vm[:, 0, :], 0.0).then_inc(s_kz0, 1)
                    nc.gpsimd.memset(qbd[:], 0.0).then_inc(s_kz0, 1)
                for i in range(-2, T + 1):
                    k = i - 1
                    if 0 <= k < T:
                        for w in range(2):
                            K2 = 2 * (T * L + k) + w
                            pool.wait_ge(s_p_rsum, K2 + 1)
                            nc.gpsimd.tensor_tensor(prob[:, w], prob[:, w], rs[:, w, :].unsqueeze(2).to_broadcast([P, PAIRS, P]), ALU.mult).then_inc(s_p_norm, 1)
                    if 0 <= i < T:
                        K = T * L + i
                        pool.wait_ge(s_ssum, K + 1)
                        if K - 1 > 0:
                            pool.wait_ge(s_qk_scaled, K - 1)
                        nc.gpsimd.tensor_tensor(rn[:, i % 2], ss[:, i % 2], nhalf[:, 0:16], ALU.pow).then_inc(s_qk_rnorm, 1)
                        pool.wait_ge(s_rope_terms, K + 1)
                        nc.gpsimd.tensor_tensor(ra[:], ra[:], rb[:], ALU.add).then_inc(s_rope_sum, 1)
                    if 0 <= i + 2 < T:
                        k = i + 2
                        K = T * L + k
                        if K - 1 > 0:
                            pool.wait_ge(s_x_T, K - 1)
                        nc.gpsimd.tensor_copy(xs[:, k % 2], x_in[:, k + 1, :]).then_inc(s_x_copy, 1)
                for g in range(NG):
                    Gk = NG * L + g
                    if g == 0:
                        pool.wait_ge(s_attn_add, T * (L + 1))
                    tiles = x_in[:, 1 + G * g:1 + G * (g + 1), :]
                    if Gk - 1 > 0:
                        pool.wait_ge(s_h_stats, Gk - 1)
                    if Gk - 1 > 0:
                        pool.wait_ge(s_h_norm, Gk - 1)
                    nc.gpsimd.tensor_copy(hb[:, g % 2, :, 0:DIM // 2], tiles[:, :, 0:DIM // 2]).then_inc(s_h_left, 1)
                    if Gk - 1 > 0:
                        pool.wait_ge(s_ff_out, Gk - 1)
                    nc.gpsimd.tensor_tensor(xb2[:, g % 2], tiles, b2[:, L % DEPTH, :].unsqueeze(1).to_broadcast([P, G, DIM]), ALU.add).then_inc(s_x_bias, 1)
                    pool.wait_ge(s_h_stats, Gk + 1)
                    if Gk - 1 > 0:
                        pool.wait_ge(s_h_norm, Gk - 1)
                    nc.gpsimd.tensor_tensor(frs[:, g % 2], fve[:, g % 2], nhalf[:, 0:G], ALU.pow).then_inc(s_h_rstd, 1)

            ln_rstd(1)
            for L in range(DEPTH):
                layer(L)
            ln_rstd(2)
            pool.wait_ge(s_mla_free, 1)
            nc.gpsimd.memset(kz[:], 0.0).then_inc(s_m_zero, 1)
            nc.gpsimd.memset(vv[:], 0.0).then_inc(s_m_zero, 1)
            nc.gpsimd.memset(stk[:], 0.0).then_inc(s_m_zero, 1)
            nc.gpsimd.memset(mst[:], 0.0).then_inc(s_m_zero, 1)
            pool.wait_ge(s_m_zero, 4)
            nc.gpsimd.memset(vv[:, :, :, HD:HD + 1], 1.0).then_inc(s_m_zero, 1)
            nc.gpsimd.memset(stk[:, 1, :, 4, 0:3], 1.0).then_inc(s_m_zero, 1)
            pool.dma_start(wqk[:, 0, :], I["m_qn"].partition_broadcast(P)).then_inc(s_wqk_in, 16)
            pool.dma_start(wqk[:, 1, :], I["m_kn"].partition_broadcast(P)).then_inc(s_wqk_in, 16)
            for k in range(T):
                pool.wait_ge(s_m_ms, k + 1)
                if k - 1 > 0:
                    pool.wait_ge(s_m_scaled, k - 1)
                nc.gpsimd.tensor_tensor(mrn[:, k % 2], mss[:, k % 2], nhalf[:], ALU.pow).then_inc(s_m_rms, 1)
            ln_rstd(3)
            for L in range(DEPTH, NL):
                layer(L)

        @block.scalar
        def _(act):
            sc = nc.scalar

            def layer(L):
                for i in range(-1, T + 1):
                    k = i - 1
                    K = T * L + k
                    if 0 <= k < T:
                        act.wait_ge(s_qk_T, K + 1)
                        if 2 * K > 0:
                            act.wait_ge(s_score, 2 * K)
                        if k == 0:
                            act.wait_ge(s_kz0, NKZ[L])
                        qsrc = psum[3].rearrange("p (c w q) -> p c w q", c=PAIRS, w=2)
                        sc.copy(qbd[0:64, :, :, 0:64], qsrc[0:64]).then_inc(s_q_Tev0, 1)
                        sc.copy(qbd[64:128, :, :, 64:128], qsrc[64:128]).then_inc(s_q_Tev, 1)
                        for w in range(2):
                            K2 = 2 * K + w
                            act.wait_ge(s_score_max, K2 + 1)
                            if K2 - 1 > 0:
                                act.wait_ge(s_prob_T, K2 - 1)
                            for p in range(PAIRS):
                                last = sc.activation(prob[:, w, p, :], psum[5 + w][:, p * P:(p + 1) * P], ACT.Exp,
                                                     bias=nm[:, w, p:p + 1], accum_out=sm[:, w, p:p + 1])
                            last.then_inc(s_p_exp, 1)
                    Ki = T * L + i
                    if 0 <= i < T:
                        act.wait_ge(s_qkv, Ki + 1)
                        if Ki > 0:
                            act.wait_ge(s_ssum, Ki)
                        sc.activation(sqb[:, 0:INNER], psum[0], ACT.Square)
                        sc.activation(sqb[:, INNER:], psum[1], ACT.Square).then_inc(s_qk_sq, 1)
                    if 0 <= i + 1 < T:
                        n = i + 1
                        N = T * L + n
                        act.wait_ge(s_x_T, N + 1)
                        if N - 1 > 0:
                            act.wait_ge(s_qkv, N - 1)
                        if N > 0:
                            act.wait_ge(s_h_T, N)
                        if n == 0:
                            act.wait_ge(s_kz0, NKZ[L])
                        sc.copy(hT[0:64, n % 2, 0:P], psum[7][0:64, 0:P])
                        if n > 0:
                            sc.copy(hT[64:128, n % 2, 0:1], hT[64:128, (n - 1) % 2, P:P + 1])
                        else:
                            sc.copy(hT[64:128, 0, 0:1], xa[L % 2][64:128, 0, 0:1])
                        sc.copy(hT[64:128, n % 2, 1:P + 1], psum[7][64:128, 0:P]).then_inc(s_h_T, 1)
                    if 0 <= k < T:
                        for w in range(2):
                            K2 = 2 * K + w
                            act.wait_ge(s_prob_T, K2 + 1)
                            if K2 - 1 > 0:
                                act.wait_ge(s_pv, K2 - 1)
                            sc.copy(pT[:, w].rearrange("p a b -> p (a b)"), psum[5 + w]).then_inc(s_prob_Tev, 1)
                    if 0 <= i < T:
                        if 2 * Ki - 1 > 0:
                            act.wait_ge(s_pv, 2 * Ki - 1)
                        if i == 0:
                            act.wait_ge(s_kz0, NKZ[L])
                        sc.copy(va[:, i % 2], psum[2])
                        sc.copy(vm[0:64, i % 2], psum[2][0:64])
                        sc.copy(vm[64:128, (i + 1) % 2], psum[2][64:128]).then_inc(s_v_ev, 1)
                for i in range(NG + 1):
                    g = i
                    if g < NG:
                        Gk = NG * L + g
                        act.wait_ge(s_h_shift, Gk + 1)
                        if Gk - 1 > 0:
                            act.wait_ge(s_h_norm, Gk - 1)
                        if Gk - 1 > 0:
                            act.wait_ge(s_h_stats, Gk - 1)
                        sc.copy(hb[:, g % 2, :, DIM // 2:], psum[0][:, 0:G * 64].rearrange("p (t d) -> p t d", t=G)).then_inc(s_h_right, 1)
                        act.wait_ge(s_hn_T, Gk + 1)
                        if HC * 2 * (Gk - 1) > 0:
                            act.wait_ge(s_ff_up, HC * 2 * (Gk - 1))
                        sc.activation(hnT[:, g % 2], psum[1], ACT.Identity, bias=lb[:, L % DEPTH:L % DEPTH + 1],
                                      scale=lg[:, L % DEPTH:L % DEPTH + 1]).then_inc(s_hn_Tev, 1)
                    g = i - 1
                    if g >= 0:
                        Gk = NG * L + g
                        for h in range(HC):
                            act.wait_ge(s_ff_up, HC * 2 * Gk + 2 * h + 1)
                            if Gk > 0:
                                act.wait_ge(s_ff_hid, HC * (Gk - 1) + h + 1)
                            sc.activation(gl[:, h], psum[2 + 2 * h], ACT.Gelu,
                                          bias=b1[:, L % DEPTH, HC + h:HC + h + 1]).then_inc(s_ff_gelu, 1)

            def bd_maps():
                act.wait_ge(s_bd_u, 1)
                sc.copy(bdu, psum[6][:, 0:P]).then_inc(s_bd_uev, 1)

            act.wait_ge(s_all_in, 1)
            bd_maps()
            for L in range(DEPTH):
                layer(L)
            act.wait_ge(s_m_zero, 6)
            for i in range(T + 1):
                k = i
                if k < T:
                    act.wait_ge(s_m_yT, k + 1)
                    if k - 1 > 0:
                        act.wait_ge(s_m_proj, k - 1)
                    sc.copy(yT[:, k % 2], psum[0][:, 0:P]).then_inc(s_m_yTev, 1)
                    act.wait_ge(s_m_proj, k + 1)
                    if k > 0:
                        act.wait_ge(s_m_ms, k)
                    sc.activation(msq[:], psum[1][:, 0:2 * P], ACT.Square)
                    sc.copy(vv[:, k, :, 0:HD], psum[1][:, 3 * P:].rearrange("p (h d) -> p h d", h=MH)).then_inc(s_m_sq, 1)
                    act.wait_ge(s_m_split, 3 * k + 1)
                    if 16 * k > 0:
                        act.wait_ge(s_m_QKT, 16 * k)
                    nbq = nb[:, 0:P].rearrange("p (h d) -> p h d", h=MH)
                    nbk = nb[:, P:].rearrange("p (h d) -> p h d", h=MH)
                    c1q, c1k = (c1[:, a * P:(a + 1) * P].rearrange("p (h d) -> p h d", h=MH) for a in range(2))
                    c2q, c2k = (c2[:, a * P:(a + 1) * P].rearrange("p (h d) -> p h d", h=MH) for a in range(2))
                    r1q, r1k = (r1[:, a * P:(a + 1) * P].rearrange("p (h d) -> p h d", h=MH) for a in range(2))
                    for s in QS[0]:
                        sc.copy(stk[:, 0, :, s, :], c1q)
                    for s in KS[0]:
                        last = sc.copy(stk[:, 1, :, s, :], c1k)
                    last.then_inc(s_m_stk, 1)
                    act.wait_ge(s_m_split, 3 * k + 2)
                    for s in QS[1]:
                        sc.copy(stk[:, 0, :, s, :], c2q)
                    for s in KS[1]:
                        last = sc.copy(stk[:, 1, :, s, :], c2k)
                    last.then_inc(s_m_stk, 1)
                    act.wait_ge(s_m_split, 3 * k + 3)
                    for s in QS[2]:
                        sc.copy(stk[:, 0, :, s, :], r1q)
                    for s in KS[2]:
                        last = sc.copy(stk[:, 1, :, s, :], r1k)
                    last.then_inc(s_m_stk, 1)
                    act.wait_ge(s_m_QKT, 16 * k + 16)
                    sc.copy(qst[:, :, k * P:(k + 1) * P], psum[2].bitcast(bf16).rearrange("p (c t) -> p c t", c=MH // 2)).then_inc(s_m_qst, 1)

            for ev, n, *_ in sched:
                if ev == "M":
                    g, q = divmod(n, NQ)
                    act.wait_ge(s_m_mT, n + 1)
                    src = psum[BM].bitcast(bf16).rearrange("p (t c q) -> p c t q", t=G, c=2)
                    for r in (8 * MS, 64 + 8 * MS):
                        last = sc.copy(qst[r:r + HD, 2 * g:2 * g + 2, 512 * q:512 * (q + 1)].rearrange("p c (t q) -> p c t q", t=G),
                                       src[r:r + HD])
                    last.then_inc(s_m_mrow, 1)
                elif ev == "S":
                    m, j, hp = s_units[n]
                    w = 512 - max(0, P * (j - 4 * (m % NQ)))
                    act.wait_ge(s_b_score, n + 1)
                    if n // 2 - 1 > 0:
                        act.wait_ge(s_b_pv, n // 2 - 1)
                    sc.activation(pb[:, n % 4, :, 0:w], banks[:, psB[n % 2]:psB[n % 2] + 2, 0:w], ACT.Exp).then_inc(s_b_exp, 1)
                elif ev == "C":
                    act.wait_ge(s_b_pv, v_last[n] + 1)
                    act.wait_ge(s_c_T, n)
                    sc.copy(cT[:], psum[BC]).then_inc(s_c_ev, 1)
            for L in range(DEPTH, NL):
                layer(L)

        @block.vector
        def _(dve):
            ve = nc.vector
            own = [0]

            def link(ins):
                own[0] += 1
                ins.then_inc(s_dve_link, 1)
                dve.wait_ge(s_dve_link, own[0])

            def layer_norm(n, dst):
                for t in range(T):
                    last = ve.bn_stats(stat[:, t, :], xm[:, t, :])
                link(last)
                for t in range(T):
                    last = ve.bn_aggr(mv[:, t, :], stat[:, t, :])
                link(last)
                ve.tensor_scalar(mv[:, :, 1], mv[:, :, 1], LN_EPS, None, ALU.add).then_inc(s_ln_var, 1)
                dve.wait_ge(s_ln_var, n)
                dve.wait_ge(s_ln_rstd, n)
                for t in range(T):
                    last = ve.tensor_scalar(dst[:, t + 1, :], xm[:, t, :], mv[:, t, 0:1], rstd[:, t:t + 1], ALU.subtract, ALU.mult)
                last.then_inc(s_ln_done, 1)
                dve.wait_ge(s_ln_done, n)

            def layer(L):
                l = L % DEPTH
                x_in, x_out = xa[L % 2], xa[(L + 1) % 2]
                dve.wait_ge(s_rot_in, 16 * (L // DEPTH + 1))
                for t in range(T):
                    s = qks[:, l]
                    ve.tensor_tensor(rts[:, t, 0], rot[:, t, 0], s, ALU.mult)
                    ve.tensor_tensor(rts[:, t, 1, :, 0:32], rot[:, t, 1, :, 0:32], s[:, :, 32:64], ALU.mult)
                    last = ve.tensor_tensor(rts[:, t, 1, :, 32:64], rot[:, t, 1, :, 32:64], s[:, :, 0:32], ALU.mult)
                link(last)
                ve.memset(tick[:], 0.0).then_inc(s_layer_free, 1)
                dve.wait_ge(s_layer_free, L + 1)
                for i in range(0, T + 2):
                    k = i - 1
                    K = T * L + k
                    if 0 <= k < T:
                        dve.wait_ge(s_qk_T, K + 1)
                        if 2 * K > 0:
                            dve.wait_ge(s_score, 2 * K)
                        if k == 0:
                            dve.wait_ge(s_kz0, NKZ[L])
                        ve.tensor_copy(kring[:, :, :, k % 2, :], psum[4].rearrange("p (c h q) -> p c h q", c=PAIRS, h=2)).then_inc(s_k_Tev, 1)
                    if 0 <= i - 2 < T:
                        dve.wait_ge(s_proj, T * L + i - 2 + 1)
                        xt = x_in[:, i - 1, :]
                        ve.tensor_tensor(xt, psum[7][:, 0:DIM], xt, ALU.add).then_inc(s_attn_add, 1)
                    if 0 <= k < T:
                        for w in range(2):
                            K2 = 2 * K + w
                            dve.wait_ge(s_score, K2 + 1)
                            if K2 - 1 > 0:
                                dve.wait_ge(s_p_exp, K2 - 1)
                            ve.tensor_reduce(nm[:, w, :], psum[5 + w].rearrange("p (c k) -> p c k", c=PAIRS), AX.X, ALU.max, negate=True).then_inc(s_score_max, 1)
                        for w in range(2):
                            K2 = 2 * K + w
                            dve.wait_ge(s_p_exp, K2 + 1)
                            if K2 - 1 > 0:
                                dve.wait_ge(s_p_norm, K2 - 1)
                            ve.reciprocal(rs[:, w, :], sm[:, w, :]).then_inc(s_p_rsum, 1)
                    Ki = T * L + i
                    if 0 <= i < T:
                        dve.wait_ge(s_qk_sq, Ki + 1)
                        if Ki - 1 > 0:
                            dve.wait_ge(s_qk_rnorm, Ki - 1)
                        link(ve.tensor_reduce(ss[:, i % 2, :], sqb[:].rearrange("p (h d) -> p h d", h=16), AX.X, ALU.add))
                        ve.tensor_scalar(ss[:, i % 2, :], ss[:, i % 2, :], 1e-24, None, ALU.max).then_inc(s_ssum, 1)
                        if Ki > 0:
                            dve.wait_ge(s_qk_scaled, Ki)
                        for a in range(2):
                            src = psum[a].rearrange("p (h d) -> p h d", h=HEADS)
                            o1 = ra[:, a * INNER:(a + 1) * INNER].rearrange("p (h d) -> p h d", h=HEADS)
                            o2 = rb[:, a * INNER:(a + 1) * INNER].rearrange("p (h d) -> p h d", h=HEADS)
                            tc = rts[:, i, 0, a, :].unsqueeze(1).to_broadcast([P, HEADS, DH])
                            ve.tensor_tensor(o1, src, tc, ALU.mult)
                            ts = rts[:, i, 1, a, :].unsqueeze(1).to_broadcast([P, HEADS, DH])
                            ve.tensor_tensor(o2[:, :, 0:32], src[:, :, 32:64], ts[:, :, 0:32], ALU.mult)
                            last = ve.tensor_tensor(o2[:, :, 32:64], src[:, :, 0:32], ts[:, :, 32:64], ALU.mult)
                        last.then_inc(s_rope_terms, 1)
                    if 0 <= k < T:
                        for w in range(2):
                            K2 = 2 * K + w
                            dve.wait_ge(s_pv, K2 + 1)
                            if K - 1 > 0:
                                dve.wait_ge(s_proj, K - 1)
                            src = psum[3 + w].rearrange("p (c q) -> p c q", c=PAIRS)
                            ve.tensor_copy(oT[0:64, k % 2, :, 64 * w:64 * w + 64], src[0:64, :, 0:64])
                            ve.tensor_copy(oT[64:128, k % 2, :, 64 * w:64 * w + 64], src[64:128, :, 64:128]).then_inc(s_o_ev, 1)
                    if 0 <= i < T:
                        dve.wait_ge(s_rope_sum, Ki + 1)
                        dve.wait_ge(s_qk_rnorm, Ki + 1)
                        if Ki > 0:
                            dve.wait_ge(s_qk_T, Ki)
                        ve.tensor_tensor(qk[:].rearrange("p (h d) -> p h d", h=16), ra[:].rearrange("p (h d) -> p h d", h=16),
                                         rn[:, i % 2, :].unsqueeze(2).to_broadcast([P, 16, DH]), ALU.mult).then_inc(s_qk_scaled, 1)
                for i in range(NG + 2):
                    g = i
                    if g < NG:
                        Gk = NG * L + g
                        dve.wait_ge(s_h_left, Gk + 1)
                        dve.wait_ge(s_h_right, Gk + 1)
                        if Gk - 1 > 0:
                            dve.wait_ge(s_h_rstd, Gk - 1)
                        for t in range(G):
                            last = ve.bn_stats(fst[:, g % 2, t, :], hb[:, g % 2, t, :])
                        link(last)
                        for t in range(G):
                            last = ve.bn_aggr(fmv[:, g % 2, t, :], fst[:, g % 2, t, :])
                        link(last)
                        ve.tensor_scalar(fve[:, g % 2, :], fmv[:, g % 2, :, 1], LN_EPS, None, ALU.add).then_inc(s_h_stats, 1)
                        dve.wait_ge(s_h_rstd, Gk + 1)
                        if Gk - 1 > 0:
                            dve.wait_ge(s_hn_T, Gk - 1)
                        for t in range(G):
                            last = ve.tensor_scalar(hn[:, g % 2, t, :], hb[:, g % 2, t, :], fmv[:, g % 2, t, 0:1], frs[:, g % 2, t:t + 1], ALU.subtract, ALU.mult)
                        last.then_inc(s_h_norm, 1)
                    g = i - 1
                    if 0 <= g < NG:
                        Gk = NG * L + g
                        for h in range(HC):
                            dve.wait_ge(s_ff_gelu, HC * Gk + h + 1)
                            dve.wait_ge(s_ff_up, HC * 2 * Gk + 2 * h + 2)
                            if Gk > 0:
                                dve.wait_ge(s_ff_down, Gk)
                            ve.scalar_tensor_tensor(hid[:, h], psum[3 + 2 * h], b1[:, l, h:h + 1], gl[:, h], ALU.add, ALU.mult).then_inc(s_ff_hid, 1)
                        dve.wait_ge(s_ff_down, Gk + 1)
                        dve.wait_ge(s_x_bias, Gk + 1)
                        ve.tensor_tensor(x_out[:, 1 + G * g:1 + G * (g + 1), :], psum[0].rearrange("p (t d) -> p t d", t=G), xb2[:, g % 2], ALU.add).then_inc(s_ff_out, 1)

            def half_add(n):
                dve.wait_ge(s_ff_out, NG * DEPTH * n)
                last = ve.scalar_tensor_tensor(xm[:], xa[0][:, 1:, :], 0.5, xm[:], ALU.mult, ALU.add)
                return last

            dve.wait_ge(s_x_in, 32)
            dve.wait_ge(s_const_in, NCONST)
            dve.wait_ge(s_weights_in, 16 * 15)
            dve.wait_ge(s_const2, 64)
            dve.wait_ge(s_w_zero, 6)
            dve.wait_ge(s_rot_in, 16)
            ve.tensor_copy(identb[:], ident[:])
            ve.tensor_copy(masks[:], mask_in)
            ve.memset(tick[:], 0.0).then_inc(s_all_in, 1)
            dve.wait_ge(s_all_in, 1)
            dve.wait_ge(s_bd_prod, 1)
            for m in range(4):
                last = ve.tensor_tensor(bd[:, m * P:(m + 1) * P], psum[7][:, m * P:(m + 1) * P], bdm[:], ALU.mult)
            last.then_inc(s_bd_ready, 1)
            layer_norm(1, xa[0])
            for L in range(DEPTH):
                layer(L)
            link(half_add(1))
            ve.memset(tick[:], 0.0).then_inc(s_mla_free, 1)
            dve.wait_ge(s_mla_free, 1)
            layer_norm(2, xa[0])
            ve.memset(psum[BC], 0.0).then_inc(s_c_zero, 1)
            dve.wait_ge(s_wqk_in, 32)
            link(ve.tensor_scalar(wqk[:, 0, :], wqk[:, 0, :], MSCALE, None, ALU.mult))
            dve.wait_ge(s_m_zero, 6)
            for k in range(T):
                dve.wait_ge(s_m_sq, k + 1)
                if k - 1 > 0:
                    dve.wait_ge(s_m_rms, k - 1)
                link(ve.tensor_reduce(mss[:, k % 2, :], msq[:].rearrange("p (h d) -> p h d", d=HD), AX.X, ALU.add))
                ve.tensor_scalar(mss[:, k % 2, :], mss[:, k % 2, :], 1.0 / HD, RMS_EPS, ALU.mult, ALU.add).then_inc(s_m_ms, 1)
                dve.wait_ge(s_m_rms, k + 1)
                if 3 * k > 0:
                    dve.wait_ge(s_m_stk, 3 * k)
                link(ve.tensor_tensor(nb[:].rearrange("p (h d) -> p h d", d=HD), psum[1][:, 0:2 * P].rearrange("p (h d) -> p h d", d=HD),
                                      mrn[:, k % 2, :].unsqueeze(2).to_broadcast([P, 2 * MH, HD]), ALU.mult))
                ve.tensor_tensor(nb[:], nb[:], wqk[:].rearrange("p a b -> p (a b)"), ALU.mult).then_inc(s_m_scaled, 1)
                dve.wait_ge(s_m_scaled, k + 1)
                link(ve.tensor_tensor(nb[:, P:], psum[1][:, 2 * P:3 * P], nb[:, P:], ALU.add))
                ve.tensor_copy(c1[:], nb[:]).then_inc(s_m_split, 1)
                dve.wait_ge(s_m_split, 3 * k + 1)
                link(ve.tensor_tensor(r1[:], nb[:], c1[:], ALU.subtract))
                ve.tensor_copy(c2[:], r1[:]).then_inc(s_m_split, 1)
                dve.wait_ge(s_m_split, 3 * k + 2)
                ve.tensor_tensor(r1[:], r1[:], c2[:], ALU.subtract).then_inc(s_m_split, 1)
                dve.wait_ge(s_m_split, 3 * k + 3)
                dve.wait_ge(s_m_QKT, 16 * k + 16)
                src = psum[3].bitcast(bf16).rearrange("p (c t) -> p c t", c=MH // 2)
                kzv = kz[:, :, k * P:(k + 1) * P].rearrange("p (c a) t -> p a c t", a=2)
                ve.tensor_copy(kzv[0:64, 0], src[0:64])
                ve.tensor_copy(kzv[64:128, 1], src[64:128]).then_inc(s_m_kz, 1)
            nu = 0
            for ev, g, *r in sched:
                if ev == "A":
                    k, h, cch = r
                    n = min(512, P * (k + 1) - 512 * cch)
                    dve.wait_ge(s_a_score, nu + 1)
                    ve.tensor_reduce(mpart[:, 4 * g + h, k, cch:cch + 1], psum[psA[nu % 2]][:, 0:n], AX.X, ALU.max).then_inc(s_a_max, 1)
                    nu += 1
                elif ev == "P":
                    dve.wait_ge(s_a_max, nu)
                    for q in range(NQ):
                        kk = slice(4 * q, 4 * q + 4)
                        last = ve.tensor_reduce(nmx[:, 4 * g:4 * g + 4, kk], mpart[:, 4 * g:4 * g + 4, kk, 0:q + 1], AX.X, ALU.max, negate=True)
                    link(last)
                    src = nmx[:, 4 * g:4 * g + 4, :].rearrange("p (c a) t -> p a t c", a=2)
                    if NQ * g > 0:
                        dve.wait_ge(s_m_mT, NQ * g)
                    for a in range(2):
                        dst = mst[:, :, :, 64 * a + 8 * MS:64 * a + 8 * MS + 3]
                        link(ve.tensor_copy(dst[:, :, :, 0], src[:, a]))
                        link(ve.tensor_tensor(mr1[:, a], src[:, a], dst[:, :, :, 0], ALU.subtract))
                        link(ve.tensor_copy(dst[:, :, :, 1], mr1[:, a]))
                        link(ve.tensor_tensor(mr1[:, a], mr1[:, a], dst[:, :, :, 1], ALU.subtract))
                        last = ve.tensor_copy(dst[:, :, :, 2], mr1[:, a])
                    last.then_inc(s_m_parts, 1)
                    dve.wait_ge(s_m_parts, g + 1)
                elif ev == "C":
                    m = g
                    hg, q = divmod(m, NQ)
                    dve.wait_ge(s_c_T, m + 1)
                    src = psum[BM].rearrange("p (t h c) -> p t h c", t=G, h=4)
                    link(ve.reciprocal(rden[:], src[:, :, :, HD]))
                    link(ve.tensor_tensor(cO[:].rearrange("p (t h d) -> p t h d", t=G, h=4), src[:, :, :, 0:HD],
                                          rden[:].unsqueeze(3).to_broadcast([P, G, 4, HD]), ALU.mult))
                    xt = xm[:, G * q:G * (q + 1), 4 * HD * hg:4 * HD * (hg + 1)]
                    ve.tensor_tensor(xt, xt, cO[:].rearrange("p (t d) -> p t d", t=G), ALU.add).then_inc(s_c_out, 1)
                    dve.wait_ge(s_c_out, m + 1)
            ve.memset(tick[:], 0.0).then_inc(s_mla_done, 1)
            dve.wait_ge(s_mla_done, 1)
            layer_norm(3, xa[0])
            for L in range(DEPTH, NL):
                layer(L)
            half_add(2).then_inc(s_fin, 1)

        @block.tensor
        def _(pe):
            te = nc.tensor

            def layer(L):
                l = L % DEPTH
                x_in = xa[L % 2]
                for i in range(-1, T + 2):
                    k = i - 1
                    K = T * L + k
                    if 0 <= k < T:
                        pe.wait_ge(s_qk_scaled, K + 1)
                        if 2 * K > 0:
                            pe.wait_ge(s_o_ev, 2 * K)
                        for a in range(2):
                            for p in range(PAIRS):
                                last = te.transpose(psum[3 + a][:, p * P:(p + 1) * P], qk[:, a * INNER + p * P:a * INNER + (p + 1) * P], ident[:])
                        last.then_inc(s_qk_T, 1)
                    if 0 <= i - 2 < T:
                        kk = i - 2
                        KK = T * L + kk
                        pe.wait_ge(s_o_ev, 2 * KK + 2)
                        pe.wait_ge(s_h_T, T * L + min(kk + 3, T))
                        for p in range(PAIRS):
                            last = te.matmul(psum[7][:, 0:DIM], oT[:, kk % 2, p, :], wo[:, l, p, :], start=p == 0, stop=p == PAIRS - 1)
                        last.then_inc(s_proj, 1)
                    if 0 <= k < T:
                        pe.wait_ge(s_q_Tev, K + 1)
                        pe.wait_ge(s_k_Tev, K + 1)
                        u = k % 2
                        for w in range(2):
                            K2 = 2 * K + w
                            if K2 - 1 > 0:
                                pe.wait_ge(s_prob_Tev, K2 - 1)
                            bank = psum[5 + w]
                            mask = wmask[:, 1 if w else (2 if k == 0 else 0), :].unsqueeze(1).to_broadcast([P, PAIRS, P])
                            te.matmul(bank[:], identb[:], mask, start=True, stop=False, skip_group_check=True)
                            for p in range(PAIRS):
                                flat = kring[:, p].rearrange("p h s q -> p (h s) q")
                                keys = flat[:, u:u + 3:2, :] if w else (flat[:, 0:4:3, :] if u == 0 else flat[:, 1:3, :])
                                last = te.matmul(bank[:, p * P:(p + 1) * P], qbd[:, p, w, :], keys, start=False, stop=True, skip_group_check=True)
                            last.then_inc(s_score, 1)
                    if 0 <= i < T:
                        Ki = T * L + i
                        pe.wait_ge(s_h_T, Ki + 1)
                        if Ki > 0:
                            pe.wait_ge(s_rope_terms, Ki)
                        if Ki > 0:
                            pe.wait_ge(s_v_ev, Ki)
                        for c in range(3):
                            last = te.matmul(psum[c], hT[:, i % 2, 0:P], wqkv[:, l, c * INNER:(c + 1) * INNER], start=True, stop=True)
                        last.then_inc(s_qkv, 1)
                    if 0 <= i + 1 < T:
                        n = i + 1
                        N = T * L + n
                        pe.wait_ge(s_x_copy, N + 1)
                        if N > 0:
                            pe.wait_ge(s_h_T, N)
                        if T * L + max(n - 2, 0) > 0:
                            pe.wait_ge(s_attn_add, T * L + max(n - 2, 0))
                        if n == 0:
                            pe.wait_ge(s_ln_done, 1)
                        te.transpose(psum[7][:, 0:P], xs[:, n % 2], ident[:]).then_inc(s_x_T, 1)
                    if 0 <= k < T:
                        for w in range(2):
                            pe.wait_ge(s_p_norm, 2 * K + w + 1)
                            for p in range(PAIRS):
                                last = te.transpose(psum[5 + w][:, p * P:(p + 1) * P], prob[:, w, p, :], ident[:])
                            last.then_inc(s_prob_T, 1)
                        for w in range(2):
                            pe.wait_ge(s_prob_Tev, 2 * K + w + 1)
                            pe.wait_ge(s_v_ev, K + 1)
                            v = va[:, k % 2] if w else vm[:, k % 2]
                            for p in range(PAIRS):
                                last = te.matmul(psum[3 + w][:, p * P:(p + 1) * P], v[:, p * P:(p + 1) * P], pT[:, w, p, :], start=True, stop=True)
                            last.then_inc(s_pv, 1)
                for i in range(-1, NG):
                    g = i + 1
                    if g < NG:
                        Gk = NG * L + g
                        if g == 0:
                            pe.wait_ge(s_attn_add, T * (L + 1))
                            pe.wait_ge(s_rope_terms, T * (L + 1))
                            pe.wait_ge(s_v_ev, T * (L + 1))
                            pe.wait_ge(s_o_ev, 2 * T * (L + 1))
                        if Gk - 1 > 0:
                            pe.wait_ge(s_ff_out, Gk - 1)
                        for s in range(2):
                            last = te.matmul(psum[0][:, 0:G * 64], shift[:, s], x_in[:, 1 + G * g - s:1 + G * (g + 1) - s, 64:128], start=s == 0, stop=s == 1)
                        last.then_inc(s_h_shift, 1)
                    g = i
                    if g >= 0:
                        Gk = NG * L + g
                        pe.wait_ge(s_hn_Tev, Gk + 1)
                        for h in range(HC):
                            for a, col in ((0, HT_), (1, 0)):
                                if a == 0:
                                    if Gk > 0:
                                        pe.wait_ge(s_ff_gelu, HC * (Gk - 1) + h + 1)
                                else:
                                    if Gk > 0:
                                        pe.wait_ge(s_ff_hid, HC * (Gk - 1) + h + 1)
                                te.matmul(psum[2 + 2 * h + a], w1[:, l, col + h * P:col + (h + 1) * P], hnT[:, g % 2], start=True, stop=True).then_inc(s_ff_up, 1)
                    g = i + 1
                    if g < NG:
                        Gk = NG * L + g
                        pe.wait_ge(s_h_norm, Gk + 1)
                        if Gk > 0:
                            pe.wait_ge(s_hn_Tev, Gk)
                        for t in range(G):
                            last = te.transpose(psum[1][:, t * P:(t + 1) * P], hn[:, g % 2, t, :], ident[:])
                        last.then_inc(s_hn_T, 1)
                    g = i
                    if g >= 0:
                        Gk = NG * L + g
                        pe.wait_ge(s_ff_hid, HC * (Gk + 1))
                        pe.wait_ge(s_h_right, min(Gk + 2, NG * (L + 1)))
                        for t in range(G):
                            for h in range(HC):
                                last = te.matmul(psum[0][:, t * P:(t + 1) * P], hid[:, h, t * P:(t + 1) * P], w2[:, l, h, :], start=h == 0, stop=h == HC - 1)
                        last.then_inc(s_ff_down, 1)
                pe.wait_ge(s_ff_out, NG * (L + 1))

            pe.wait_ge(s_all_in, 1)
            UQ, DQ, UK, DKV, QR, KR, UV, WO = range(8)
            te.matmul(psum[6][:, 0:P], bdw[:, UV, :], bdw[:, WO, :], start=True, stop=True).then_inc(s_bd_u, 1)
            te.matmul(psum[7][:, 0:P], bdw[:, DQ, :], bdw[:, UQ, :], start=True, stop=True)
            te.matmul(psum[7][:, P:2 * P], bdw[:, DKV, :], bdw[:, UK, :], start=True, stop=True)
            te.matmul(psum[7][:, 2 * P:3 * P], bdw[:, KR, :], bdw[:, QR, :], start=True, stop=True)
            pe.wait_ge(s_bd_uev, 1)
            te.matmul(psum[7][:, 3 * P:], bdw[:, DKV, :], bdu, start=True, stop=True).then_inc(s_bd_prod, 1)
            pe.wait_ge(s_bd_ready, 1)
            for L in range(DEPTH):
                layer(L)
            pe.wait_ge(s_ln_done, 2)
            pe.wait_ge(s_m_zero, 6)
            for k in range(T):
                if k > 0:
                    pe.wait_ge(s_m_yTev, k)
                te.transpose(psum[0][:, 0:P], xa[0][:, k + 1, :], ident[:]).then_inc(s_m_yT, 1)
                pe.wait_ge(s_m_yTev, k + 1)
                if 3 * k > 0:
                    pe.wait_ge(s_m_split, 3 * k)
                if k > 0:
                    pe.wait_ge(s_m_sq, k)
                te.matmul(psum[1], yT[:, k % 2], bd[:], start=True, stop=True).then_inc(s_m_proj, 1)
                pe.wait_ge(s_m_stk, 3 * k + 3)
                if k > 0:
                    pe.wait_ge(s_m_qst, k)
                if k > 0:
                    pe.wait_ge(s_m_kz, k)
                for a in range(2):
                    for c in range(MH // 2):
                        src = stk[:, a, 2 * c:2 * c + 2].rearrange("p h s d -> p (h s d)")
                        te.transpose(psum[2 + a].bitcast(bf16)[:, c * P:(c + 1) * P], src, identb[:]).then_inc(s_m_QKT, 1)
            pe.wait_ge(s_m_qst, T)
            pe.wait_ge(s_m_kz, T)
            nu = 0
            for ev, n, *r in sched:
                if ev == "A":
                    k, h, c = r
                    hd = 4 * n + h
                    w = min(512, P * (k + 1) - 512 * c)
                    diag = c == k // 4
                    if nu - 1 > 0:
                        pe.wait_ge(s_a_max, nu - 1)
                    bank = psum[psA[nu % 2]]
                    ins = te.matmul(bank[:, 0:w], qst[:, hd // 2, k * P:(k + 1) * P], kz[:, hd, 512 * c:512 * c + w],
                                    start=True, stop=not diag, skip_group_check=True)
                    if diag:
                        ins = te.matmul(bank[:, w - P:w], identb[:], cmask[:, 0, :], start=False, stop=True, skip_group_check=True)
                    ins.then_inc(s_a_score, 1)
                    nu += 1
                elif ev == "M":
                    pe.wait_ge(s_m_parts, n // NQ + 1)
                    pe.wait_ge(s_c_out, n)
                    for t in range(G):
                        for c in range(2):
                            last = te.transpose(psum[BM].bitcast(bf16)[:, (2 * t + c) * P:(2 * t + c + 1) * P],
                                                mst[:, G * (n % NQ) + t, c, :], identb[:])
                    last.then_inc(s_m_mT, 1)
                    pe.wait_ge(s_m_mrow, n + 1)
                elif ev == "S":
                    m, j, hp = s_units[n]
                    g, q = divmod(m, NQ)
                    lo = max(0, P * (j - 4 * q))
                    if n - 1 > 0:
                        pe.wait_ge(s_b_exp, n - 1)
                    for h2 in range(2):
                        hd = 4 * g + 2 * hp + h2
                        bank = psum[psB[n % 2] + h2]
                        diag = j >= 4 * q
                        last = te.matmul(bank[:, 0:512 - lo], kz[:, hd, j * P:(j + 1) * P], qst[:, hd // 2, 512 * q + lo:512 * (q + 1)],
                                         start=True, stop=not diag, skip_group_check=True)
                        if diag:
                            last = te.matmul(bank[:, 0:P], identb[:], cmask[:, 1, :], start=False, stop=True, skip_group_check=True)
                    last.then_inc(s_b_score, 1)
                elif ev == "V":
                    m, j = v_units[n]
                    g, q = divmod(m, NQ)
                    lo = max(0, P * (j - 4 * q))
                    pe.wait_ge(s_b_exp, 2 * n + 2)
                    if j == 0:
                        if m > 0:
                            pe.wait_ge(s_c_ev, m)
                        pe.wait_ge(s_c_zero, 1)
                    for h in range(4):
                        last = te.matmul(psum[BC][32 * h:32 * h + VW, lo:512], vv[:, j, 4 * g + h, :],
                                         pb[:, (2 * n + h // 2) % 4, h % 2, 0:512 - lo],
                                         start=j == 0, stop=j == 4 * q + 3, skip_group_check=True)
                    last.then_inc(s_b_pv, 1)
                elif ev == "C":
                    pe.wait_ge(s_c_ev, n + 1)
                    for t in range(G):
                        last = te.transpose(psum[BM][:, t * P:(t + 1) * P], cT[:, t * P:(t + 1) * P], ident[:])
                    last.then_inc(s_c_T, 1)
            pe.wait_ge(s_c_out, 16)
            pe.wait_ge(s_ln_done, 3)
            for L in range(DEPTH, NL):
                layer(L)


_DATA = ['L0_attn_x', 'L0_ffn_wqkv', 'L0_ffn_q_scale', 'L0_ffn_k_scale', 'L0_ffn_wo', 'L0_ffn_ln_g', 'L0_ffn_ln_b',
         'L0_ffn_w1', 'L0_ffn_b1', 'L0_ffn_w2', 'L0_ffn_b2']


def constants(ntok):
    P, DH, WIN, HEADS = 128, 64, 64, 8
    T = ntok // P
    c = {"c_ident": np.eye(P, dtype=np.float32)}
    sh = np.zeros((P, 2, P), np.float32)
    sh[np.arange(P - 1), 0, np.arange(1, P)] = 1
    sh[P - 1, 1, 0] = 1
    c["c_shift"] = sh
    q = np.arange(P)[:, None] % WIN
    k = np.arange(P)[None, :]
    even = np.where(k < WIN, k <= q, k >= q + WIN)
    odd = (k >= q) & (k <= q + WIN)
    first = (k < WIN) & (k <= q)
    BIG = np.float32(-1e30)
    a = np.arange(P)
    by_query, by_key = a[None, :] <= a[:, None], a[:, None] <= a[None, :]
    c["c_masks"] = np.stack([np.where(m, np.float32(0), BIG) for m in (even, odd, first, by_query, by_key)], 1)
    c["c_bdmask"] = (a[:, None] // 8 == a[None, :] // 8).astype(np.float32)
    half = np.arange(0, DH, 2, dtype=np.float32)
    inv = (1.0 / np.float32(10000.0) ** (half / np.float32(DH))).astype(np.float32)
    t = np.arange(ntok, dtype=np.float32)
    fr = (t[:, None] * inv[None, :]).astype(np.float32)
    fr = np.concatenate([fr, fr], 1).astype(np.float64)
    base = ((half + np.float32(0.4 * DH)) / np.float32(1.4 * DH)).astype(np.float32)
    power = ((t - ntok // 2) / np.float32(WIN // 2)).astype(np.float32)
    sc = base[None, :].astype(np.float64) ** power[:, None].astype(np.float64)
    sc = np.concatenate([sc, sc], 1)
    cos, sin = np.cos(fr), np.sin(fr)
    sin[:, :DH // 2] *= -1
    rot = np.stack([np.stack([cos * sc * 8.0, cos / sc], 1), np.stack([sin * sc * 8.0, sin / sc], 1)], 1)
    c["c_rot"] = rot.reshape(T, P, 2, 2, DH).transpose(1, 0, 2, 3, 4).astype(np.float32)
    return c


def kernel(**inputs):
    import concourse.bacc as _bacc
    from concourse.bass_utils import run_bass_kernel_spmd as _run

    nc = _bacc.Bacc("TRN2", target_bir_lowering=False, num_devices=1)
    a = {n: np.ascontiguousarray(inputs[n]) for n in _DATA}
    a.update(constants(a["L0_attn_x"].shape[1]))
    g = {n: np.asarray(inputs["L0_attn_" + n]) for n in ("W_DQ", "W_UQ", "W_DKV", "W_UKV", "W_QR", "W_KR", "W_O", "q_norm_w", "k_norm_w")}

    def factor(w, heads):
        w = np.tile(w, (1, heads))
        out = np.zeros((128, 128), w.dtype)
        out[:w.shape[0], :w.shape[1]] = w
        return out

    a["m_factors"] = np.stack([factor(g["W_UQ"].T, 16), factor(g["W_DQ"], 16), factor(g["W_UKV"][:8].T, 16), factor(g["W_DKV"], 16),
                               factor(g["W_QR"], 16), factor(g["W_KR"], 16), factor(g["W_UKV"][8:], 1), factor(g["W_O"].T, 16)])
    a["m_qn"] = np.tile(g["q_norm_w"], 16)
    a["m_kn"] = np.tile(g["k_norm_w"], 16)
    arrays, I = {}, {}
    for name, v in a.items():
        v = np.ascontiguousarray(v)
        arrays[name] = v
        I[name] = nc.dram_tensor(name, v.shape, mybir.dt.from_np(v.dtype), kind="ExternalInput").ap()
    out = nc.dram_tensor("out", a["L0_attn_x"].shape, mybir.dt.float32, kind="ExternalOutput").ap()
    macaron_kernel(nc, I, out)
    r = _run(nc, [arrays], core_ids=[0])
    return r.results[0]["out"]
```

```python
import numpy as np
from contextlib import ExitStack

import concourse.bass as bass
from concourse import mybir


def macaron_kernel(nc: bass.Bass, I: dict, out: bass.AP):
    f32 = mybir.dt.float32
    bf16 = mybir.dt.bfloat16
    ALU = mybir.AluOpType
    ACT = mybir.ActivationFunctionType
    AX = mybir.AxisListType

    P = 128
    NTOK, DIM = I["L0_attn_x"].shape[1:]
    T = NTOK // P
    DEPTH = I["L0_ffn_wqkv"].shape[0]
    HEADS, DH, WIN = 8, 64, 64
    INNER = HEADS * DH
    PAIRS = HEADS // 2
    HID = I["L0_ffn_w2"].shape[1]
    HC = -(-HID // P)
    HT_ = HC * P
    G = 4
    NG = T // G
    MH, HD = 16, 8
    MG = MH // 4
    VW = 16
    LN_EPS = 1e-5
    RMS_EPS = 1.1920929e-07
    MSCALE = HD ** -0.5

    with ExitStack() as ctx:
        def sb(name, shape, dt=f32):
            return ctx.enter_context(nc.sbuf_tensor(name, shape, dt))

        def sem(name):
            return ctx.enter_context(nc.semaphore(name))

        s_mla_done = sem("mla_done")
        s_fin = sem("fin")
        s_w_zero = sem("w_zero")
        s_ln_var = sem("ln_var")
        s_layer_free = sem("layer_free")
        s_ssum = sem("ssum")
        s_qk_scaled = sem("qk_scaled")
        s_rope_terms = sem("rope_terms")
        s_x_T = sem("x_T")
        s_attn_add = sem("attn_add")
        s_h_stats = sem("h_stats")
        s_h_norm = sem("h_norm")
        s_ff_out = sem("ff_out")
        s_mla_free = sem("mla_free")
        s_m_ms = sem("m_ms")
        s_q_T = sem("q_T")
        s_k_T = sem("k_T")
        s_score = sem("score")
        s_kz0 = sem("kz0")
        s_score_max = sem("score_max")
        s_prob_T = sem("prob_T")
        s_h_T = sem("h_T")
        s_pv0 = sem("pv0")
        s_pv1 = sem("pv1")
        s_h_shift = sem("h_shift")
        s_hn_T = sem("hn_T")
        s_ff_up = sem("ff_up")
        s_ff_hid = sem("ff_hid")
        s_bd_u = sem("bd_u")
        s_all_in = sem("all_in")
        s_m_yT = sem("m_yT")
        s_m_proj = sem("m_proj")
        s_m_mT = sem("m_mT")
        s_b_score = sem("b_score")
        s_b_pv = sem("b_pv")
        s_c_T = sem("c_T")
        s_ln_rstd = sem("ln_rstd")
        s_rot_in = sem("rot_in")
        s_proj = sem("proj")
        s_p_exp = sem("p_exp")
        s_p_norm = sem("p_norm")
        s_qk_sq = sem("qk_sq")
        s_qk_rnorm = sem("qk_rnorm")
        s_rope_sum = sem("rope_sum")
        s_h_left = sem("h_left")
        s_h_right = sem("h_right")
        s_h_rstd = sem("h_rstd")
        s_ff_gelu = sem("ff_gelu")
        s_ff_down = sem("ff_down")
        s_x_bias = sem("x_bias")
        s_x_in = sem("x_in")
        s_const_in = sem("const_in")
        s_weights_in = sem("weights_in")
        s_const2 = sem("const2")
        s_bd_prod = sem("bd_prod")
        s_wqk_in = sem("wqk_in")
        s_m_sq = sem("m_sq")
        s_m_rms = sem("m_rms")
        s_m_stk = sem("m_stk")
        s_a_score = sem("a_score")
        s_o_ev0 = sem("o_ev0")
        s_o_ev1 = sem("o_ev1")
        s_qk = sem("qk")
        s_v = sem("v")
        s_q_Tev = sem("q_Tev")
        s_k_Tev = sem("k_Tev")
        s_prob_Tev = sem("prob_Tev")
        s_v_ev = sem("v_ev")
        s_x_copy = sem("x_copy")
        s_ln_done = sem("ln_done")
        s_hn_Tev = sem("hn_Tev")
        s_bd_uev = sem("bd_uev")
        s_bd_ready = sem("bd_ready")
        s_m_yTev = sem("m_yTev")
        s_m_qst = sem("m_qst")
        s_m_kz = sem("m_kz")
        s_a_max = sem("a_max")
        s_m_parts = sem("m_parts")
        s_c_out = sem("c_out")
        s_m_mrow = sem("m_mrow")
        s_b_exp = sem("b_exp")
        s_c_ev = sem("c_ev")
        s_c_zero = sem("c_zero")
        s_stored = sem("stored")
        s_dve_link = sem("dve_link")
        s_kz_zero = sem("kz_zero")
        s_m_KT = sem("m_KT")
        s_m_QT = sem("m_QT")
        s_m_normed = sem("m_normed")
        s_m_part = sem("m_part")
        s_m_proj_used = sem("m_proj_used")
        s_m_sd = sem("m_sd")
        s_m_vev = sem("m_vev")
        s_m_weighted = sem("m_weighted")
        s_mst_zero = sem("mst_zero")
        s_stk_zero = sem("stk_zero")
        s_wqk_scaled = sem("wqk_scaled")

        xm = sb("xm", [P, T, DIM])
        xa = [sb("xa0", [P, T + 1, DIM]), sb("xa1", [P, T + 1, DIM])]
        wqkv = sb("wqkv", [P, DEPTH, 3 * INNER])
        wo = sb("wo", [P, DEPTH, PAIRS, DIM])
        w1 = sb("w1", [P, DEPTH, 2 * HT_])
        w2 = sb("w2", [P, DEPTH, HC, DIM])
        b1 = sb("b1", [P, DEPTH, 2 * HC])
        b2 = sb("b2", [P, DEPTH, DIM])
        lg = sb("lg", [P, DEPTH])
        lb = sb("lb", [P, DEPTH])
        qks = sb("qks", [P, DEPTH, 2, DH])
        ident = sb("ident", [P, P])
        identb = sb("identb", [P, P], bf16)
        shift = sb("shift", [P, 2, P])
        masks = sb("masks", [P, 5, P], bf16)
        wmask, cmask = masks[:, 0:3], masks[:, 3:5]
        nhalf = sb("nhalf", [P, 32])
        bd = sb("bd", [P, 4 * P])
        stat = sb("stat", [P, T, 6])
        mv = sb("mv", [P, T, 2])
        rstd = sb("rstd", [P, T])

        banks = ctx.enter_context(nc.psum_tensor("banks", [P, 8, 512], f32))
        psum = [banks[:, i, :] for i in range(8)]
        psA = [0, 1]
        BM, BC = 2, 3
        psB = [4, 6]

        ARENA = 38400
        arena = sb("arena", [P, ARENA])
        at = [0]

        def view(shape, dt=f32):
            n = int(np.prod(shape[1:])) * (4 if dt == f32 else 2) // 4
            v = arena[:, at[0]:at[0] + n]
            at[0] += n
            assert at[0] <= ARENA
            if dt != f32:
                v = v.bitcast(dt)
            names = "abcdef"[:len(shape) - 1]
            if len(shape) > 2:
                v = v.rearrange(f"p ({' '.join(names)}) -> p {' '.join(names)}", **{c: s for c, s in zip(names, shape[1:])})
            return v

        rot = view([P, T, 2, 2, DH])
        rts = view([P, T, 2, 2, DH])
        xs = view([P, 2, DIM])
        hT = view([P, 2, P + 1])
        sqb = view([P, 2 * INNER])
        ss = view([P, 2, 16])
        rn = view([P, 2, 16])
        ra = view([P, 2 * INNER])
        rb = view([P, 2 * INNER])
        qk = view([P, 2 * INNER])
        va = view([P, 2, INNER])
        vm = view([P, 2, INNER])
        qbd = view([P, PAIRS, 2, P])
        kring = view([P, PAIRS, 2, 2, WIN])
        nm = view([P, 2, PAIRS])
        sm = view([P, 2, PAIRS])
        rs = view([P, 2, PAIRS])
        prob = view([P, 2, PAIRS, P])
        pT = view([P, 2, PAIRS, P])
        oT = view([P, 2, PAIRS, P])
        hb = view([P, 2, G, DIM])
        xb2 = view([P, 2, G, DIM])
        hn = view([P, 2, G, DIM])
        hnT = view([P, 2, G * P])
        gl = view([P, HC, G * P])
        hid = view([P, HC, G * P])
        fst = view([P, 2, G, 6])
        fmv = view([P, 2, G, 2])
        fve = view([P, 2, G])
        frs = view([P, 2, G])
        ffn_words = at[0]
        spare = xa[1][:, 1:, :].rearrange("p t d -> p (t d)")
        bdw = spare[:, 0:8 * P].rearrange("p (n c) -> p n c", n=8)
        bdu = spare[:, 8 * P:9 * P]
        bdm = spare[:, 14 * P:15 * P]
        mask_in = spare[:, 9 * P:14 * P].rearrange("p (n c) -> p n c", n=5)
        yT = spare[:, 0:2 * G * P].rearrange("p (n c) -> p n c", n=2)
        mst = spare.bitcast(bf16).rearrange("p (n t c r) -> p n t c r", n=4, t=G, c=2)
        at[0] = 0
        kz = view([P, MH, NTOK], bf16)
        qst = view([P, MH // 2, NTOK], bf16)
        vv = view([P, T, MH, VW])
        shared = at[0]
        SW = MH * HD
        wqk = view([P, 2, SW])
        msq = view([P, G, 2 * SW])
        mss = view([P, G * 2 * MH])
        msd = view([P, G * 2 * MH])
        mrn = view([P, G * 2 * MH])
        mnt = view([P, G * 2 * MH])
        nb = view([P, 2, G, SW])
        stk = view([P, 2, G, MH, 8, HD], bf16)
        at[0] = shared
        mpart = view([P, MH, T, 4])
        nmx = view([P, 2, 2, G, 2])
        mr1 = view([P, 2, G, 2])
        pb = view([P, 4, 2, 512])
        cT = view([P, 512])
        rden = view([P, G, 4])
        cO = view([P, G * 4 * HD])

        tick = sb("tick", [P, 1])

        block = ctx.enter_context(nc.Block())

        NL = 2 * DEPTH
        QS = ((0, 1, 5), (2, 3), (6,))
        KS = ((3, 5, 6), (1, 2), (0,))
        MS = 4
        NKZ = []
        for L in range(NL):
            NKZ.append((NKZ[-1] if NKZ else 0) + 1 + 2 * (L % DEPTH == 0))

        NQ = NTOK // 512
        CH = [(g, q) for g in range(MG) for q in (range(NQ) if g % 2 == 0 else reversed(range(NQ)))]
        A_PER_S, M_LAG, C_LAG = 2, 6, 3
        sched, a_units, s_units, v_units = [], [], [], []
        a_list = []
        for n, (g, q) in enumerate(CH):
            for k in range(4 * q, 4 * q + 4):
                for h in range(4):
                    for c in range(q + 1):
                        a_list.append(("A", len(a_units)))
                        a_units.append((n, k, h, c))
            a_list.append(("P", n))
        b_lists = []
        for n, (g, q) in enumerate(CH):
            b = []
            for j in range(4 * q + 4):
                for hp in range(2):
                    b.append(("S", len(s_units)))
                    s_units.append((n, j, hp))
                if j:
                    b.append(("V", len(v_units)))
                    v_units.append((n, j - 1))
            b.append(("V", len(v_units)))
            v_units.append((n, 4 * q + 3))
            b_lists.append(b)
        due = []

        def emit(ev):
            sched.append(ev)
            for d in due:
                d[0] -= 1
            while due and due[0][0] <= 0:
                sched.append(due.pop(0)[1])
            if ev[0] == "P":
                due.append([M_LAG, ("M", ev[1])])

        for n, b in enumerate(b_lists):
            while ("M", n) not in sched:
                if a_list:
                    emit(a_list.pop(0))
                else:
                    due.sort(key=lambda d: d[0])
                    sched.append(due.pop(0)[1])
            for ev in b:
                emit(ev)
                if ev[0] == "S":
                    for _ in range(A_PER_S):
                        if a_list:
                            emit(a_list.pop(0))
            due.append([C_LAG, ("C", n)])
        sched += [d[1] for d in due]
        v_last = {n: i for i, (n, j) in enumerate(v_units)}

        @block.sync
        def _(sp):
            x_v = I["L0_attn_x"].rearrange("b (t p) d -> p (b t) d", p=P)
            for h in range(2):
                sp.dma_start(xm[:, h * T // 2:(h + 1) * T // 2, :], x_v[:, h * T // 2:(h + 1) * T // 2, :]).then_inc(s_x_in, 16)
            sp.dma_start(ident[:], I["c_ident"]).then_inc(s_const_in, 16)
            sp.dma_start(shift[:], I["c_shift"]).then_inc(s_const_in, 16)
            sp.dma_start(mask_in, I["c_masks"]).then_inc(s_const_in, 16)
            sp.dma_start(bdm, I["c_bdmask"]).then_inc(s_const_in, 16)
            sp.dma_start(wqkv[:], I["L0_ffn_wqkv"].rearrange("l k n -> k l n")).then_inc(s_const_in, 16)
            for l in range(DEPTH):
                sp.dma_start(wo[:, l], I["L0_ffn_wo"][l].rearrange("(c k) n -> k c n", k=P)).then_inc(s_const_in, 16)
            for f in range(2):
                if f:
                    sp.wait_ge(s_mla_done, 1)
                sp.dma_start(rot[:], I["c_rot"]).then_inc(s_rot_in, 16)
            sp.wait_ge(s_fin, 1)
            sp.dma_start(out.rearrange("b (t p) d -> p (b t) d", p=P), xm[:]).then_inc(s_stored, 16)
            sp.wait_ge(s_stored, 16)

        NCONST = 16 * 7

        @block.gpsimd
        def _(pool):
            w_tail = HID - (HC - 1) * P
            nc.gpsimd.memset(w1[:], 0.0).then_inc(s_w_zero, 1)
            nc.gpsimd.memset(w2[:], 0.0).then_inc(s_w_zero, 1)
            nc.gpsimd.memset(b1[:], 0.0).then_inc(s_w_zero, 1)
            nc.gpsimd.memset(nhalf[:], -0.5).then_inc(s_w_zero, 1)
            nc.gpsimd.memset(xa[0][:, 0, :], 0.0).then_inc(s_w_zero, 1)
            nc.gpsimd.memset(xa[1][:, 0, :], 0.0).then_inc(s_w_zero, 1)
            pool.wait_ge(s_w_zero, 6)
            c = s_weights_in
            for a in range(2):
                pool.dma_start(w1[:, :, a * HT_:a * HT_ + HID], I["L0_ffn_w1"][:, :, a * HID:(a + 1) * HID].rearrange("l k n -> k l n")).then_inc(c, 16)
            for l in range(DEPTH):
                pool.dma_start(w2[:, l, 0:HC - 1, :], I["L0_ffn_w2"][l, 0:(HC - 1) * P, :].rearrange("(c k) n -> k c n", k=P)).then_inc(c, 16)
            pool.dma_start(w2[0:w_tail, :, HC - 1, :], I["L0_ffn_w2"][:, (HC - 1) * P:HID, :].rearrange("l k n -> k l n")).then_inc(c, 16)
            with nc.allow_non_contiguous_dma(reason="bias and scale vectors, a few hundred words"):
                for a in range(2):
                    for l in range(DEPTH):
                        pool.dma_start(b1[:, l, a * HC:a * HC + HC - 1],
                                       I["L0_ffn_b1"][l, a * HID:a * HID + (HC - 1) * P].rearrange("(c k) -> k c", k=P)).then_inc(c, 16)
                        pool.dma_start(b1[0:w_tail, l, a * HC + HC - 1:a * HC + HC],
                                       I["L0_ffn_b1"][l, a * HID + (HC - 1) * P:(a + 1) * HID].rearrange("(k o) -> k o", o=1)).then_inc(c, 16)
                pool.dma_start(lg[:], I["L0_ffn_ln_g"].rearrange("l k -> k l")).then_inc(c, 16)
                pool.dma_start(lb[:], I["L0_ffn_ln_b"].rearrange("l k -> k l")).then_inc(c, 16)
            pool.dma_start(b2[:], I["L0_ffn_b2"].partition_broadcast(P)).then_inc(s_const2, 16)
            pool.dma_start(qks[:, :, 0, :], I["L0_ffn_q_scale"].partition_broadcast(P)).then_inc(s_const2, 16)
            pool.dma_start(qks[:, :, 1, :], I["L0_ffn_k_scale"].partition_broadcast(P)).then_inc(s_const2, 16)
            pool.dma_start(bdw[:], I["m_factors"].rearrange("n k c -> k n c")).then_inc(s_const2, 16)

            def ln_rstd(n):
                pool.wait_ge(s_ln_var, n)
                nc.gpsimd.tensor_tensor(rstd[:], mv[:, :, 1], nhalf[:, 0:T], ALU.pow).then_inc(s_ln_rstd, 1)

            def layer(L):
                x_in = xa[L % 2]
                pool.wait_ge(s_layer_free, L + 1)
                nc.gpsimd.memset(kring[:, :, 1, 1, :], 0.0).then_inc(s_kz0, 1)
                if L % DEPTH == 0:
                    nc.gpsimd.memset(vm[:, 0, :], 0.0).then_inc(s_kz0, 1)
                    nc.gpsimd.memset(qbd[:], 0.0).then_inc(s_kz0, 1)
                for i in range(-2, T):
                    K = T * L + i
                    if i >= 0:
                        pool.wait_ge(s_rope_terms, 2 * K + 1)
                        nc.gpsimd.tensor_tensor(ra[:, 0:INNER], ra[:, 0:INNER], rb[:, 0:INNER], ALU.add).then_inc(s_rope_sum, 1)
                        pool.wait_ge(s_ssum, K + 1)
                        if K > 1:
                            pool.wait_ge(s_qk_scaled, 2 * (K - 1))
                        nc.gpsimd.tensor_tensor(rn[:, i % 2], ss[:, i % 2], nhalf[:, 0:16], ALU.pow).then_inc(s_qk_rnorm, 1)
                        pool.wait_ge(s_rope_terms, 2 * K + 2)
                        nc.gpsimd.tensor_tensor(ra[:, INNER:], ra[:, INNER:], rb[:, INNER:], ALU.add).then_inc(s_rope_sum, 1)
                    if i + 2 < T:
                        k = i + 2
                        if K + 1 > 0:
                            pool.wait_ge(s_x_T, K + 1)
                        nc.gpsimd.tensor_copy(xs[:, k % 2], x_in[:, k + 1, :]).then_inc(s_x_copy, 1)
                pool.wait_ge(s_attn_add, T * (L + 1))
                for i in range(-2, NG):
                    g = i + 2
                    Gk = NG * L + g
                    if g < NG:
                        if Gk > 1:
                            pool.wait_ge(s_h_norm, Gk - 1)
                        nc.gpsimd.tensor_copy(hb[:, g % 2, :, 0:DIM // 2], x_in[:, 1 + G * g:1 + G * (g + 1), 0:DIM // 2]).then_inc(s_h_left, 1)
                        pool.wait_ge(s_h_stats, Gk + 1)
                        nc.gpsimd.tensor_tensor(frs[:, g % 2], fve[:, g % 2], nhalf[:, 0:G], ALU.pow).then_inc(s_h_rstd, 1)
                    g = i
                    Gk = NG * L + g
                    if g >= 0:
                        if Gk > 1:
                            pool.wait_ge(s_ff_out, Gk - 1)
                        nc.gpsimd.tensor_tensor(xb2[:, g % 2], x_in[:, 1 + G * g:1 + G * (g + 1), :],
                                                b2[:, L % DEPTH, :].unsqueeze(1).to_broadcast([P, G, DIM]), ALU.add).then_inc(s_x_bias, 1)

            ln_rstd(1)
            for L in range(DEPTH):
                layer(L)
            pool.wait_ge(s_mla_free, 1)
            pool.dma_start(wqk[:, 0, :], I["m_qn"].partition_broadcast(P)).then_inc(s_wqk_in, 16)
            pool.dma_start(wqk[:, 1, :], I["m_kn"].partition_broadcast(P)).then_inc(s_wqk_in, 16)
            ln_rstd(2)
            nc.gpsimd.memset(stk[:].bitcast(f32), 0.0).then_inc(s_stk_zero, 1)
            pool.wait_ge(s_stk_zero, 1)
            nc.gpsimd.memset(stk[:, 1, :, :, MS, 0:3], 1.0).then_inc(s_stk_zero, 1)
            nc.gpsimd.memset(vv[:, :, :, HD:], 1.0).then_inc(s_stk_zero, 1)
            for g in range(NG):
                nc.gpsimd.memset(kz[:, :, g * G * P:(g + 1) * G * P].bitcast(f32), 0.0).then_inc(s_kz_zero, 1)
                pool.wait_ge(s_m_normed, g + 1)
                for a in range(2):
                    last = nc.gpsimd.tensor_tensor(nb[:, a], nb[:, a], wqk[:, a].unsqueeze(1).to_broadcast([P, G, SW]), ALU.mult)
                last.then_inc(s_m_weighted, 1)
            pool.wait_ge(s_m_proj, NG)
            nc.gpsimd.memset(mst.rearrange("p n t c r -> p (n t c r)").bitcast(f32), 0.0).then_inc(s_mst_zero, 1)
            ln_rstd(3)
            for L in range(DEPTH, NL):
                layer(L)

        @block.scalar
        def _(act):
            sc = nc.scalar

            def layer(L):
                for k in range(-3, T):
                    i = k + 2
                    K, Ki = T * L + k, T * L + i
                    if 0 <= k:
                        for w in range(2):
                            K2 = 2 * K + w
                            act.wait_ge(s_score_max, K2 + 1)
                            if K > 0:
                                act.wait_ge(s_prob_T, K2 - 1)
                            for p in range(PAIRS):
                                last = sc.activation(prob[:, w, p, :], psum[5 + w][:, p * P:(p + 1) * P], ACT.Exp,
                                                     bias=nm[:, w, p:p + 1], accum_out=sm[:, w, p:p + 1])
                            last.then_inc(s_p_exp, 1)
                    if 0 <= i < T:
                        act.wait_ge(s_qk, 2 * Ki + 1)
                        if Ki > 0:
                            act.wait_ge(s_ssum, Ki)
                        sc.activation(sqb[:, 0:INNER], psum[0], ACT.Square).then_inc(s_qk_sq, 1)
                        act.wait_ge(s_qk, 2 * Ki + 2)
                        sc.activation(sqb[:, INNER:], psum[1], ACT.Square).then_inc(s_qk_sq, 1)
                    if 0 <= k:
                        act.wait_ge(s_prob_T, 2 * K + 1)
                        if K > 0:
                            act.wait_ge(s_pv0, K)
                        sc.copy(pT[:, 0].rearrange("p a b -> p (a b)"), psum[5]).then_inc(s_prob_Tev, 1)
                    if 0 <= k + 1 < T:
                        act.wait_ge(s_q_T, K + 2)
                        if K >= 0:
                            act.wait_ge(s_score, 2 * K + 2)
                        if k + 1 == 0:
                            act.wait_ge(s_kz0, NKZ[L])
                        qsrc = psum[7].rearrange("p (c w q) -> p c w q", c=PAIRS, w=2)
                        sc.copy(qbd[0:64, :, :, 0:64], qsrc[0:64])
                        sc.copy(qbd[64:128, :, :, 64:128], qsrc[64:128]).then_inc(s_q_Tev, 1)
                    if 0 <= k:
                        act.wait_ge(s_prob_T, 2 * K + 2)
                        if K > 0:
                            act.wait_ge(s_pv1, K)
                        sc.copy(pT[:, 1].rearrange("p a b -> p (a b)"), psum[6]).then_inc(s_prob_Tev, 1)
                        act.wait_ge(s_pv1, K + 1)
                        if K > 1:
                            act.wait_ge(s_proj, K - 1)
                        osrc = psum[4].rearrange("p (c q) -> p c q", c=PAIRS)
                        sc.copy(oT[0:64, k % 2, :, 64:128], osrc[0:64, :, 0:64])
                        sc.copy(oT[64:128, k % 2, :, 64:128], osrc[64:128, :, 64:128]).then_inc(s_o_ev1, 1)
                    if 0 <= i + 1 < T:
                        n = i + 1
                        N = T * L + n
                        act.wait_ge(s_x_T, N + 1)
                        if N > 1:
                            act.wait_ge(s_v, N - 1)
                        sc.copy(hT[0:64, n % 2, 0:P], psum[6][0:64, 0:P])
                        if n > 0:
                            act.wait_ge(s_h_T, N)
                            sc.copy(hT[64:128, n % 2, 0:1], hT[64:128, (n - 1) % 2, P:P + 1])
                        else:
                            sc.copy(hT[64:128, 0, 0:1], xa[L % 2][64:128, 0, 0:1])
                        sc.copy(hT[64:128, n % 2, 1:P + 1], psum[6][64:128, 0:P]).then_inc(s_h_T, 1)
                    if 0 <= k + 1 < T:
                        act.wait_ge(s_v, K + 2)
                        if K >= 0:
                            act.wait_ge(s_pv0, K + 1)
                        if K > 0:
                            act.wait_ge(s_pv1, K)
                        sc.copy(va[:, (k + 1) % 2], psum[2])
                        sc.copy(vm[0:64, (k + 1) % 2], psum[2][0:64])
                        sc.copy(vm[64:128, k % 2], psum[2][64:128]).then_inc(s_v_ev, 1)

                def norm_ev(g):
                    Gk = NG * L + g
                    act.wait_ge(s_hn_T, Gk + 1)
                    if Gk > 1:
                        act.wait_ge(s_ff_up, HC * 2 * (Gk - 1))
                    sc.activation(hnT[:, g % 2], psum[1], ACT.Identity, bias=lb[:, L % DEPTH:L % DEPTH + 1],
                                  scale=lg[:, L % DEPTH:L % DEPTH + 1]).then_inc(s_hn_Tev, 1)

                for i in range(-2, NG):
                    g = i + 2
                    Gk = NG * L + g
                    if g < NG:
                        act.wait_ge(s_h_shift, Gk + 1)
                        if Gk > 1:
                            act.wait_ge(s_h_norm, Gk - 1)
                        sc.copy(hb[:, g % 2, :, DIM // 2:], psum[0][:, 0:G * 64].rearrange("p (t d) -> p t d", t=G)).then_inc(s_h_right, 1)
                    g = i
                    Gk = NG * L + g
                    if g >= 0:
                        for h in range(HC):
                            act.wait_ge(s_ff_up, HC * 2 * Gk + 2 * h + 1)
                            if Gk > 0:
                                act.wait_ge(s_ff_hid, HC * (Gk - 1) + h + 1)
                            sc.activation(gl[:, h], psum[2 + 2 * h], ACT.Gelu,
                                          bias=b1[:, L % DEPTH, HC + h:HC + h + 1]).then_inc(s_ff_gelu, 1)
                    if 0 <= i + 1 < NG:
                        norm_ev(i + 1)

            def bd_maps():
                act.wait_ge(s_bd_u, 1)
                sc.copy(bdu, psum[6][:, 0:P]).then_inc(s_bd_uev, 1)

            act.wait_ge(s_all_in, 1)
            bd_maps()
            for L in range(DEPTH):
                layer(L)
            act.wait_ge(s_stk_zero, 3)

            def project_ev(g):
                act.wait_ge(s_m_yT, g + 1)
                if g > 1:
                    act.wait_ge(s_m_proj, g - 1)
                sc.copy(yT[:, g % 2], psum[0]).then_inc(s_m_yTev, 1)
                act.wait_ge(s_m_proj, g + 1)
                if g > 0:
                    act.wait_ge(s_m_ms, g)
                sc.activation(msq[:], banks[:, 4:8, 0:2 * SW], ACT.Square).then_inc(s_m_sq, 1)
                sc.copy(vv[:, G * g:G * (g + 1), :, 0:HD], banks[:, 4:8, 3 * SW:].rearrange("p t (h d) -> p t h d", h=MH)).then_inc(s_m_vev, 1)
                act.wait_ge(s_m_ms, g + 1)
                if g > 0:
                    act.wait_ge(s_m_rms, g)
                sc.activation(msd[:], mss[:], ACT.Sqrt).then_inc(s_m_sd, 1)

            def stack_copies(g):
                q, k = (stk[:, a].rearrange("p t h s d -> p (t h) s d") for a in range(2))
                act.wait_ge(s_m_part, 3 * g + 1)
                sc.copy(q[:, :, 0:2, :], q[:, :, 5:6, :].to_broadcast([P, G * MH, 2, HD]))
                sc.copy(k[:, :, 3:7:3, :], k[:, :, 5:6, :].to_broadcast([P, G * MH, 2, HD]))
                act.wait_ge(s_m_part, 3 * g + 2)
                sc.copy(q[:, :, 3, :], q[:, :, 2, :])
                sc.copy(k[:, :, 1, :], k[:, :, 2, :])
                act.wait_ge(s_m_part, 3 * g + 3)
                sc.copy(q[:, :, 6, :], nb[:, 0].rearrange("p t (h d) -> p (t h) d", h=MH))
                sc.copy(k[:, :, 0, :], nb[:, 1].rearrange("p t (h d) -> p (t h) d", h=MH)).then_inc(s_m_stk, 1)

            def q_stack_ev(g):
                for t in range(G):
                    k = G * g + t
                    act.wait_ge(s_m_QT, k + 1)
                    sc.copy(qst[:, :, k * P:(k + 1) * P], psum[1].bitcast(bf16).rearrange("p (c t) -> p c t", c=MH // 2)).then_inc(s_m_qst, 1)

            project_ev(0)
            stack_copies(0)
            for g in range(NG):
                if g + 1 < NG:
                    project_ev(g + 1)
                q_stack_ev(g)
                if g + 1 < NG:
                    stack_copies(g + 1)

            for ev, n in sched:
                if ev == "M":
                    g, q = CH[n]
                    act.wait_ge(s_m_mT, n + 1)
                    src = psum[BM].bitcast(bf16).rearrange("p (t c q) -> p c t q", t=G, c=2)
                    for r in (8 * MS, 64 + 8 * MS):
                        last = sc.copy(qst[r:r + HD, 2 * g:2 * g + 2, 512 * q:512 * (q + 1)].rearrange("p c (t q) -> p c t q", t=G),
                                       src[r:r + HD])
                    last.then_inc(s_m_mrow, 1)
                elif ev == "S":
                    ch, j, hp = s_units[n]
                    w = 512 - max(0, P * (j - 4 * CH[ch][1]))
                    act.wait_ge(s_b_score, n + 1)
                    if n > 3:
                        act.wait_ge(s_b_pv, n // 2 - 1)
                    sc.activation(pb[:, n % 4, :, 0:w], banks[:, psB[n % 2]:psB[n % 2] + 2, 0:w], ACT.Exp).then_inc(s_b_exp, 1)
                elif ev == "C":
                    act.wait_ge(s_b_pv, v_last[n] + 1)
                    if n > 0:
                        act.wait_ge(s_c_T, n)
                    sc.copy(cT[:], psum[BC]).then_inc(s_c_ev, 1)
            for L in range(DEPTH, NL):
                layer(L)

        @block.vector
        def _(dve):
            ve = nc.vector
            own = [0]

            def link(ins):
                own[0] += 1
                ins.then_inc(s_dve_link, 1)
                dve.wait_ge(s_dve_link, own[0])

            def layer_norm(n, dst):
                for t in range(T):
                    last = ve.bn_stats(stat[:, t, :], xm[:, t, :])
                link(last)
                for t in range(T):
                    last = ve.bn_aggr(mv[:, t, :], stat[:, t, :])
                link(last)
                ve.tensor_scalar(mv[:, :, 1], mv[:, :, 1], LN_EPS, None, ALU.add).then_inc(s_ln_var, 1)
                dve.wait_ge(s_ln_var, n)
                dve.wait_ge(s_ln_rstd, n)
                for t in range(T):
                    last = ve.tensor_scalar(dst[:, t + 1, :], xm[:, t, :], mv[:, t, 0:1], rstd[:, t:t + 1], ALU.subtract, ALU.mult)
                last.then_inc(s_ln_done, 1)
                dve.wait_ge(s_ln_done, n)

            def layer(L):
                l = L % DEPTH
                x_in, x_out = xa[L % 2], xa[(L + 1) % 2]
                dve.wait_ge(s_rot_in, 16 * (L // DEPTH + 1))
                for t in range(T):
                    s = qks[:, l]
                    ve.tensor_tensor(rts[:, t, 0], rot[:, t, 0], s, ALU.mult)
                    ve.tensor_tensor(rts[:, t, 1, :, 0:32], rot[:, t, 1, :, 0:32], s[:, :, 32:64], ALU.mult)
                    last = ve.tensor_tensor(rts[:, t, 1, :, 32:64], rot[:, t, 1, :, 32:64], s[:, :, 0:32], ALU.mult)
                link(last)
                ve.memset(tick[:], 0.0).then_inc(s_layer_free, 1)
                dve.wait_ge(s_layer_free, L + 1)
                def rope(i, a):
                    src = psum[a].rearrange("p (h d) -> p h d", h=HEADS)
                    o1 = ra[:, a * INNER:(a + 1) * INNER].rearrange("p (h d) -> p h d", h=HEADS)
                    o2 = rb[:, a * INNER:(a + 1) * INNER].rearrange("p (h d) -> p h d", h=HEADS)
                    tc, ts = (rts[:, i, f, a, :].unsqueeze(1).to_broadcast([P, HEADS, DH]) for f in range(2))
                    ve.tensor_tensor(o1, src, tc, ALU.mult)
                    ve.tensor_tensor(o2[:, :, 0:32], src[:, :, 32:64], ts[:, :, 0:32], ALU.mult)
                    return ve.tensor_tensor(o2[:, :, 32:64], src[:, :, 0:32], ts[:, :, 32:64], ALU.mult)

                def scaled(t, a):
                    Kt = T * L + t
                    dve.wait_ge(s_qk_rnorm, Kt + 1)
                    dve.wait_ge(s_rope_sum, 2 * Kt + a + 1)
                    if Kt > 0:
                        dve.wait_ge(s_k_T if a else s_q_T, Kt)
                    half = slice(a * INNER, (a + 1) * INNER)
                    ve.tensor_tensor(qk[:, half].rearrange("p (h d) -> p h d", h=HEADS), ra[:, half].rearrange("p (h d) -> p h d", h=HEADS),
                                     rn[:, t % 2, 8 * a:8 * a + 8].unsqueeze(2).to_broadcast([P, HEADS, DH]), ALU.mult).then_inc(s_qk_scaled, 1)

                def normalised(t, w):
                    dve.wait_ge(s_p_exp, 2 * (T * L + t) + w + 1)
                    link(ve.reciprocal(rs[:, w, :], sm[:, w, :]))
                    ve.tensor_tensor(prob[:, w], prob[:, w], rs[:, w, :].unsqueeze(2).to_broadcast([P, PAIRS, P]), ALU.mult).then_inc(s_p_norm, 1)

                for k in range(-2, T + 1):
                    i = k + 2
                    K, Ki = T * L + k, T * L + i
                    if 0 <= k < T:
                        for w in range(2):
                            K2 = 2 * K + w
                            dve.wait_ge(s_score, K2 + 1)
                            if K > 0:
                                dve.wait_ge(s_p_exp, K2 - 1)
                            ve.tensor_reduce(nm[:, w, :], psum[5 + w].rearrange("p (c k) -> p c k", c=PAIRS), AX.X, ALU.max, negate=True).then_inc(s_score_max, 1)
                    if 0 <= k + 1 < T:
                        scaled(k + 1, 0)
                    if 0 <= k < T:
                        normalised(k, 0)
                    if 0 <= k + 1 < T:
                        scaled(k + 1, 1)
                    if 0 <= k - 1:
                        dve.wait_ge(s_proj, K)
                        xt = x_in[:, k, :]
                        ve.tensor_tensor(xt, psum[7][:, 0:DIM], xt, ALU.add).then_inc(s_attn_add, 1)
                    if 0 <= k < T:
                        normalised(k, 1)
                    if i < T:
                        dve.wait_ge(s_qk_sq, 2 * Ki + 1)
                        if Ki > 0:
                            dve.wait_ge(s_qk_scaled, 2 * Ki)
                        rope(i, 0).then_inc(s_rope_terms, 1)
                        dve.wait_ge(s_qk_sq, 2 * Ki + 2)
                        if Ki > 1:
                            dve.wait_ge(s_qk_rnorm, Ki - 1)
                        link(ve.tensor_reduce(ss[:, i % 2, :], sqb[:].rearrange("p (h d) -> p h d", h=16), AX.X, ALU.add))
                        ve.tensor_scalar(ss[:, i % 2, :], ss[:, i % 2, :], 1e-24, None, ALU.max).then_inc(s_ssum, 1)
                    if 0 <= k + 1 < T:
                        dve.wait_ge(s_k_T, K + 2)
                        if K + 1 > 0:
                            dve.wait_ge(s_score, 2 * (K + 1))
                        if k + 1 == 0:
                            dve.wait_ge(s_kz0, NKZ[L])
                        ve.tensor_copy(kring[:, :, :, (k + 1) % 2, :], psum[5].rearrange("p (c h q) -> p c h q", c=PAIRS, h=2)).then_inc(s_k_Tev, 1)
                    if 0 <= k < T:
                        dve.wait_ge(s_pv0, K + 1)
                        if K > 1:
                            dve.wait_ge(s_proj, K - 1)
                        src = psum[3].rearrange("p (c q) -> p c q", c=PAIRS)
                        ve.tensor_copy(oT[0:64, k % 2, :, 0:64], src[0:64, :, 0:64])
                        ve.tensor_copy(oT[64:128, k % 2, :, 0:64], src[64:128, :, 64:128]).then_inc(s_o_ev0, 1)
                    if i < T:
                        rope(i, 1).then_inc(s_rope_terms, 1)

                def stats(g):
                    Gk = NG * L + g
                    dve.wait_ge(s_h_left, Gk + 1)
                    dve.wait_ge(s_h_right, Gk + 1)
                    if Gk > 1:
                        dve.wait_ge(s_h_rstd, Gk - 1)
                    for t in range(G):
                        last = ve.bn_stats(fst[:, g % 2, t, :], hb[:, g % 2, t, :])
                    link(last)
                    for t in range(G):
                        last = ve.bn_aggr(fmv[:, g % 2, t, :], fst[:, g % 2, t, :])
                    link(last)
                    ve.tensor_scalar(fve[:, g % 2, :], fmv[:, g % 2, :, 1], LN_EPS, None, ALU.add).then_inc(s_h_stats, 1)

                def norm(g):
                    Gk = NG * L + g
                    dve.wait_ge(s_h_rstd, Gk + 1)
                    if Gk > 1:
                        dve.wait_ge(s_hn_T, Gk - 1)
                    for t in range(G):
                        last = ve.tensor_scalar(hn[:, g % 2, t, :], hb[:, g % 2, t, :], fmv[:, g % 2, t, 0:1], frs[:, g % 2, t:t + 1], ALU.subtract, ALU.mult)
                    last.then_inc(s_h_norm, 1)

                for i in range(-2, NG):
                    if i < 0:
                        stats(i + 2)
                        norm(i + 2)
                        continue
                    Gk = NG * L + i
                    for h in range(HC):
                        dve.wait_ge(s_ff_gelu, HC * Gk + h + 1)
                        dve.wait_ge(s_ff_up, HC * 2 * Gk + 2 * h + 2)
                        if Gk > 0:
                            dve.wait_ge(s_ff_down, Gk)
                        ve.scalar_tensor_tensor(hid[:, h], psum[3 + 2 * h], b1[:, l, h:h + 1], gl[:, h], ALU.add, ALU.mult).then_inc(s_ff_hid, 1)
                        if h == 1 and i + 2 < NG:
                            stats(i + 2)
                    if i + 2 < NG:
                        norm(i + 2)
                    dve.wait_ge(s_ff_down, Gk + 1)
                    dve.wait_ge(s_x_bias, Gk + 1)
                    ve.tensor_tensor(x_out[:, 1 + G * i:1 + G * (i + 1), :], psum[0].rearrange("p (t d) -> p t d", t=G), xb2[:, i % 2], ALU.add).then_inc(s_ff_out, 1)

            def half_add(n):
                dve.wait_ge(s_ff_out, NG * DEPTH * n)
                last = ve.scalar_tensor_tensor(xm[:], xa[0][:, 1:, :], 0.5, xm[:], ALU.mult, ALU.add)
                return last

            dve.wait_ge(s_x_in, 32)
            dve.wait_ge(s_const_in, NCONST)
            dve.wait_ge(s_weights_in, 16 * 15)
            dve.wait_ge(s_const2, 64)
            dve.wait_ge(s_w_zero, 6)
            dve.wait_ge(s_rot_in, 16)
            ve.tensor_copy(identb[:], ident[:])
            ve.tensor_copy(masks[:], mask_in)
            ve.memset(tick[:], 0.0).then_inc(s_all_in, 1)
            dve.wait_ge(s_all_in, 1)
            dve.wait_ge(s_bd_prod, 1)
            for m in range(4):
                last = ve.tensor_tensor(bd[:, m * P:(m + 1) * P], psum[7][:, m * P:(m + 1) * P], bdm, ALU.mult)
            last.then_inc(s_bd_ready, 1)
            layer_norm(1, xa[0])
            for L in range(DEPTH):
                layer(L)
            link(half_add(1))
            ve.memset(tick[:], 0.0).then_inc(s_mla_free, 1)
            dve.wait_ge(s_mla_free, 1)
            layer_norm(2, xa[0])
            ve.memset(psum[BC], 0.0).then_inc(s_c_zero, 1)
            dve.wait_ge(s_wqk_in, 32)
            ve.tensor_scalar(wqk[:, 0, :], wqk[:, 0, :], MSCALE, None, ALU.mult).then_inc(s_wqk_scaled, 1)
            dve.wait_ge(s_wqk_scaled, 1)
            dve.wait_ge(s_stk_zero, 3)

            def normalise(g):
                dve.wait_ge(s_m_sq, g + 1)
                link(ve.tensor_reduce(mss[:], msq[:].rearrange("p t (h d) -> p (t h) d", d=HD), AX.X, ALU.add))
                ve.tensor_scalar(mss[:], mss[:], 1.0 / HD, RMS_EPS, ALU.mult, ALU.add).then_inc(s_m_ms, 1)
                dve.wait_ge(s_m_sd, g + 1)
                link(ve.reciprocal(mrn[:], msd[:]))
                link(ve.tensor_tensor(mnt[:], mrn[:], mrn[:], ALU.mult))
                link(ve.tensor_tensor(mnt[:], mnt[:], mss[:], ALU.mult))
                link(ve.tensor_scalar(mnt[:], mnt[:], -0.5, 1.5, ALU.mult, ALU.add))
                ve.tensor_tensor(mrn[:], mrn[:], mnt[:], ALU.mult).then_inc(s_m_rms, 1)
                dve.wait_ge(s_m_rms, g + 1)
                if g > 0:
                    dve.wait_ge(s_m_stk, g)
                r = mrn[:].rearrange("p (t a h) -> p a t h", t=G, a=2)
                dve.wait_ge(s_m_vev, g + 1)
                for a in range(2):
                    for t in range(G):
                        last = ve.tensor_tensor(nb[:, a, t].rearrange("p (h d) -> p h d", h=MH),
                                                banks[:, 4 + t, a * SW:(a + 1) * SW].rearrange("p (h d) -> p h d", h=MH),
                                                r[:, a, t].unsqueeze(2).to_broadcast([P, MH, HD]), ALU.mult)
                last.then_inc(s_m_normed, 1)
                dve.wait_ge(s_m_weighted, g + 1)
                ve.tensor_tensor(nb[:, 1], banks[:, 4:8, 2 * SW:3 * SW], nb[:, 1], ALU.add).then_inc(s_m_proj_used, 1)
                dve.wait_ge(s_m_proj_used, g + 1)

            def parts(g):
                if g > 0:
                    dve.wait_ge(s_m_KT, G * g)
                rest = nb[:].rearrange("p a t (h d) -> p (a t h) d", h=MH)
                slots = stk[:].rearrange("p a t h s d -> p (a t h) s d")
                ve.tensor_copy(slots[:, :, 5, :], rest).then_inc(s_m_part, 1)
                dve.wait_ge(s_m_part, 3 * g + 1)
                link(ve.tensor_tensor(rest, rest, slots[:, :, 5, :], ALU.subtract))
                ve.tensor_copy(slots[:, :, 2, :], rest).then_inc(s_m_part, 1)
                dve.wait_ge(s_m_part, 3 * g + 2)
                ve.tensor_tensor(rest, rest, slots[:, :, 2, :], ALU.subtract).then_inc(s_m_part, 1)

            def k_stack_ev(g):
                dve.wait_ge(s_kz_zero, g + 1)
                for t in range(G):
                    k = G * g + t
                    dve.wait_ge(s_m_KT, k + 1)
                    src = psum[2 + t % 2].bitcast(bf16).rearrange("p (c t) -> p c t", c=MH // 2)
                    kzv = kz[:, :, k * P:(k + 1) * P].rearrange("p (c a) t -> p a c t", a=2)
                    ve.tensor_copy(kzv[0:64, 0], src[0:64])
                    ve.tensor_copy(kzv[64:128, 1], src[64:128]).then_inc(s_m_kz, 1)

            normalise(0)
            parts(0)
            for g in range(NG):
                if g + 1 < NG:
                    normalise(g + 1)
                k_stack_ev(g)
                if g + 1 < NG:
                    parts(g + 1)
            for ev, n in sched:
                if ev == "A":
                    ch, k, h, c = a_units[n]
                    w = min(512, P * (k + 1) - 512 * c)
                    dve.wait_ge(s_a_score, n + 1)
                    ve.tensor_reduce(mpart[:, 4 * CH[ch][0] + h, k, c:c + 1], psum[psA[n % 2]][:, 0:w], AX.X, ALU.max).then_inc(s_a_max, 1)
                elif ev == "P":
                    g, q = CH[n]
                    dve.wait_ge(s_a_max, max(i for i, u in enumerate(a_units) if u[0] == n) + 1)
                    nx = nmx[:, n % 2]
                    link(ve.tensor_reduce(nx.rearrange("p a t c -> p c a t"), mpart[:, 4 * g:4 * g + 4, 4 * q:4 * q + 4, 0:q + 1].rearrange("p (c a) t n -> p c a t n", a=2),
                                          AX.X, ALU.max, negate=True))
                    if n == 0:
                        dve.wait_ge(s_mst_zero, 1)
                    if n > 3:
                        dve.wait_ge(s_m_mT, n - 3)
                    dst = mst[:, n % 4].rearrange("p t c (a r) -> p a t c r", a=2)[:, :, :, :, 8 * MS:8 * MS + 3]
                    link(ve.tensor_copy(dst[:, :, :, :, 0], nx))
                    link(ve.tensor_tensor(mr1[:], nx, dst[:, :, :, :, 0], ALU.subtract))
                    link(ve.tensor_copy(dst[:, :, :, :, 1], mr1[:]))
                    link(ve.tensor_tensor(mr1[:], mr1[:], dst[:, :, :, :, 1], ALU.subtract))
                    ve.tensor_copy(dst[:, :, :, :, 2], mr1[:]).then_inc(s_m_parts, 1)
                elif ev == "C":
                    hg, q = CH[n]
                    dve.wait_ge(s_c_T, n + 1)
                    src = psum[BM].rearrange("p (t h c) -> p t h c", t=G, h=4)
                    link(ve.reciprocal(rden[:], src[:, :, :, HD]))
                    link(ve.tensor_tensor(cO[:].rearrange("p (t h d) -> p t h d", t=G, h=4), src[:, :, :, 0:HD],
                                          rden[:].unsqueeze(3).to_broadcast([P, G, 4, HD]), ALU.mult))
                    xt = xm[:, G * q:G * (q + 1), 4 * HD * hg:4 * HD * (hg + 1)]
                    ve.tensor_tensor(xt, xt, cO[:].rearrange("p (t d) -> p t d", t=G), ALU.add).then_inc(s_c_out, 1)
            ve.memset(tick[:], 0.0).then_inc(s_mla_done, 1)
            dve.wait_ge(s_mla_done, 1)
            layer_norm(3, xa[0])
            for L in range(DEPTH, NL):
                layer(L)
            half_add(2).then_inc(s_fin, 1)

        @block.tensor
        def _(pe):
            te = nc.tensor

            def layer(L):
                l = L % DEPTH
                x_in = xa[L % 2]
                for k in range(-3, T + 1):
                    i = k + 2
                    K, Ki = T * L + k, T * L + i
                    if 0 <= k < T:
                        pe.wait_ge(s_q_Tev, K + 1)
                        pe.wait_ge(s_k_Tev, K + 1)
                        u = k % 2
                        for w in range(2):
                            if w and i < T:
                                pe.wait_ge(s_h_T, Ki + 1)
                            mask = wmask[:, 1 if w else (2 if k == 0 else 0), :].unsqueeze(1).to_broadcast([P, PAIRS, P])
                            te.matmul(psum[5 + w], identb[:], mask, start=True, stop=False, skip_group_check=True)
                            for p in range(PAIRS):
                                flat = kring[:, p].rearrange("p h s q -> p (h s) q")
                                keys = flat[:, u:u + 3:2, :] if w else (flat[:, 0:4:3, :] if u == 0 else flat[:, 1:3, :])
                                last = te.matmul(psum[5 + w][:, p * P:(p + 1) * P], qbd[:, p, w, :], keys, start=False, stop=True, skip_group_check=True)
                            last.then_inc(s_score, 1)
                    if 1 <= k:
                        pe.wait_ge(s_o_ev0, K)
                        pe.wait_ge(s_o_ev1, K)
                        for p in range(PAIRS):
                            last = te.matmul(psum[7][:, 0:DIM], oT[:, (k - 1) % 2, p, :], wo[:, l, p, :], start=p == 0, stop=p == PAIRS - 1)
                        last.then_inc(s_proj, 1)
                    if 0 <= k + 1 < T:
                        if K + 1 > 0:
                            pe.wait_ge(s_v_ev, K + 1)
                        te.matmul(psum[2], hT[:, (k + 1) % 2, 0:P], wqkv[:, l, 2 * INNER:3 * INNER], start=True, stop=True).then_inc(s_v, 1)
                    if 0 <= i < T:
                        pe.wait_ge(s_h_T, Ki + 1)
                        if Ki > 0:
                            pe.wait_ge(s_rope_terms, 2 * Ki)
                        for c in range(2):
                            te.matmul(psum[c], hT[:, i % 2, 0:P], wqkv[:, l, c * INNER:(c + 1) * INNER], start=True, stop=True).then_inc(s_qk, 1)
                    if 0 <= k < T:
                        pe.wait_ge(s_p_norm, 2 * K + 1)
                        for p in range(PAIRS):
                            last = te.transpose(psum[5][:, p * P:(p + 1) * P], prob[:, 0, p, :], ident[:])
                        last.then_inc(s_prob_T, 1)
                    if 0 <= k + 1 < T:
                        pe.wait_ge(s_qk_scaled, 2 * K + 3)
                        if K > 0:
                            pe.wait_ge(s_attn_add, K)
                        for p in range(PAIRS):
                            last = te.transpose(psum[7][:, p * P:(p + 1) * P], qk[:, p * P:(p + 1) * P], ident[:])
                        last.then_inc(s_q_T, 1)
                    if 0 <= k < T:
                        pe.wait_ge(s_p_norm, 2 * K + 2)
                        for p in range(PAIRS):
                            last = te.transpose(psum[6][:, p * P:(p + 1) * P], prob[:, 1, p, :], ident[:])
                        last.then_inc(s_prob_T, 1)
                        pe.wait_ge(s_prob_Tev, 2 * K + 1)
                        pe.wait_ge(s_v_ev, K + 1)
                        for p in range(PAIRS):
                            last = te.matmul(psum[3][:, p * P:(p + 1) * P], vm[:, k % 2, p * P:(p + 1) * P], pT[:, 0, p, :], start=True, stop=True)
                        last.then_inc(s_pv0, 1)
                    if 0 <= k + 1 < T:
                        pe.wait_ge(s_qk_scaled, 2 * K + 4)
                        if K >= 0:
                            pe.wait_ge(s_prob_Tev, 2 * K + 1)
                        for p in range(PAIRS):
                            last = te.transpose(psum[5][:, p * P:(p + 1) * P], qk[:, INNER + p * P:INNER + (p + 1) * P], ident[:])
                        last.then_inc(s_k_T, 1)
                    if 0 <= k < T:
                        pe.wait_ge(s_prob_Tev, 2 * K + 2)
                        for p in range(PAIRS):
                            last = te.matmul(psum[4][:, p * P:(p + 1) * P], va[:, k % 2, p * P:(p + 1) * P], pT[:, 1, p, :], start=True, stop=True)
                        last.then_inc(s_pv1, 1)
                    if 0 <= i + 1 < T:
                        pe.wait_ge(s_x_copy, Ki + 2)
                        if Ki + 1 > 0:
                            pe.wait_ge(s_h_T, Ki + 1)
                        te.transpose(psum[6][:, 0:P], xs[:, (i + 1) % 2], ident[:]).then_inc(s_x_T, 1)

                def shift_h(g):
                    Gk = NG * L + g
                    if Gk > 2:
                        pe.wait_ge(s_ff_out, min(Gk - 2, NG * L + max(g - 2, 0)))
                    if Gk > 0:
                        pe.wait_ge(s_h_right, Gk)
                    for f in range(2):
                        last = te.matmul(psum[0][:, 0:G * 64], shift[:, f], x_in[:, 1 + G * g - f:1 + G * (g + 1) - f, 64:128], start=f == 0, stop=f == 1)
                    last.then_inc(s_h_shift, 1)

                def norm_T(g):
                    Gk = NG * L + g
                    pe.wait_ge(s_h_norm, Gk + 1)
                    if Gk > 0:
                        pe.wait_ge(s_hn_Tev, Gk)
                    for t in range(G):
                        last = te.transpose(psum[1][:, t * P:(t + 1) * P], hn[:, g % 2, t, :], ident[:])
                    last.then_inc(s_hn_T, 1)

                pe.wait_ge(s_attn_add, T * (L + 1))
                pe.wait_ge(s_rope_terms, 2 * T * (L + 1))
                pe.wait_ge(s_v_ev, T * (L + 1))
                pe.wait_ge(s_o_ev0, T * (L + 1))
                pe.wait_ge(s_o_ev1, T * (L + 1))
                shift_h(0)
                shift_h(1)
                norm_T(0)
                for g in range(NG):
                    Gk = NG * L + g
                    pe.wait_ge(s_hn_Tev, Gk + 1)
                    for h in range(HC):
                        if Gk > 0:
                            pe.wait_ge(s_ff_gelu, HC * (Gk - 1) + h + 1)
                        te.matmul(psum[2 + 2 * h], w1[:, l, HT_ + h * P:HT_ + (h + 1) * P], hnT[:, g % 2], start=True, stop=True).then_inc(s_ff_up, 1)
                        if Gk > 0:
                            pe.wait_ge(s_ff_hid, HC * (Gk - 1) + h + 1)
                        te.matmul(psum[3 + 2 * h], w1[:, l, h * P:(h + 1) * P], hnT[:, g % 2], start=True, stop=True).then_inc(s_ff_up, 1)
                    if g + 2 < NG:
                        if Gk > 0:
                            pe.wait_ge(s_ff_out, Gk)
                        shift_h(g + 2)
                    if g + 1 < NG:
                        norm_T(g + 1)
                    pe.wait_ge(s_ff_hid, HC * (Gk + 1))
                    pe.wait_ge(s_h_right, min(Gk + 3, NG * (L + 1)))
                    if Gk > 0:
                        pe.wait_ge(s_ff_out, Gk)
                    for t in range(G):
                        for h in range(HC):
                            last = te.matmul(psum[0][:, t * P:(t + 1) * P], hid[:, h, t * P:(t + 1) * P], w2[:, l, h, :], start=h == 0, stop=h == HC - 1)
                    last.then_inc(s_ff_down, 1)
                pe.wait_ge(s_ff_out, NG * (L + 1))

            pe.wait_ge(s_all_in, 1)
            UQ, DQ, UK, DKV, QR, KR, UV, WO = range(8)
            te.matmul(psum[6][:, 0:P], bdw[:, UV, :], bdw[:, WO, :], start=True, stop=True).then_inc(s_bd_u, 1)
            te.matmul(psum[7][:, 0:P], bdw[:, DQ, :], bdw[:, UQ, :], start=True, stop=True)
            te.matmul(psum[7][:, P:2 * P], bdw[:, DKV, :], bdw[:, UK, :], start=True, stop=True)
            te.matmul(psum[7][:, 2 * P:3 * P], bdw[:, KR, :], bdw[:, QR, :], start=True, stop=True)
            pe.wait_ge(s_bd_uev, 1)
            te.matmul(psum[7][:, 3 * P:], bdw[:, DKV, :], bdu, start=True, stop=True).then_inc(s_bd_prod, 1)
            pe.wait_ge(s_bd_ready, 1)
            for L in range(DEPTH):
                layer(L)
            pe.wait_ge(s_ln_done, 2)
            pe.wait_ge(s_stk_zero, 3)

            def project(g):
                if g > 0:
                    pe.wait_ge(s_m_yTev, g)
                for t in range(G):
                    last = te.transpose(psum[0][:, t * P:(t + 1) * P], xa[0][:, 1 + G * g + t, :], ident[:])
                last.then_inc(s_m_yT, 1)
                pe.wait_ge(s_m_yTev, g + 1)
                if g > 0:
                    pe.wait_ge(s_m_proj_used, g)
                for t in range(G):
                    last = te.matmul(psum[4 + t], yT[:, g % 2, t * P:(t + 1) * P], bd[:], start=True, stop=True)
                last.then_inc(s_m_proj, 1)

            def stack_T(g):
                pe.wait_ge(s_m_stk, g + 1)
                for t in range(G):
                    k = G * g + t
                    for a in range(2):
                        if a == 0 and k > 0:
                            pe.wait_ge(s_m_qst, k)
                        if a == 1 and k > 1:
                            pe.wait_ge(s_m_kz, k - 1)
                        bank = psum[1 if a == 0 else 2 + t % 2].bitcast(bf16)
                        for c in range(MH // 2):
                            src = stk[:, a, t, 2 * c:2 * c + 2].rearrange("p h s d -> p (h s d)")
                            last = te.transpose(bank[:, c * P:(c + 1) * P], src, identb[:])
                        last.then_inc(s_m_KT if a else s_m_QT, 1)

            project(0)
            for g in range(NG):
                if g + 1 < NG:
                    project(g + 1)
                stack_T(g)
            pe.wait_ge(s_m_qst, T)
            pe.wait_ge(s_m_kz, T)
            n_m = n_c = 0
            for ev, n in sched:
                if ev == "A":
                    ch, k, h, c = a_units[n]
                    hd = 4 * CH[ch][0] + h
                    w = min(512, P * (k + 1) - 512 * c)
                    diag = c == k // 4
                    if n > 1:
                        pe.wait_ge(s_a_max, n - 1)
                    bank = psum[psA[n % 2]]
                    ins = te.matmul(bank[:, 0:w], qst[:, hd // 2, k * P:(k + 1) * P], kz[:, hd, 512 * c:512 * c + w],
                                    start=True, stop=not diag, skip_group_check=True)
                    if diag:
                        ins = te.matmul(bank[:, w - P:w], identb[:], cmask[:, 0, :], start=False, stop=True, skip_group_check=True)
                    ins.then_inc(s_a_score, 1)
                elif ev == "M":
                    pe.wait_ge(s_m_parts, n + 1)
                    if n_m > 0:
                        pe.wait_ge(s_m_mrow, n_m)
                    if n_c > 0:
                        pe.wait_ge(s_c_out, n_c)
                    for t in range(G):
                        for c in range(2):
                            last = te.transpose(psum[BM].bitcast(bf16)[:, (2 * t + c) * P:(2 * t + c + 1) * P],
                                                mst[:, n % 4, t, c, :], identb[:])
                    last.then_inc(s_m_mT, 1)
                    n_m += 1
                elif ev == "S":
                    ch, j, hp = s_units[n]
                    g, q = CH[ch]
                    lo = max(0, P * (j - 4 * q))
                    if j == 0:
                        pe.wait_ge(s_m_mrow, ch + 1)
                    if n > 1:
                        pe.wait_ge(s_b_exp, n - 1)
                    for h2 in range(2):
                        hd = 4 * g + 2 * hp + h2
                        bank = psum[psB[n % 2] + h2]
                        diag = j >= 4 * q
                        last = te.matmul(bank[:, 0:512 - lo], kz[:, hd, j * P:(j + 1) * P], qst[:, hd // 2, 512 * q + lo:512 * (q + 1)],
                                         start=True, stop=not diag, skip_group_check=True)
                        if diag:
                            last = te.matmul(bank[:, 0:P], identb[:], cmask[:, 1, :], start=False, stop=True, skip_group_check=True)
                    last.then_inc(s_b_score, 1)
                elif ev == "V":
                    ch, j = v_units[n]
                    g, q = CH[ch]
                    lo = max(0, P * (j - 4 * q))
                    pe.wait_ge(s_b_exp, 2 * n + 2)
                    if j == 0:
                        if ch > 0:
                            pe.wait_ge(s_c_ev, ch)
                        pe.wait_ge(s_c_zero, 1)
                    for h in range(4):
                        last = te.matmul(psum[BC][32 * h:32 * h + VW, lo:512], vv[:, j, 4 * g + h, :],
                                         pb[:, (2 * n + h // 2) % 4, h % 2, 0:512 - lo],
                                         start=j == 0, stop=j == 4 * q + 3, skip_group_check=True)
                    last.then_inc(s_b_pv, 1)
                elif ev == "C":
                    pe.wait_ge(s_c_ev, n + 1)
                    if n_m > 0:
                        pe.wait_ge(s_m_mrow, n_m)
                    if n_c > 0:
                        pe.wait_ge(s_c_out, n_c)
                    for t in range(G):
                        last = te.transpose(psum[BM][:, t * P:(t + 1) * P], cT[:, t * P:(t + 1) * P], ident[:])
                    last.then_inc(s_c_T, 1)
                    n_c += 1
            pe.wait_ge(s_c_out, 16)
            pe.wait_ge(s_ln_done, 3)
            for L in range(DEPTH, NL):
                layer(L)


_DATA = ['L0_attn_x', 'L0_ffn_wqkv', 'L0_ffn_q_scale', 'L0_ffn_k_scale', 'L0_ffn_wo', 'L0_ffn_ln_g', 'L0_ffn_ln_b',
         'L0_ffn_w1', 'L0_ffn_b1', 'L0_ffn_w2', 'L0_ffn_b2']


def constants(ntok):
    P, DH, WIN, HEADS = 128, 64, 64, 8
    T = ntok // P
    c = {"c_ident": np.eye(P, dtype=np.float32)}
    sh = np.zeros((P, 2, P), np.float32)
    sh[np.arange(P - 1), 0, np.arange(1, P)] = 1
    sh[P - 1, 1, 0] = 1
    c["c_shift"] = sh
    q = np.arange(P)[:, None] % WIN
    k = np.arange(P)[None, :]
    even = np.where(k < WIN, k <= q, k >= q + WIN)
    odd = (k >= q) & (k <= q + WIN)
    first = (k < WIN) & (k <= q)
    BIG = np.float32(-1e30)
    a = np.arange(P)
    by_query, by_key = a[None, :] <= a[:, None], a[:, None] <= a[None, :]
    c["c_masks"] = np.stack([np.where(m, np.float32(0), BIG) for m in (even, odd, first, by_query, by_key)], 1)
    c["c_bdmask"] = (a[:, None] // 8 == a[None, :] // 8).astype(np.float32)
    half = np.arange(0, DH, 2, dtype=np.float32)
    inv = (1.0 / np.float32(10000.0) ** (half / np.float32(DH))).astype(np.float32)
    t = np.arange(ntok, dtype=np.float32)
    fr = (t[:, None] * inv[None, :]).astype(np.float32)
    fr = np.concatenate([fr, fr], 1).astype(np.float64)
    base = ((half + np.float32(0.4 * DH)) / np.float32(1.4 * DH)).astype(np.float32)
    power = ((t - ntok // 2) / np.float32(WIN // 2)).astype(np.float32)
    sc = base[None, :].astype(np.float64) ** power[:, None].astype(np.float64)
    sc = np.concatenate([sc, sc], 1)
    cos, sin = np.cos(fr), np.sin(fr)
    sin[:, :DH // 2] *= -1
    rot = np.stack([np.stack([cos * sc * 8.0, cos / sc], 1), np.stack([sin * sc * 8.0, sin / sc], 1)], 1)
    c["c_rot"] = rot.reshape(T, P, 2, 2, DH).transpose(1, 0, 2, 3, 4).astype(np.float32)
    return c


def kernel(**inputs):
    import concourse.bacc as _bacc
    from concourse.bass_utils import run_bass_kernel_spmd as _run

    nc = _bacc.Bacc("TRN2", target_bir_lowering=False, num_devices=1)
    a = {n: np.ascontiguousarray(inputs[n]) for n in _DATA}
    a.update(constants(a["L0_attn_x"].shape[1]))
    g = {n: np.asarray(inputs["L0_attn_" + n]) for n in ("W_DQ", "W_UQ", "W_DKV", "W_UKV", "W_QR", "W_KR", "W_O", "q_norm_w", "k_norm_w")}

    def factor(w, heads):
        w = np.tile(w, (1, heads))
        out = np.zeros((128, 128), w.dtype)
        out[:w.shape[0], :w.shape[1]] = w
        return out

    a["m_factors"] = np.stack([factor(g["W_UQ"].T, 16), factor(g["W_DQ"], 16), factor(g["W_UKV"][:8].T, 16), factor(g["W_DKV"], 16),
                               factor(g["W_QR"], 16), factor(g["W_KR"], 16), factor(g["W_UKV"][8:], 1), factor(g["W_O"].T, 16)])
    a["m_qn"] = np.tile(g["q_norm_w"], 16)
    a["m_kn"] = np.tile(g["k_norm_w"], 16)
    arrays, I = {}, {}
    for name, v in a.items():
        v = np.ascontiguousarray(v)
        arrays[name] = v
        I[name] = nc.dram_tensor(name, v.shape, mybir.dt.from_np(v.dtype), kind="ExternalInput").ap()
    out = nc.dram_tensor("out", a["L0_attn_x"].shape, mybir.dt.float32, kind="ExternalOutput").ap()
    macaron_kernel(nc, I, out)
    r = _run(nc, [arrays], core_ids=[0])
    return r.results[0]["out"]
```

```python
import numpy as np
from contextlib import ExitStack

import concourse.bass as bass
from concourse import mybir


def macaron_kernel(nc: bass.Bass, I: dict, out: bass.AP):
    f32 = mybir.dt.float32
    bf16 = mybir.dt.bfloat16
    ALU = mybir.AluOpType
    ACT = mybir.ActivationFunctionType
    AX = mybir.AxisListType

    P = 128
    NTOK, DIM = I["L0_attn_x"].shape[1:]
    T = NTOK // P
    DEPTH = I["L0_ffn_wqkv"].shape[0]
    HEADS, DH, WIN = 8, 64, 64
    INNER = HEADS * DH
    PAIRS = HEADS // 2
    HID = I["L0_ffn_w2"].shape[1]
    HC = -(-HID // P)
    HT_ = HC * P
    G = 4
    NG = T // G
    MH, HD = 16, 8
    MG = MH // 4
    VW = 16
    LN_EPS = 1e-5
    RMS_EPS = 1.1920929e-07
    MSCALE = HD ** -0.5

    with ExitStack() as ctx:
        def sb(name, shape, dt=f32):
            return ctx.enter_context(nc.sbuf_tensor(name, shape, dt))

        def sem(name):
            return ctx.enter_context(nc.semaphore(name))

        s_mla_done = sem("mla_done")
        s_fin = sem("fin")
        s_w_zero = sem("w_zero")
        s_init = sem("init")
        s_ln_var = sem("ln_var")
        s_ssum = sem("ssum")
        s_ss_floor = sem("ss_floor")
        s_q_scaled = sem("q_scaled")
        s_k_scaled = sem("k_scaled")
        s_rope_terms = sem("rope_terms")
        s_x_T = sem("x_T")
        s_attn_add = sem("attn_add")
        s_h_stats = sem("h_stats")
        s_h_norm = sem("h_norm")
        s_ff_out = sem("ff_out")
        s_mla_free = sem("mla_free")
        s_m_ms = sem("m_ms")
        s_q_T = sem("q_T")
        s_k_T = sem("k_T")
        s_score = sem("score")
        s_no_keys = sem("no_keys")
        s_att_zero = sem("att_zero")
        s_score_max = sem("score_max")
        s_prob_T = sem("prob_T")
        s_h_T = sem("h_T")
        s_pv0 = sem("pv0")
        s_pv1 = sem("pv1")
        s_h_shift = sem("h_shift")
        s_hn_T = sem("hn_T")
        s_ff_up = sem("ff_up")
        s_ff_hid = sem("ff_hid")
        s_bd_u = sem("bd_u")
        s_all_in = sem("all_in")
        s_m_yT = sem("m_yT")
        s_m_proj = sem("m_proj")
        s_m_mT = sem("m_mT")
        s_b_score = sem("b_score")
        s_b_pv = sem("b_pv")
        s_c_T = sem("c_T")
        s_ln_rstd = sem("ln_rstd")
        s_rot_first = sem("rot_first")
        s_rot_in = sem("rot_in")
        s_proj = sem("proj")
        s_p_exp = sem("p_exp")
        s_p_norm = sem("p_norm")
        s_p_recip = sem("p_recip")
        s_qk_sq = sem("qk_sq")
        s_qk_rnorm = sem("qk_rnorm")
        s_rope_sum = sem("rope_sum")
        s_h_left = sem("h_left")
        s_h_right = sem("h_right")
        s_h_rstd = sem("h_rstd")
        s_ff_gelu = sem("ff_gelu")
        s_ff_down = sem("ff_down")
        s_x_bias = sem("x_bias")
        s_x_in = sem("x_in")
        s_const_in = sem("const_in")
        s_weights_in = sem("weights_in")
        s_bd_prod = sem("bd_prod")
        s_wqk_in = sem("wqk_in")
        s_m_sq = sem("m_sq")
        s_m_rms = sem("m_rms")
        s_m_stk = sem("m_stk")
        s_a_score = sem("a_score")
        s_o_ev0 = sem("o_ev0")
        s_o_ev1 = sem("o_ev1")
        s_qk = sem("qk")
        s_v = sem("v")
        s_q_Tev = sem("q_Tev")
        s_k_Tev = sem("k_Tev")
        s_prob_Tev = sem("prob_Tev")
        s_v_ev = sem("v_ev")
        s_ln_done = sem("ln_done")
        s_hn_Tev = sem("hn_Tev")
        s_bd_uev = sem("bd_uev")
        s_bd_ready = sem("bd_ready")
        s_m_yTev = sem("m_yTev")
        s_m_qst = sem("m_qst")
        s_m_kz = sem("m_kz")
        s_a_max = sem("a_max")
        s_m_parts = sem("m_parts")
        s_c_out = sem("c_out")
        s_m_mrow = sem("m_mrow")
        s_b_exp = sem("b_exp")
        s_c_ev = sem("c_ev")
        s_c_zero = sem("c_zero")
        s_stored = sem("stored")
        s_dve_link = sem("dve_link")
        s_kz_zero = sem("kz_zero")
        s_m_KT = sem("m_KT")
        s_m_QT = sem("m_QT")
        s_m_normed = sem("m_normed")
        s_m_part = sem("m_part")
        s_m_qkg_used = sem("m_qkg_used")
        s_m_sd = sem("m_sd")
        s_m_qkg = sem("m_qkg")
        s_m_weighted = sem("m_weighted")
        s_m_k_weighted = sem("m_k_weighted")
        s_mst_zero = sem("mst_zero")
        s_stk_zero = sem("stk_zero")
        s_v_one = sem("v_one")
        s_wqk_scaled = sem("wqk_scaled")

        xm = sb("xm", [P, T, DIM])
        xa = [sb("xa0", [P, T + 1, DIM]), sb("xa1", [P, T + 1, DIM])]
        wqkv = sb("wqkv", [P, DEPTH, 3 * INNER])
        wo = sb("wo", [P, DEPTH, PAIRS, DIM])
        w1 = sb("w1", [P, DEPTH, 2 * HT_])
        w2 = sb("w2", [P, DEPTH, HC, DIM])
        b1 = sb("b1", [P, DEPTH, 2 * HC])
        b2 = sb("b2", [P, DEPTH, DIM])
        lg = sb("lg", [P, DEPTH])
        lb = sb("lb", [P, DEPTH])
        qks = sb("qks", [P, DEPTH, 2, DH])
        ident = sb("ident", [P, P])
        identb = sb("identb", [P, P], bf16)
        shift = sb("shift", [P, 2, P])
        masks = sb("masks", [P, 5, P], bf16)
        wmask, cmask = masks[:, 0:3], masks[:, 3:5]
        nhalf = sb("nhalf", [P, 32])
        bd = sb("bd", [P, 4 * P])
        stat = sb("stat", [P, T, 6])
        mv = sb("mv", [P, T, 2])
        rstd = sb("rstd", [P, T])

        banks = ctx.enter_context(nc.psum_tensor("banks", [P, 8, 512], f32))
        psum = [banks[:, i, :] for i in range(8)]
        RING, BC = (0, 1, 2), 3
        psB = [4, 6]

        ARENA = 38384
        arena = sb("arena", [P, ARENA])
        at = [0]

        def view(shape, dt=f32):
            n = int(np.prod(shape[1:])) * (4 if dt == f32 else 2) // 4
            v = arena[:, at[0]:at[0] + n]
            at[0] += n
            assert at[0] <= ARENA
            if dt != f32:
                v = v.bitcast(dt)
            names = "abcdef"[:len(shape) - 1]
            if len(shape) > 2:
                v = v.rearrange(f"p ({' '.join(names)}) -> p {' '.join(names)}", **{c: s for c, s in zip(names, shape[1:])})
            return v

        rot = view([P, T, 2, 2, DH])
        rts = view([P, T, 2, 2, DH])
        hT = view([P, 2, P + 1])
        sqb = view([P, 2 * INNER])
        ss = view([P, 2, 16])
        rn = view([P, 2, 16])
        ra = view([P, 2 * INNER])
        rb = view([P, 2 * INNER])
        qk = view([P, 2 * INNER])
        va = view([P, 2, INNER])
        vm = view([P, 2, INNER])
        qbd = view([P, PAIRS, 2, P])
        kring = view([P, PAIRS, 2, 2, WIN])
        nm = view([P, 2, PAIRS])
        sm = view([P, 2, PAIRS])
        rs = view([P, 2, PAIRS])
        prob = view([P, 2, PAIRS, P])
        pT = view([P, 2, PAIRS, P])
        oT = view([P, 2, PAIRS, P])
        hb = view([P, 2, G, DIM])
        xb2 = view([P, 2, G, DIM])
        hn = view([P, 2, G, DIM])
        hnT = view([P, 2, G * P])
        gl = view([P, HC, G * P])
        hid = view([P, HC, G * P])
        fst = view([P, 2, G, 6])
        fmv = view([P, 2, G, 2])
        fve = view([P, 2, G])
        frs = view([P, 2, G])
        ffn_words = at[0]
        spare = xa[1][:, 1:, :].rearrange("p t d -> p (t d)")
        bdw = spare[:, 0:8 * P].rearrange("p (n c) -> p n c", n=8)
        bdu = spare[:, 8 * P:9 * P]
        bdm = spare[:, 14 * P:15 * P]
        mask_in = spare[:, 9 * P:14 * P].rearrange("p (n c) -> p n c", n=5)
        yT = spare[:, 0:2 * G * P].rearrange("p (n c) -> p n c", n=2)
        mst = spare.bitcast(bf16).rearrange("p (n t c r) -> p n t c r", n=4, t=G, c=2)
        at[0] = 0
        kz = view([P, MH, NTOK], bf16)
        qst = view([P, MH // 2, NTOK], bf16)
        vv = view([P, T, MH, VW])
        shared = at[0]
        SW = MH * HD
        wqk = view([P, 2, SW])
        msq = view([P, G, 2 * SW])
        mqkg = view([P, G, 3 * SW])
        mss = view([P, G * 2 * MH])
        msd = view([P, G * 2 * MH])
        mrn = view([P, G * 2 * MH])
        mnt = view([P, G * 2 * MH])
        nb = view([P, 2, G, SW])
        stk = view([P, 2, G, MH, 8, HD], bf16)
        at[0] = shared
        mpart = view([P, MH, T, 4])
        nmx = view([P, 2, 2, G, 2])
        mr1 = view([P, 2, G, 2])
        pb = view([P, 4, 2, 512])
        cT = view([P, 512])
        rden = view([P, G, 4])
        cO = view([P, G * 4 * HD])

        tick = sb("tick", [P, 1])
        warm = sb("warm", [P, 1])

        block = ctx.enter_context(nc.Block())

        NL = 2 * DEPTH
        QS = ((0, 1, 5), (2, 3), (6,))
        KS = ((3, 5, 6), (1, 2), (0,))
        MS = 4

        NQ = NTOK // 512
        CH_TABLES = NQ * MG // 2
        CH = [(g, q) for g in range(MG) for q in (range(NQ) if g % 2 == 0 else reversed(range(NQ)))]
        V_LAG, M_LAG, C_LAG = 2, 10, 5
        sched, a_units, s_units = [], [], []
        a_list = []
        for n, (g, q) in enumerate(CH):
            for k in range(4 * q, 4 * q + 4):
                for h in range(4):
                    for c in range(q + 1):
                        a_list.append(("A", len(a_units)))
                        a_units.append((n, k, h, c))
            a_list.append(("P", n))
        due = []

        def emit(ev):
            sched.append(ev)
            for d in due:
                d[0] -= 1
            while due and due[0][0] <= 0:
                sched.append(due.pop(0)[1])
            if ev[0] == "P":
                due.append([M_LAG, ("M", ev[1])])

        a_events = list(a_list)
        a_due = {m: a_events.index(("P", m)) + 1 for m in range(len(CH))}
        s_start = {m: sum(8 * (q + 1) for g, q in CH[:m]) for m in range(len(CH))}
        MARGIN = 8
        credit = 0
        v_next, v_last = 0, {}
        for n, (g, q) in enumerate(CH):
            while ("M", n) not in sched:
                if a_list:
                    emit(a_list.pop(0))
                else:
                    due.sort(key=lambda d: d[0])
                    sched.append(due.pop(0)[1])
            for j in range(4 * q + 4):
                for hp in range(2):
                    emit(("S", len(s_units)))
                    s_units.append((n, j, hp))
                    done, now = len(a_events) - len(a_list), len(s_units)
                    credit += max([0] + [(a_due[m] - done) / max(1, s_start[m] - now - MARGIN) for m in range(n + 1, len(CH))])
                    credit = min(credit, 3)
                    if a_list and credit >= 1:
                        credit -= 1
                        emit(a_list.pop(0))
                    while v_next < len(s_units) - (0 if (n, j, hp) == (len(CH) - 1, 4 * q + 3, 1) else V_LAG):
                        emit(("V", v_next))
                        ch, jj, hh = s_units[v_next]
                        if (jj, hh) == (4 * CH[ch][1] + 3, 1):
                            v_last[ch] = v_next
                            sched.append(("E", ch))
                            due.append([C_LAG, ("C", ch)])
                        v_next += 1
                    while a_list and credit >= 1:
                        credit -= 1
                        emit(a_list.pop(0))
        due.sort(key=lambda d: d[0])
        sched += [d[1] for d in due]
        ring = [e for e in sched if e[0] in "AMC"]
        ring_bank = {e: psum[RING[i % len(RING)]] for i, e in enumerate(ring)}
        ring_before = {e: ring[i - len(RING)] if i >= len(RING) else ("", 0) for i, e in enumerate(ring)}

        @block.sync
        def _(sp):
            x_v, out_v = (d.rearrange("b (t p) d -> p (b t) d", p=P) for d in (I["L0_attn_x"], out))
            for h in range(2):
                sp.dma_start(xm[:, h * T // 2:(h + 1) * T // 2, :], x_v[:, h * T // 2:(h + 1) * T // 2, :]).then_inc(s_x_in, 16)
            sp.dma_start(ident[:], I["c_ident"]).then_inc(s_const_in, 16)
            sp.dma_start(rot[:, 0:G], I["c_rot"][:, 0:G]).then_inc(s_rot_first, 16)
            sp.dma_start(wqkv[:, 0], I["L0_ffn_wqkv"][0]).then_inc(s_const_in, 16)
            sp.dma_start(mask_in, I["c_masks"]).then_inc(s_const_in, 16)
            sp.dma_start(bdw[:], I["m_factors"].rearrange("n k c -> k n c")).then_inc(s_const_in, 16)
            sp.dma_start(bdm, I["c_bdmask"]).then_inc(s_const_in, 16)
            sp.dma_start(qks[:, :, 0, :], I["L0_ffn_q_scale"].partition_broadcast(P)).then_inc(s_const_in, 16)
            sp.dma_start(qks[:, :, 1, :], I["L0_ffn_k_scale"].partition_broadcast(P)).then_inc(s_const_in, 16)
            sp.dma_start(rot[:, G:], I["c_rot"][:, G:]).then_inc(s_rot_in, 16)
            for l in range(DEPTH):
                if l:
                    sp.dma_start(wqkv[:, l], I["L0_ffn_wqkv"][l]).then_inc(s_weights_in, 16)
                sp.dma_start(wo[:, l], I["L0_ffn_wo"][l].rearrange("(c k) n -> k c n", k=P)).then_inc(s_weights_in, 16)
            sp.dma_start(shift[:], I["c_shift"]).then_inc(s_weights_in, 16)
            sp.dma_start(b2[:], I["L0_ffn_b2"].partition_broadcast(P)).then_inc(s_weights_in, 16)
            w_tail = HID - (HC - 1) * P
            sp.wait_ge(s_w_zero, 3)
            for a in range(2):
                sp.dma_start(w1[:, :, a * HT_:a * HT_ + HID], I["L0_ffn_w1"][:, :, a * HID:(a + 1) * HID].rearrange("l k n -> k l n")).then_inc(s_weights_in, 16)
            for l in range(DEPTH):
                sp.dma_start(w2[:, l, 0:HC - 1, :], I["L0_ffn_w2"][l, 0:(HC - 1) * P, :].rearrange("(c k) n -> k c n", k=P)).then_inc(s_weights_in, 16)
            sp.dma_start(w2[0:w_tail, :, HC - 1, :], I["L0_ffn_w2"][:, (HC - 1) * P:HID, :].rearrange("l k n -> k l n")).then_inc(s_weights_in, 16)
            with nc.allow_non_contiguous_dma(reason="bias and scale vectors, a few hundred words"):
                for a in range(2):
                    for l in range(DEPTH):
                        sp.dma_start(b1[:, l, a * HC:a * HC + HC - 1],
                                     I["L0_ffn_b1"][l, a * HID:a * HID + (HC - 1) * P].rearrange("(c k) -> k c", k=P)).then_inc(s_weights_in, 16)
                        sp.dma_start(b1[0:w_tail, l, a * HC + HC - 1:a * HC + HC],
                                     I["L0_ffn_b1"][l, a * HID + (HC - 1) * P:(a + 1) * HID].rearrange("(k o) -> k o", o=1)).then_inc(s_weights_in, 16)
                sp.dma_start(lg[:], I["L0_ffn_ln_g"].rearrange("l k -> k l")).then_inc(s_weights_in, 16)
                sp.dma_start(lb[:], I["L0_ffn_ln_b"].rearrange("l k -> k l")).then_inc(s_weights_in, 16)
            sp.wait_ge(s_c_T, CH_TABLES)
            sp.dma_start(rot[:], I["c_rot"]).then_inc(s_rot_in, 16)
            for g in range(NG):
                sp.wait_ge(s_fin, g + 1)
                sp.dma_start(out_v[:, G * g:G * (g + 1), :], xm[:, G * g:G * (g + 1), :]).then_inc(s_stored, 16)
            sp.wait_ge(s_stored, 16 * NG)

        NCONST = 16 * 7
        NWEIGHT = 16 * (2 * DEPTH - 1 + 2 + 2 + DEPTH + 1 + 4 * DEPTH + 2)

        @block.gpsimd
        def _(pool):
            nc.gpsimd.memset(nhalf[:], -0.5).then_inc(s_init, 1)
            nc.gpsimd.memset(xa[0][:, 0, :], 0.0).then_inc(s_init, 1)
            nc.gpsimd.memset(xa[1][:, 0, :], 0.0).then_inc(s_init, 1)
            pool.wait_ge(s_init, 3)

            def att_zero():
                nc.gpsimd.memset(qbd[:], 0.0).then_inc(s_att_zero, 1)
                nc.gpsimd.memset(vm[:, 0, :], 0.0).then_inc(s_att_zero, 1)

            def ln_rstd(i, g):
                pool.wait_ge(s_ln_var, i + 1)
                ts = slice(G * g, G * (g + 1))
                nc.gpsimd.tensor_tensor(rstd[:, ts], mv[:, ts, 1], nhalf[:, 0:G], ALU.pow).then_inc(s_ln_rstd, 1)

            def no_keys(L):
                if L > 0:
                    pool.wait_ge(s_score, 2 * T * L)
                nc.gpsimd.memset(kring[:, :, 1, 1, :], 0.0).then_inc(s_no_keys, 1)

            def h_left(L, g):
                Gk = NG * L + g
                pool.wait_ge(s_attn_add, T * L + G * (g + 1))
                if Gk > 1:
                    pool.wait_ge(s_h_norm, Gk - 1)
                nc.gpsimd.tensor_copy(hb[:, g % 2, :, 0:DIM // 2], xa[L % 2][:, 1 + G * g:1 + G * (g + 1), 0:DIM // 2]).then_inc(s_h_left, 1)

            def h_rstd(L, g):
                pool.wait_ge(s_h_stats, NG * L + g + 1)
                nc.gpsimd.tensor_tensor(frs[:, g % 2], fve[:, g % 2], nhalf[:, 0:G], ALU.pow).then_inc(s_h_rstd, 1)

            def layer(L):
                if L % DEPTH == 0:
                    if L:
                        att_zero()
                    no_keys(L)
                for i in range(T + 2):
                    K = T * L + i
                    if i < T:
                        pool.wait_ge(s_rope_terms, 2 * K + 1)
                        nc.gpsimd.tensor_tensor(ra[:, 0:INNER], ra[:, 0:INNER], rb[:, 0:INNER], ALU.add).then_inc(s_rope_sum, 1)
                        pool.wait_ge(s_ssum, K + 1)
                        if K > 1:
                            pool.wait_ge(s_q_scaled, K - 1)
                            pool.wait_ge(s_k_scaled, K - 1)
                        nc.gpsimd.tensor_scalar(ss[:, i % 2], ss[:, i % 2], 1e-24, None, ALU.max).then_inc(s_ss_floor, 1)
                        pool.wait_ge(s_ss_floor, K + 1)
                        nc.gpsimd.tensor_tensor(rn[:, i % 2], ss[:, i % 2], nhalf[:, 0:16], ALU.pow).then_inc(s_qk_rnorm, 1)
                        pool.wait_ge(s_rope_terms, 2 * K + 2)
                        nc.gpsimd.tensor_tensor(ra[:, INNER:], ra[:, INNER:], rb[:, INNER:], ALU.add).then_inc(s_rope_sum, 1)
                        pool.wait_ge(s_rope_sum, 2 * K + 2)
                        pool.wait_ge(s_qk_rnorm, K + 1)
                        if K > 0:
                            pool.wait_ge(s_k_T, K)
                        nc.gpsimd.tensor_tensor(qk[:, INNER:].rearrange("p (h d) -> p h d", h=HEADS), ra[:, INNER:].rearrange("p (h d) -> p h d", h=HEADS),
                                                rn[:, i % 2, HEADS:].unsqueeze(2).to_broadcast([P, HEADS, DH]), ALU.mult).then_inc(s_k_scaled, 1)
                    else:
                        h_left(L, i - T)
                        h_rstd(L, i - T)
                for g in range(NG):
                    Gk = NG * L + g
                    if g + 2 < NG:
                        h_left(L, g + 2)
                    elif g == NG - 1 and (L + 1) % DEPTH:
                        no_keys(L + 1)
                    if L == 0 and g == 0:
                        pool.wait_ge(s_weights_in, NWEIGHT)
                    pool.wait_ge(s_attn_add, T * L + G * (g + 1))
                    if Gk > 1:
                        pool.wait_ge(s_ff_out, Gk - 1)
                    nc.gpsimd.tensor_tensor(xb2[:, g % 2], xa[L % 2][:, 1 + G * g:1 + G * (g + 1), :],
                                            b2[:, L % DEPTH, :].unsqueeze(1).to_broadcast([P, G, DIM]), ALU.add).then_inc(s_x_bias, 1)
                    if g + 2 < NG:
                        h_rstd(L, g + 2)
                    if L == DEPTH - 1 and g > 0:
                        ln_rstd(NG + g - 1, g - 1)

            att_zero()
            for g in range(NG):
                ln_rstd(g, g)
            for L in range(DEPTH):
                layer(L)
            ln_rstd(2 * NG - 1, NG - 1)
            pool.wait_ge(s_mla_free, 1)
            pool.dma_start(wqk[:, 0, :], I["m_qn"].partition_broadcast(P)).then_inc(s_wqk_in, 16)
            pool.dma_start(wqk[:, 1, :], I["m_kn"].partition_broadcast(P)).then_inc(s_wqk_in, 16)
            nc.gpsimd.memset(stk[:].bitcast(f32), 0.0).then_inc(s_stk_zero, 1)
            pool.wait_ge(s_stk_zero, 1)
            nc.gpsimd.memset(stk[:, 1, :, :, MS, 0:3], 1.0).then_inc(s_stk_zero, 1)
            for g in range(NG):
                nc.gpsimd.memset(kz[:, :, g * G * P:(g + 1) * G * P].bitcast(f32), 0.0).then_inc(s_kz_zero, 1)
                if g == 0:
                    pool.wait_ge(s_wqk_scaled, 1)
                pool.wait_ge(s_m_normed, g + 1)
                nc.gpsimd.tensor_tensor(nb[:, 1], nb[:, 1], wqk[:, 1].unsqueeze(1).to_broadcast([P, G, SW]), ALU.mult).then_inc(s_m_k_weighted, 1)
                nc.gpsimd.tensor_tensor(nb[:, 0], nb[:, 0], wqk[:, 0].unsqueeze(1).to_broadcast([P, G, SW]), ALU.mult).then_inc(s_m_weighted, 1)
                pool.wait_ge(s_m_k_weighted, g + 1)
                nc.gpsimd.tensor_tensor(nb[:, 1], mqkg[:, :, 2 * SW:], nb[:, 1], ALU.add).then_inc(s_m_qkg_used, 1)
            nc.gpsimd.memset(vv[:, :, :, HD:], 1.0).then_inc(s_v_one, 1)
            pool.wait_ge(s_m_proj, NG)
            nc.gpsimd.memset(mst.rearrange("p n t c r -> p (n t c r)").bitcast(f32), 0.0).then_inc(s_mst_zero, 1)
            for i in range(NG):
                ln_rstd(2 * NG + i, CH[NQ * (MG - 1) + i][1])
            pool.wait_ge(s_mla_done, 1)
            for L in range(DEPTH, NL):
                layer(L)

        @block.scalar
        def _(act):
            sc = nc.scalar

            def norm_ev(L, g):
                Gk = NG * L + g
                if Gk == 0:
                    act.wait_ge(s_weights_in, NWEIGHT)
                act.wait_ge(s_hn_T, Gk + 1)
                if Gk > 1:
                    act.wait_ge(s_ff_up, HC * 2 * (Gk - 1))
                sc.activation(hnT[:, g % 2], psum[1], ACT.Identity, bias=lb[:, L % DEPTH:L % DEPTH + 1],
                              scale=lg[:, L % DEPTH:L % DEPTH + 1]).then_inc(s_hn_Tev, 1)

            def right_ev(L, g):
                Gk = NG * L + g
                act.wait_ge(s_h_shift, Gk + 1)
                if Gk > 1:
                    act.wait_ge(s_h_norm, Gk - 1)
                sc.copy(hb[:, g % 2, :, DIM // 2:], psum[0][:, 0:G * 64].rearrange("p (t d) -> p t d", t=G)).then_inc(s_h_right, 1)

            def attend(L, k):
                i = k + 2
                K, Ki = T * L + k, T * L + i
                if 0 <= k:
                    for w in range(2):
                        K2 = 2 * K + w
                        act.wait_ge(s_score_max, K2 + 1)
                        if K > 0:
                            act.wait_ge(s_prob_T, K2 - 1)
                        for p in range(PAIRS):
                            last = sc.activation(prob[:, w, p, :], psum[5 + w][:, p * P:(p + 1) * P], ACT.Exp,
                                                 bias=nm[:, w, p:p + 1], accum_out=sm[:, w, p:p + 1])
                        last.then_inc(s_p_exp, 1)
                if 0 <= i < T:
                    act.wait_ge(s_qk, 2 * Ki + 1)
                    if Ki > 0:
                        act.wait_ge(s_ssum, Ki)
                    sc.activation(sqb[:, 0:INNER], psum[0], ACT.Square).then_inc(s_qk_sq, 1)
                    act.wait_ge(s_qk, 2 * Ki + 2)
                    sc.activation(sqb[:, INNER:], psum[1], ACT.Square).then_inc(s_qk_sq, 1)
                if i >= T and k < T:
                    if i > T:
                        norm_ev(L, i - T - 1)
                    right_ev(L, i - T)
                if 0 <= k:
                    act.wait_ge(s_prob_T, 2 * K + 1)
                    if K > 0:
                        act.wait_ge(s_pv0, K)
                    sc.copy(pT[:, 0].rearrange("p a b -> p (a b)"), psum[5]).then_inc(s_prob_Tev, 1)
                    act.wait_ge(s_prob_T, 2 * K + 2)
                    if K > 0:
                        act.wait_ge(s_pv1, K)
                    sc.copy(pT[:, 1].rearrange("p a b -> p (a b)"), psum[6]).then_inc(s_prob_Tev, 1)
                if 0 <= k + 1 < T:
                    act.wait_ge(s_q_T, K + 2)
                    if K >= 0:
                        act.wait_ge(s_score, 2 * K + 2)
                    if k + 1 == 0:
                        act.wait_ge(s_att_zero, 2 * (L // DEPTH + 1))
                    qsrc = psum[7].rearrange("p (c w q) -> p c w q", c=PAIRS, w=2)
                    sc.copy(qbd[0:64, :, :, 0:64], qsrc[0:64])
                    sc.copy(qbd[64:128, :, :, 64:128], qsrc[64:128]).then_inc(s_q_Tev, 1)
                if 0 <= k:
                    act.wait_ge(s_pv1, K + 1)
                    if K > 1:
                        act.wait_ge(s_proj, K - 1)
                    sc.copy(oT[:, k % 2, :, 64:128], psum[4][:, 0:PAIRS * WIN].rearrange("p (c q) -> p c q", c=PAIRS)).then_inc(s_o_ev1, 1)
                if 0 <= i + 1 < T:
                    n = i + 1
                    N = T * L + n
                    act.wait_ge(s_x_T, N + 1)
                    if N > 1:
                        act.wait_ge(s_v, N - 1)
                    sc.copy(hT[0:64, n % 2, 0:P], psum[6][0:64, 0:P])
                    if n > 0:
                        act.wait_ge(s_h_T, N)
                        sc.copy(hT[64:128, n % 2, 0:1], hT[64:128, (n - 1) % 2, P:P + 1])
                    else:
                        sc.copy(hT[64:128, 0, 0:1], xa[L % 2][64:128, 0, 0:1])
                    sc.copy(hT[64:128, n % 2, 1:P + 1], psum[6][64:128, 0:P]).then_inc(s_h_T, 1)
                if 0 <= k + 1 < T:
                    act.wait_ge(s_v, K + 2)
                    if K >= 0:
                        act.wait_ge(s_pv0, K + 1)
                    if K > 0:
                        act.wait_ge(s_pv1, K)
                    sc.copy(va[:, (k + 1) % 2], psum[2])
                    sc.copy(vm[0:64, (k + 1) % 2], psum[2][0:64])
                    sc.copy(vm[64:128, k % 2], psum[2][64:128]).then_inc(s_v_ev, 1)

            def layer(L):
                for k in range(-3 if L == DEPTH else -1, T):
                    attend(L, k)
                ahead = (L + 1) % DEPTH
                for g in range(NG):
                    for h in range(HC):
                        u = HC * (NG * L + g) + h
                        act.wait_ge(s_ff_up, 2 * u + 1)
                        if u >= HC:
                            act.wait_ge(s_ff_hid, u - HC + 1)
                        sc.activation(gl[:, h], psum[2 + 2 * (u % 2)], ACT.Gelu,
                                      bias=b1[:, L % DEPTH, HC + h:HC + h + 1]).then_inc(s_ff_gelu, 1)
                        if h == 0 and g + 1 < NG:
                            norm_ev(L, g + 1)
                        if h == 0 and g == NG - 1 and ahead:
                            attend(L + 1, -3)
                        if h == 1 and g + 2 < NG:
                            right_ev(L, g + 2)
                if ahead:
                    attend(L + 1, -2)

            def bd_maps():
                act.wait_ge(s_bd_u, 1)
                sc.copy(bdu, psum[3][:, 0:P]).then_inc(s_bd_uev, 1)

            act.wait_ge(s_init, 3)
            sc.activation(warm[:], nhalf[:, 0:1], ACT.Square)
            act.wait_ge(s_all_in, 1)
            attend(0, -3)
            attend(0, -2)
            bd_maps()
            for L in range(DEPTH):
                layer(L)
            act.wait_ge(s_mla_free, 1)

            def y_ev(g):
                act.wait_ge(s_m_yT, g + 1)
                if g > 1:
                    act.wait_ge(s_m_proj, g - 1)
                sc.copy(yT[:, g % 2], psum[0]).then_inc(s_m_yTev, 1)

            def squares(g):
                act.wait_ge(s_m_proj, g + 1)
                if g > 0:
                    act.wait_ge(s_m_ms, g)
                sc.activation(msq[:], banks[:, 4:8, 0:2 * SW], ACT.Square).then_inc(s_m_sq, 1)
                sc.copy(vv[:, G * g:G * (g + 1), :, 0:HD], banks[:, 4:8, 3 * SW:].rearrange("p t (h d) -> p t h d", h=MH))

            def qkg_copy(g):
                if g > 0:
                    act.wait_ge(s_m_qkg_used, g)
                sc.copy(mqkg[:], banks[:, 4:8, 0:3 * SW]).then_inc(s_m_qkg, 1)

            def root(g):
                act.wait_ge(s_m_ms, g + 1)
                if g > 0:
                    act.wait_ge(s_m_rms, g)
                sc.activation(msd[:], mss[:], ACT.Sqrt).then_inc(s_m_sd, 1)

            def stack_copies(g):
                q, k = (stk[:, a].rearrange("p t h s d -> p (t h) s d") for a in range(2))
                if g == 0:
                    act.wait_ge(s_stk_zero, 2)
                act.wait_ge(s_m_part, 3 * g + 1)
                sc.copy(q[:, :, 0:2, :], q[:, :, 5:6, :].to_broadcast([P, G * MH, 2, HD]))
                sc.copy(k[:, :, 3:7:3, :], k[:, :, 5:6, :].to_broadcast([P, G * MH, 2, HD]))
                act.wait_ge(s_m_part, 3 * g + 2)
                sc.copy(q[:, :, 3, :], q[:, :, 2, :])
                sc.copy(k[:, :, 1, :], k[:, :, 2, :])
                act.wait_ge(s_m_part, 3 * g + 3)
                sc.copy(q[:, :, 6, :], nb[:, 0].rearrange("p t (h d) -> p (t h) d", h=MH))
                sc.copy(k[:, :, 0, :], nb[:, 1].rearrange("p t (h d) -> p (t h) d", h=MH)).then_inc(s_m_stk, 1)

            def q_stack_ev(g):
                for t in range(G):
                    k = G * g + t
                    act.wait_ge(s_m_QT, k + 1)
                    sc.copy(qst[:, :, k * P:(k + 1) * P], psum[1 - t % 2].bitcast(bf16).rearrange("p (c t) -> p c t", c=MH // 2)).then_inc(s_m_qst, 1)

            y_ev(0)
            squares(0)
            qkg_copy(0)
            y_ev(1)
            root(0)
            squares(1)
            y_ev(2)
            qkg_copy(1)
            for g in range(NG):
                if g + 1 < NG:
                    root(g + 1)
                stack_copies(g)
                if g + 2 < NG:
                    squares(g + 2)
                if g + 3 < NG:
                    y_ev(g + 3)
                q_stack_ev(g)
                if g + 2 < NG:
                    qkg_copy(g + 2)

            for ev, n in sched:
                if ev == "M":
                    g, q = CH[n]
                    act.wait_ge(s_m_mT, n + 1)
                    src = ring_bank[ev, n].bitcast(bf16).rearrange("p (t c q) -> p c t q", t=G, c=2)
                    for r in (8 * MS, 64 + 8 * MS):
                        last = sc.copy(qst[r:r + HD, 2 * g:2 * g + 2, 512 * q:512 * (q + 1)].rearrange("p c (t q) -> p c t q", t=G),
                                       src[r:r + HD])
                    last.then_inc(s_m_mrow, 1)
                elif ev == "S":
                    ch, j, hp = s_units[n]
                    w = 512 - max(0, P * (j - 4 * CH[ch][1]))
                    act.wait_ge(s_b_score, n + 1)
                    if n > 3:
                        act.wait_ge(s_b_pv, n - 3)
                    sc.activation(pb[:, n % 4, :, 0:w], banks[:, psB[n % 2]:psB[n % 2] + 2, 0:w], ACT.Exp).then_inc(s_b_exp, 1)
                elif ev == "E":
                    act.wait_ge(s_b_pv, v_last[n] + 1)
                    if n > 0:
                        act.wait_ge(s_c_T, n)
                    sc.copy(cT[:], psum[BC]).then_inc(s_c_ev, 1)
            for L in range(DEPTH, NL):
                layer(L)

        @block.vector
        def _(dve):
            ve = nc.vector
            own = [0]

            def link(ins):
                own[0] += 1
                ins.then_inc(s_dve_link, 1)
                dve.wait_ge(s_dve_link, own[0])

            def ln_stats(i, g):
                if i >= NG:
                    dve.wait_ge(s_ln_done, i - NG + 1)
                for t in range(G * g, G * (g + 1)):
                    last = ve.bn_stats(stat[:, t, :], xm[:, t, :])
                link(last)
                for t in range(G * g, G * (g + 1)):
                    last = ve.bn_aggr(mv[:, t, :], stat[:, t, :])
                link(last)
                ts = slice(G * g, G * (g + 1))
                ve.tensor_scalar(mv[:, ts, 1], mv[:, ts, 1], LN_EPS, None, ALU.add).then_inc(s_ln_var, 1)

            def ln_apply(i, g):
                dve.wait_ge(s_ln_rstd, i + 1)
                for t in range(G * g, G * (g + 1)):
                    last = ve.tensor_scalar(xa[0][:, t + 1, :], xm[:, t, :], mv[:, t, 0:1], rstd[:, t:t + 1], ALU.subtract, ALU.mult)
                last.then_inc(s_ln_done, 1)

            def tables(L, tiles):
                scale = qks[:, L % DEPTH]
                other = scale.rearrange("p a (b d) -> p a b d", b=2)[:, :, ::-1, :]
                for t in tiles:
                    ve.tensor_tensor(rts[:, t, 0], rot[:, t, 0], scale, ALU.mult)
                    last = ve.tensor_tensor(rts[:, t, 1].rearrange("p a (b d) -> p a b d", b=2), rot[:, t, 1].rearrange("p a (b d) -> p a b d", b=2), other, ALU.mult)
                link(last)

            def rope(L, i, a):
                src = psum[a].rearrange("p (h d) -> p h d", h=HEADS)
                o1 = ra[:, a * INNER:(a + 1) * INNER].rearrange("p (h d) -> p h d", h=HEADS)
                ve.tensor_tensor(o1, src, rts[:, i, 0, a, :].unsqueeze(1).to_broadcast([P, HEADS, DH]), ALU.mult)
                o2 = rb[:, a * INNER:(a + 1) * INNER].rearrange("p (h b d) -> p h b d", h=HEADS, b=2)
                other = psum[a].rearrange("p (h b d) -> p h b d", h=HEADS, b=2)[:, :, ::-1, :]
                ts = rts[:, i, 1, a, :].rearrange("p (b d) -> p b d", b=2).unsqueeze(1).to_broadcast([P, HEADS, 2, DH // 2])
                return ve.tensor_tensor(o2, other, ts, ALU.mult)

            def scaled(L, t):
                Kt = T * L + t
                dve.wait_ge(s_qk_rnorm, Kt + 1)
                dve.wait_ge(s_rope_sum, 2 * Kt + 1)
                if Kt > 0:
                    dve.wait_ge(s_q_T, Kt)
                ve.tensor_tensor(qk[:, 0:INNER].rearrange("p (h d) -> p h d", h=HEADS), ra[:, 0:INNER].rearrange("p (h d) -> p h d", h=HEADS),
                                 rn[:, t % 2, 0:HEADS].unsqueeze(2).to_broadcast([P, HEADS, DH]), ALU.mult).then_inc(s_q_scaled, 1)

            def normalised(L, t, w):
                dve.wait_ge(s_p_recip, 2 * (T * L + t) + w + 1)
                ve.tensor_tensor(prob[:, w], prob[:, w], rs[:, w, :].unsqueeze(2).to_broadcast([P, PAIRS, P]), ALU.mult).then_inc(s_p_norm, 1)

            def attend(L, k):
                i = k + 2
                K, Ki = T * L + k, T * L + i
                if 0 <= k < T:
                    for w in range(2):
                        K2 = 2 * K + w
                        dve.wait_ge(s_score, K2 + 1)
                        if K > 0:
                            dve.wait_ge(s_p_exp, K2 - 1)
                        ve.tensor_reduce(nm[:, w, :], psum[5 + w].rearrange("p (c k) -> p c k", c=PAIRS), AX.X, ALU.max, negate=True).then_inc(s_score_max, 1)
                if 0 <= k + 1 < T:
                    scaled(L, k + 1)
                if 0 <= k < T:
                    dve.wait_ge(s_p_exp, 2 * K + 1)
                    ve.reciprocal(rs[:, 0, :], sm[:, 0, :]).then_inc(s_p_recip, 1)
                if 0 <= k - 1:
                    dve.wait_ge(s_proj, K)
                    xt = xa[L % 2][:, k, :]
                    ve.tensor_tensor(xt, psum[7][:, 0:DIM], xt, ALU.add).then_inc(s_attn_add, 1)
                if 0 <= k < T:
                    normalised(L, k, 0)
                    dve.wait_ge(s_p_exp, 2 * K + 2)
                    ve.reciprocal(rs[:, 1, :], sm[:, 1, :]).then_inc(s_p_recip, 1)
                    normalised(L, k, 1)
                if i < T:
                    dve.wait_ge(s_qk_sq, 2 * Ki + 1)
                    if Ki > 0:
                        dve.wait_ge(s_q_scaled, Ki)
                    rope(L, i, 0).then_inc(s_rope_terms, 1)
                    dve.wait_ge(s_qk_sq, 2 * Ki + 2)
                    if Ki > 1:
                        dve.wait_ge(s_qk_rnorm, Ki - 1)
                    ve.tensor_reduce(ss[:, i % 2, :], sqb[:].rearrange("p (h d) -> p h d", h=16), AX.X, ALU.add).then_inc(s_ssum, 1)
                elif k < T:
                    stats(L, i - T)
                if 0 <= k + 1 < T:
                    dve.wait_ge(s_k_T, K + 2)
                    if K + 1 > 0:
                        dve.wait_ge(s_score, 2 * (K + 1))
                    ve.tensor_copy(kring[:, :, :, (k + 1) % 2, :], psum[5].rearrange("p (c h q) -> p c h q", c=PAIRS, h=2)).then_inc(s_k_Tev, 1)
                if 0 <= k < T:
                    dve.wait_ge(s_pv0, K + 1)
                    if K > 1:
                        dve.wait_ge(s_proj, K - 1)
                    ve.tensor_copy(oT[:, k % 2, :, 0:64], psum[3][:, 0:PAIRS * WIN].rearrange("p (c q) -> p c q", c=PAIRS)).then_inc(s_o_ev0, 1)
                if i < T:
                    if Ki > 0:
                        dve.wait_ge(s_k_scaled, Ki)
                    rope(L, i, 1).then_inc(s_rope_terms, 1)
                elif k < T:
                    norm(L, i - T)

            def stats(L, g):
                Gk = NG * L + g
                dve.wait_ge(s_h_left, Gk + 1)
                dve.wait_ge(s_h_right, Gk + 1)
                if Gk > 1:
                    dve.wait_ge(s_h_rstd, Gk - 1)
                for t in range(G):
                    last = ve.bn_stats(fst[:, g % 2, t, :], hb[:, g % 2, t, :])
                link(last)
                for t in range(G):
                    last = ve.bn_aggr(fmv[:, g % 2, t, :], fst[:, g % 2, t, :])
                link(last)
                ve.tensor_scalar(fve[:, g % 2, :], fmv[:, g % 2, :, 1], LN_EPS, None, ALU.add).then_inc(s_h_stats, 1)

            def norm(L, g):
                Gk = NG * L + g
                dve.wait_ge(s_h_rstd, Gk + 1)
                if Gk > 1:
                    dve.wait_ge(s_hn_T, Gk - 1)
                for t in range(G):
                    last = ve.tensor_scalar(hn[:, g % 2, t, :], hb[:, g % 2, t, :], fmv[:, g % 2, t, 0:1], frs[:, g % 2, t:t + 1], ALU.subtract, ALU.mult)
                last.then_inc(s_h_norm, 1)

            def ff_out(L, g):
                Gk = NG * L + g
                dve.wait_ge(s_ff_down, Gk + 1)
                dve.wait_ge(s_x_bias, Gk + 1)
                ve.tensor_tensor(xa[(L + 1) % 2][:, 1 + G * g:1 + G * (g + 1), :], psum[7].rearrange("p (t d) -> p t d", t=G), xb2[:, g % 2], ALU.add).then_inc(s_ff_out, 1)

            def part_end(L, g):
                dve.wait_ge(s_ff_out, NG * L + g + 1)
                ts = slice(G * g, G * (g + 1))
                last = ve.scalar_tensor_tensor(xm[:, ts, :], xa[0][:, 1 + G * g:1 + G * (g + 1), :], 0.5, xm[:, ts, :], ALU.mult, ALU.add)
                if L == DEPTH - 1:
                    link(last)
                    ln_stats(NG + g, g)
                else:
                    last.then_inc(s_fin, 1)

            def layer(L):
                for k in range(0 if L == 0 else -1 if L % DEPTH else -2, T + 1):
                    attend(L, k)
                    if L == 0 and k < T // 2:
                        tables(0, [T // 2 + k])
                ahead = (L + 1) % DEPTH
                if L == 0:
                    dve.wait_ge(s_weights_in, NWEIGHT)
                if ahead:
                    dve.wait_ge(s_rope_terms, 2 * T * (L + 1))
                for g in range(NG):
                    Gk = NG * L + g
                    for h in range(HC):
                        u = HC * Gk + h
                        dve.wait_ge(s_ff_gelu, u + 1)
                        dve.wait_ge(s_ff_up, 2 * u + 2)
                        if Gk > 0:
                            dve.wait_ge(s_ff_down, Gk)
                        ve.scalar_tensor_tensor(hid[:, h], psum[3 + 2 * (u % 2)], b1[:, L % DEPTH, h:h + 1], gl[:, h], ALU.add, ALU.mult).then_inc(s_ff_hid, 1)
                        if h == 0 and g > 0:
                            ff_out(L, g - 1)
                        if h == 1 and g + 2 < NG:
                            stats(L, g + 2)
                    if g + 2 < NG:
                        norm(L, g + 2)
                    if ahead and g + 1 < NG:
                        tables(L + 1, range(G * g, G * (g + 1)))
                    if L == DEPTH - 1 and g > 1:
                        ln_apply(NG + g - 2, g - 2)
                    if not ahead and g > 0:
                        part_end(L, g - 1)
                if ahead:
                    attend(L + 1, -2)
                ff_out(L, NG - 1)
                if ahead:
                    tables(L + 1, range(G * (NG - 1), T))
                if L == DEPTH - 1:
                    ln_apply(2 * NG - 2, NG - 2)
                if not ahead:
                    part_end(L, NG - 1)
                if L == DEPTH - 1:
                    ln_apply(2 * NG - 1, NG - 1)

            ve.memset(w1[:], 0.0).then_inc(s_w_zero, 1)
            ve.memset(w2[:], 0.0).then_inc(s_w_zero, 1)
            ve.memset(b1[:], 0.0).then_inc(s_w_zero, 1)
            dve.wait_ge(s_x_in, 32)
            for g in range(NG):
                ln_stats(g, g)
            dve.wait_ge(s_init, 3)
            dve.wait_ge(s_const_in, NCONST)
            ve.tensor_copy(identb[:], ident[:])
            ve.tensor_copy(masks[:], mask_in)
            ve.memset(tick[:], 0.0).then_inc(s_all_in, 1)
            dve.wait_ge(s_all_in, 1)
            for g in range(NG):
                ln_apply(g, g)
            dve.wait_ge(s_rot_first, 16)
            tables(0, range(0, 2))
            attend(0, -2)
            tables(0, range(2, G))
            dve.wait_ge(s_bd_prod, 1)
            for m in range(4):
                last = ve.tensor_tensor(bd[:, m * P:(m + 1) * P], psum[4][:, m * P:(m + 1) * P], bdm, ALU.mult)
            last.then_inc(s_bd_ready, 1)
            dve.wait_ge(s_rot_in, 16)
            tables(0, range(G, T // 2))
            attend(0, -1)
            for L in range(DEPTH):
                layer(L)
            ve.memset(tick[:], 0.0).then_inc(s_mla_free, 1)
            dve.wait_ge(s_mla_free, 1)
            ve.memset(psum[BC], 0.0).then_inc(s_c_zero, 1)
            dve.wait_ge(s_wqk_in, 32)
            ve.tensor_scalar(wqk[:, 0, :], wqk[:, 0, :], MSCALE, None, ALU.mult).then_inc(s_wqk_scaled, 1)

            def mean_square(g):
                dve.wait_ge(s_m_sq, g + 1)
                link(ve.tensor_reduce(mss[:], msq[:].rearrange("p t (h d) -> p (t h) d", d=HD), AX.X, ALU.add))
                ve.tensor_scalar(mss[:], mss[:], 1.0 / HD, RMS_EPS, ALU.mult, ALU.add).then_inc(s_m_ms, 1)

            def normalise(g):
                dve.wait_ge(s_m_sd, g + 1)
                link(ve.reciprocal(mrn[:], msd[:]))
                link(ve.tensor_tensor(mnt[:], mrn[:], mrn[:], ALU.mult))
                link(ve.tensor_tensor(mnt[:], mnt[:], mss[:], ALU.mult))
                link(ve.tensor_scalar(mnt[:], mnt[:], -0.5, 1.5, ALU.mult, ALU.add))
                ve.tensor_tensor(mrn[:], mrn[:], mnt[:], ALU.mult).then_inc(s_m_rms, 1)
                dve.wait_ge(s_m_rms, g + 1)
                if g > 0:
                    dve.wait_ge(s_m_stk, g)
                r = mrn[:].rearrange("p (t a h) -> p a t h", t=G, a=2)
                dve.wait_ge(s_m_qkg, g + 1)
                for a in range(2):
                    last = ve.tensor_tensor(nb[:, a].rearrange("p t (h d) -> p t h d", h=MH),
                                            mqkg[:, :, a * SW:(a + 1) * SW].rearrange("p t (h d) -> p t h d", h=MH),
                                            r[:, a].unsqueeze(3).to_broadcast([P, G, MH, HD]), ALU.mult)
                last.then_inc(s_m_normed, 1)

            def parts(g):
                if g > 0:
                    dve.wait_ge(s_m_KT, G * g)
                else:
                    dve.wait_ge(s_stk_zero, 2)
                dve.wait_ge(s_m_weighted, g + 1)
                dve.wait_ge(s_m_qkg_used, g + 1)
                rest = nb[:].rearrange("p a t (h d) -> p (a t h) d", h=MH)
                slots = stk[:].rearrange("p a t h s d -> p (a t h) s d")
                ve.tensor_copy(slots[:, :, 5, :], rest).then_inc(s_m_part, 1)
                dve.wait_ge(s_m_part, 3 * g + 1)
                link(ve.tensor_tensor(rest, rest, slots[:, :, 5, :], ALU.subtract))
                ve.tensor_copy(slots[:, :, 2, :], rest).then_inc(s_m_part, 1)
                dve.wait_ge(s_m_part, 3 * g + 2)
                ve.tensor_tensor(rest, rest, slots[:, :, 2, :], ALU.subtract).then_inc(s_m_part, 1)

            def k_stack_ev(g):
                dve.wait_ge(s_kz_zero, g + 1)
                for t in range(G):
                    k = G * g + t
                    dve.wait_ge(s_m_KT, k + 1)
                    src = psum[2 + t % 2].bitcast(bf16).rearrange("p (c t) -> p c t", c=MH // 2)
                    kzv = kz[:, :, k * P:(k + 1) * P].rearrange("p (c a) t -> p a c t", a=2)
                    ve.tensor_copy(kzv[0:64, 0], src[0:64])
                    ve.tensor_copy(kzv[64:128, 1], src[64:128]).then_inc(s_m_kz, 1)

            mean_square(0)
            normalise(0)
            for g in range(NG):
                if g + 1 < NG:
                    mean_square(g + 1)
                parts(g)
                if g + 1 < NG:
                    normalise(g + 1)
                k_stack_ev(g)
            for ev, n in sched:
                if ev == "A":
                    ch, k, h, c = a_units[n]
                    w = min(512, P * (k + 1) - 512 * c)
                    dve.wait_ge(s_a_score, n + 1)
                    ve.tensor_reduce(mpart[:, 4 * CH[ch][0] + h, k, c:c + 1], ring_bank[ev, n][:, 0:w], AX.X, ALU.max).then_inc(s_a_max, 1)
                elif ev == "P":
                    g, q = CH[n]
                    dve.wait_ge(s_a_max, max(i for i, u in enumerate(a_units) if u[0] == n) + 1)
                    nx = nmx[:, n % 2]
                    link(ve.tensor_reduce(nx.rearrange("p a t c -> p c a t"), mpart[:, 4 * g:4 * g + 4, 4 * q:4 * q + 4, 0:q + 1].rearrange("p (c a) t n -> p c a t n", a=2),
                                          AX.X, ALU.max, negate=True))
                    if n == 0:
                        dve.wait_ge(s_mst_zero, 1)
                    if n > 3:
                        dve.wait_ge(s_m_mT, n - 3)
                    dst = mst[:, n % 4].rearrange("p t c (a r) -> p a t c r", a=2)[:, :, :, :, 8 * MS:8 * MS + 3]
                    link(ve.tensor_copy(dst[:, :, :, :, 0], nx))
                    link(ve.tensor_tensor(mr1[:], nx, dst[:, :, :, :, 0], ALU.subtract))
                    link(ve.tensor_copy(dst[:, :, :, :, 1], mr1[:]))
                    link(ve.tensor_tensor(mr1[:], mr1[:], dst[:, :, :, :, 1], ALU.subtract))
                    ve.tensor_copy(dst[:, :, :, :, 2], mr1[:]).then_inc(s_m_parts, 1)
                elif ev == "C":
                    hg, q = CH[n]
                    dve.wait_ge(s_c_T, n + 1)
                    src = ring_bank[ev, n].rearrange("p (t h c) -> p t h c", t=G, h=4)
                    link(ve.reciprocal(rden[:], src[:, :, :, HD]))
                    link(ve.tensor_tensor(cO[:].rearrange("p (t h d) -> p t h d", t=G, h=4), src[:, :, :, 0:HD],
                                          rden[:].unsqueeze(3).to_broadcast([P, G, 4, HD]), ALU.mult))
                    xt = xm[:, G * q:G * (q + 1), 4 * HD * hg:4 * HD * (hg + 1)]
                    ve.tensor_tensor(xt, xt, cO[:].rearrange("p (t d) -> p t d", t=G), ALU.add).then_inc(s_c_out, 1)
                    i = n - NQ * (MG - 1)
                    if i >= 0:
                        dve.wait_ge(s_c_out, n + 1)
                        ln_stats(2 * NG + i, q)
                        if i > 0:
                            ln_apply(2 * NG + i - 1, CH[n - 1][1])
                        if i < NQ - 1:
                            dve.wait_ge(s_rot_in, 32)
                            tables(DEPTH, range(i * T // (NQ - 1), (i + 1) * T // (NQ - 1)))
            ve.memset(tick[:], 0.0).then_inc(s_mla_done, 1)
            ln_apply(3 * NG - 1, CH[-1][1])
            for L in range(DEPTH, NL):
                layer(L)

        @block.tensor
        def _(pe):
            te = nc.tensor

            def attend(L, k):
                i = k + 2
                K, Ki = T * L + k, T * L + i
                if 0 <= k < T:
                    pe.wait_ge(s_q_Tev, K + 1)
                    pe.wait_ge(s_k_Tev, K + 1)
                    if k == 0:
                        pe.wait_ge(s_no_keys, L + 1)
                    u = k % 2
                    for w in range(2):
                        if w and i < T:
                            pe.wait_ge(s_h_T, Ki + 1)
                        mask = wmask[:, 1 if w else (2 if k == 0 else 0), :].unsqueeze(1).to_broadcast([P, PAIRS, P])
                        te.matmul(psum[5 + w], identb[:], mask, start=True, stop=False, skip_group_check=True)
                        for p in range(PAIRS):
                            flat = kring[:, p].rearrange("p h s q -> p (h s) q")
                            keys = flat[:, u:u + 3:2, :] if w else (flat[:, 0:4:3, :] if u == 0 else flat[:, 1:3, :])
                            last = te.matmul(psum[5 + w][:, p * P:(p + 1) * P], qbd[:, p, w, :], keys, start=False, stop=True, skip_group_check=True)
                        last.then_inc(s_score, 1)
                if 1 <= k:
                    if K == 1:
                        pe.wait_ge(s_weights_in, NWEIGHT)
                    pe.wait_ge(s_o_ev0, K)
                    pe.wait_ge(s_o_ev1, K)
                    for p in range(PAIRS):
                        last = te.matmul(psum[7][:, 0:DIM], oT[:, (k - 1) % 2, p, :], wo[:, L % DEPTH, p, :], start=p == 0, stop=p == PAIRS - 1)
                    last.then_inc(s_proj, 1)
                if 0 <= k + 1 < T:
                    if K + 1 > 0:
                        pe.wait_ge(s_v_ev, K + 1)
                    if k + 1 == 0 and L % DEPTH:
                        pe.wait_ge(s_ff_hid, HC * NG * L)
                        pe.wait_ge(s_ff_gelu, HC * NG * L)
                    te.matmul(psum[2], hT[:, (k + 1) % 2, 0:P], wqkv[:, L % DEPTH, 2 * INNER:3 * INNER], start=True, stop=True).then_inc(s_v, 1)
                if 0 <= i < T:
                    pe.wait_ge(s_h_T, Ki + 1)
                    if Ki > 0:
                        pe.wait_ge(s_rope_terms, 2 * Ki)
                    if i == 0 and L % DEPTH:
                        pe.wait_ge(s_h_right, NG * L)
                        pe.wait_ge(s_hn_Tev, NG * L)
                    for c in range(2):
                        te.matmul(psum[c], hT[:, i % 2, 0:P], wqkv[:, L % DEPTH, c * INNER:(c + 1) * INNER], start=True, stop=True).then_inc(s_qk, 1)
                if i == T:
                    shift_h(L, 0)
                if i == T + 1:
                    norm_T(L, 0)
                    shift_h(L, 1)
                if 0 <= k < T:
                    pe.wait_ge(s_p_norm, 2 * K + 1)
                    for p in range(PAIRS):
                        last = te.transpose(psum[5][:, p * P:(p + 1) * P], prob[:, 0, p, :], ident[:])
                    last.then_inc(s_prob_T, 1)
                if 0 <= k + 1 < T:
                    pe.wait_ge(s_q_scaled, K + 2)
                    if K > 0:
                        pe.wait_ge(s_attn_add, K)
                    if k + 1 == 0 and L % DEPTH:
                        pe.wait_ge(s_ff_out, NG * L)
                    for p in range(PAIRS):
                        last = te.transpose(psum[7][:, p * P:(p + 1) * P], qk[:, p * P:(p + 1) * P], ident[:])
                    last.then_inc(s_q_T, 1)
                if 0 <= k < T:
                    pe.wait_ge(s_p_norm, 2 * K + 2)
                    for p in range(PAIRS):
                        last = te.transpose(psum[6][:, p * P:(p + 1) * P], prob[:, 1, p, :], ident[:])
                    last.then_inc(s_prob_T, 1)
                if 0 <= k + 1 < T:
                    pe.wait_ge(s_k_scaled, K + 2)
                    if K >= 0:
                        pe.wait_ge(s_prob_Tev, 2 * K + 1)
                    for p in range(PAIRS):
                        last = te.transpose(psum[5][:, p * P:(p + 1) * P], qk[:, INNER + p * P:INNER + (p + 1) * P], ident[:])
                    last.then_inc(s_k_T, 1)
                if 0 <= k < T:
                    pe.wait_ge(s_prob_Tev, 2 * K + 1)
                    pe.wait_ge(s_v_ev, K + 1)
                    for h in range(HEADS):
                        rows = slice(DH * (h % 2), DH * (h % 2) + DH)
                        last = te.matmul(psum[3][rows, h // 2 * WIN:(h // 2 + 1) * WIN], vm[:, k % 2, h * DH:(h + 1) * DH], pT[:, 0, h // 2, rows],
                                         start=True, stop=True, skip_group_check=True)
                    last.then_inc(s_pv0, 1)
                if 0 <= k < T:
                    pe.wait_ge(s_prob_Tev, 2 * K + 2)
                    for h in range(HEADS):
                        rows = slice(DH * (h % 2), DH * (h % 2) + DH)
                        last = te.matmul(psum[4][rows, h // 2 * WIN:(h // 2 + 1) * WIN], va[:, k % 2, h * DH:(h + 1) * DH], pT[:, 1, h // 2, rows],
                                         start=True, stop=True, skip_group_check=True)
                    last.then_inc(s_pv1, 1)
                if 0 <= i + 1 < T:
                    g = (i + 1) // G
                    if L == 0:
                        pe.wait_ge(s_ln_done, g + 1)
                    elif L == DEPTH:
                        pe.wait_ge(s_mla_done, 1)
                        pe.wait_ge(s_ln_done, 3 * NG)
                    else:
                        pe.wait_ge(s_ff_out, NG * (L - 1) + g + 1)
                    if Ki + 1 > 0:
                        pe.wait_ge(s_h_T, Ki + 1)
                    te.transpose(psum[6][:, 0:P], xa[L % 2][:, i + 2, :], ident[:]).then_inc(s_x_T, 1)

            def shift_h(L, g):
                Gk = NG * L + g
                x_in = xa[L % 2]
                pe.wait_ge(s_attn_add, T * L + G * (g + 1))
                if Gk > 0:
                    pe.wait_ge(s_h_right, Gk)
                if g == 0:
                    pe.wait_ge(s_rope_terms, 2 * T * (L + 1) - 1)
                for f in range(2):
                    last = te.matmul(psum[0][:, 0:G * 64], shift[:, f], x_in[:, 1 + G * g - f:1 + G * (g + 1) - f, 64:128], start=f == 0, stop=f == 1)
                last.then_inc(s_h_shift, 1)

            def norm_T(L, g):
                Gk = NG * L + g
                pe.wait_ge(s_h_norm, Gk + 1)
                if Gk > 0:
                    pe.wait_ge(s_hn_Tev, Gk)
                if g == 0:
                    pe.wait_ge(s_rope_terms, 2 * T * (L + 1))
                for t in range(G):
                    last = te.transpose(psum[1][:, t * P:(t + 1) * P], hn[:, g % 2, t, :], ident[:])
                last.then_inc(s_hn_T, 1)

            def up(L, g, h):
                u = HC * (NG * L + g) + h
                b = 2 + 2 * (u % 2)
                if u > 1:
                    pe.wait_ge(s_ff_gelu, u - 1)
                te.matmul(psum[b], w1[:, L % DEPTH, HT_ + h * P:HT_ + (h + 1) * P], hnT[:, g % 2], start=True, stop=True).then_inc(s_ff_up, 1)
                if u > 1:
                    pe.wait_ge(s_ff_hid, u - 1)
                te.matmul(psum[b + 1], w1[:, L % DEPTH, h * P:(h + 1) * P], hnT[:, g % 2], start=True, stop=True).then_inc(s_ff_up, 1)

            def down(L, g):
                Gk = NG * L + g
                pe.wait_ge(s_ff_hid, HC * (Gk + 1))
                if Gk > 0:
                    pe.wait_ge(s_ff_out, Gk)
                for t in range(G):
                    for h in range(HC):
                        last = te.matmul(psum[7][:, t * P:(t + 1) * P], hid[:, h, t * P:(t + 1) * P], w2[:, L % DEPTH, h, :], start=h == 0, stop=h == HC - 1)
                last.then_inc(s_ff_down, 1)

            def layer(L):
                for k in range(-3 if L == DEPTH else -1, T + 1):
                    attend(L, k)
                ahead = (L + 1) % DEPTH
                pe.wait_ge(s_v_ev, T * (L + 1))
                pe.wait_ge(s_o_ev0, T * (L + 1))
                pe.wait_ge(s_o_ev1, T * (L + 1))
                pe.wait_ge(s_k_Tev, T * (L + 1))
                pe.wait_ge(s_prob_Tev, 2 * T * (L + 1))
                for g in range(NG):
                    pe.wait_ge(s_hn_Tev, NG * L + g + 1)
                    up(L, g, 0)
                    if g == 0:
                        pe.wait_ge(s_attn_add, T * (L + 1))
                    else:
                        down(L, g - 1)
                    if g + 1 < NG:
                        norm_T(L, g + 1)
                    elif ahead:
                        attend(L + 1, -3)
                    up(L, g, 1)
                    if g + 2 < NG:
                        shift_h(L, g + 2)
                    for h in range(2, HC):
                        up(L, g, h)
                if ahead:
                    attend(L + 1, -2)
                down(L, NG - 1)
                if not ahead:
                    pe.wait_ge(s_ff_out, NG * (L + 1))

            pe.wait_ge(s_all_in, 1)
            attend(0, -3)
            attend(0, -2)
            UQ, DQ, UK, DKV, QR, KR, UV, WO = range(8)
            te.matmul(psum[3][:, 0:P], bdw[:, UV, :], bdw[:, WO, :], start=True, stop=True).then_inc(s_bd_u, 1)
            te.matmul(psum[4][:, 0:P], bdw[:, DQ, :], bdw[:, UQ, :], start=True, stop=True)
            te.matmul(psum[4][:, P:2 * P], bdw[:, DKV, :], bdw[:, UK, :], start=True, stop=True)
            te.matmul(psum[4][:, 2 * P:3 * P], bdw[:, KR, :], bdw[:, QR, :], start=True, stop=True)
            pe.wait_ge(s_bd_uev, 1)
            te.matmul(psum[4][:, 3 * P:], bdw[:, DKV, :], bdu, start=True, stop=True).then_inc(s_bd_prod, 1)
            pe.wait_ge(s_bd_ready, 1)
            for L in range(DEPTH):
                layer(L)
            pe.wait_ge(s_mla_free, 1)

            def y_T(g):
                pe.wait_ge(s_ln_done, NG + g + 1)
                if g > 0:
                    pe.wait_ge(s_m_yTev, g)
                if g > 3:
                    pe.wait_ge(s_m_qst, G * (g - 3))
                for t in range(G):
                    last = te.transpose(psum[0][:, t * P:(t + 1) * P], xa[0][:, 1 + G * g + t, :], ident[:])
                last.then_inc(s_m_yT, 1)

            def project(g):
                pe.wait_ge(s_m_yTev, g + 1)
                if g > 0:
                    pe.wait_ge(s_m_qkg, g)
                for t in range(G):
                    last = te.matmul(psum[4 + t], yT[:, g % 2, t * P:(t + 1) * P], bd[:], start=True, stop=True)
                last.then_inc(s_m_proj, 1)

            def stack_T(g):
                pe.wait_ge(s_m_stk, g + 1)
                for t in range(G):
                    k = G * g + t
                    for a in range(2):
                        if a == 0 and k > 1:
                            pe.wait_ge(s_m_qst, k - 1)
                        if a == 0 and t == 1:
                            pe.wait_ge(s_m_yTev, min(g + 4, NG))
                        if a == 1 and k > 1:
                            pe.wait_ge(s_m_kz, k - 1)
                        bank = psum[(1 - t % 2) if a == 0 else 2 + t % 2].bitcast(bf16)
                        for c in range(MH // 2):
                            src = stk[:, a, t, 2 * c:2 * c + 2].rearrange("p h s d -> p (h s d)")
                            last = te.transpose(bank[:, c * P:(c + 1) * P], src, identb[:])
                        last.then_inc(s_m_KT if a else s_m_QT, 1)

            y_T(0)
            project(0)
            y_T(1)
            project(1)
            y_T(2)
            for g in range(NG):
                if g + 2 < NG:
                    project(g + 2)
                if g + 3 < NG:
                    y_T(g + 3)
                stack_T(g)
            pe.wait_ge(s_m_qst, T)
            pe.wait_ge(s_m_kz, T)
            for ev, n in sched:
                if ev in "AMC":
                    before, m = ring_before[ev, n]
                    if before == "A":
                        pe.wait_ge(s_a_max, m + 1)
                    elif before == "M":
                        pe.wait_ge(s_m_mrow, m + 1)
                    elif before == "C":
                        pe.wait_ge(s_c_out, m + 1)
                    bank = ring_bank[ev, n]
                if ev == "A":
                    ch, k, h, c = a_units[n]
                    hd = 4 * CH[ch][0] + h
                    w = min(512, P * (k + 1) - 512 * c)
                    diag = c == k // 4
                    ins = te.matmul(bank[:, 0:w], qst[:, hd // 2, k * P:(k + 1) * P], kz[:, hd, 512 * c:512 * c + w],
                                    start=True, stop=not diag, skip_group_check=True)
                    if diag:
                        ins = te.matmul(bank[:, w - P:w], identb[:], cmask[:, 0, :], start=False, stop=True, skip_group_check=True)
                    ins.then_inc(s_a_score, 1)
                elif ev == "M":
                    pe.wait_ge(s_m_parts, n + 1)
                    for t in range(G):
                        for c in range(2):
                            last = te.transpose(bank.bitcast(bf16)[:, (2 * t + c) * P:(2 * t + c + 1) * P],
                                                mst[:, n % 4, t, c, :], identb[:])
                    last.then_inc(s_m_mT, 1)
                elif ev == "S":
                    ch, j, hp = s_units[n]
                    g, q = CH[ch]
                    lo = max(0, P * (j - 4 * q))
                    if j == 0:
                        pe.wait_ge(s_m_mrow, ch + 1)
                    if n > 1:
                        pe.wait_ge(s_b_exp, n - 1)
                    for h2 in range(2):
                        hd = 4 * g + 2 * hp + h2
                        score = psum[psB[n % 2] + h2]
                        diag = j >= 4 * q
                        last = te.matmul(score[:, 0:512 - lo], kz[:, hd, j * P:(j + 1) * P], qst[:, hd // 2, 512 * q + lo:512 * (q + 1)],
                                         start=True, stop=not diag, skip_group_check=True)
                        if diag:
                            last = te.matmul(score[:, 0:P], identb[:], cmask[:, 1, :], start=False, stop=True, skip_group_check=True)
                    last.then_inc(s_b_score, 1)
                elif ev == "V":
                    ch, j, hp = s_units[n]
                    g, q = CH[ch]
                    lo = max(0, P * (j - 4 * q))
                    pe.wait_ge(s_b_exp, n + 1)
                    if j == 0:
                        if ch > 0:
                            pe.wait_ge(s_c_ev, ch)
                        pe.wait_ge(s_c_zero, 1)
                        pe.wait_ge(s_v_one, 1)
                    for h in (2 * hp, 2 * hp + 1):
                        last = te.matmul(psum[BC][32 * h:32 * h + VW, lo:512], vv[:, j, 4 * g + h, :],
                                         pb[:, n % 4, h % 2, 0:512 - lo],
                                         start=j == 0, stop=j == 4 * q + 3, skip_group_check=True)
                    last.then_inc(s_b_pv, 1)
                elif ev == "C":
                    pe.wait_ge(s_c_ev, n + 1)
                    for t in range(G):
                        last = te.transpose(bank[:, t * P:(t + 1) * P], cT[:, t * P:(t + 1) * P], ident[:])
                    last.then_inc(s_c_T, 1)
            pe.wait_ge(s_c_out, 16)
            for L in range(DEPTH, NL):
                layer(L)


_DATA = ['L0_attn_x', 'L0_ffn_wqkv', 'L0_ffn_q_scale', 'L0_ffn_k_scale', 'L0_ffn_wo', 'L0_ffn_ln_g', 'L0_ffn_ln_b',
         'L0_ffn_w1', 'L0_ffn_b1', 'L0_ffn_w2', 'L0_ffn_b2']


def constants(ntok):
    P, DH, WIN, HEADS = 128, 64, 64, 8
    T = ntok // P
    c = {"c_ident": np.eye(P, dtype=np.float32)}
    sh = np.zeros((P, 2, P), np.float32)
    sh[np.arange(P - 1), 0, np.arange(1, P)] = 1
    sh[P - 1, 1, 0] = 1
    c["c_shift"] = sh
    q = np.arange(P)[:, None] % WIN
    k = np.arange(P)[None, :]
    even = np.where(k < WIN, k <= q, k >= q + WIN)
    odd = (k >= q) & (k <= q + WIN)
    first = (k < WIN) & (k <= q)
    BIG = np.float32(-1e30)
    a = np.arange(P)
    by_query, by_key = a[None, :] <= a[:, None], a[:, None] <= a[None, :]
    c["c_masks"] = np.stack([np.where(m, np.float32(0), BIG) for m in (even, odd, first, by_query, by_key)], 1)
    c["c_bdmask"] = (a[:, None] // 8 == a[None, :] // 8).astype(np.float32)
    half = np.arange(0, DH, 2, dtype=np.float32)
    inv = (1.0 / np.float32(10000.0) ** (half / np.float32(DH))).astype(np.float32)
    t = np.arange(ntok, dtype=np.float32)
    fr = (t[:, None] * inv[None, :]).astype(np.float32)
    fr = np.concatenate([fr, fr], 1).astype(np.float64)
    base = ((half + np.float32(0.4 * DH)) / np.float32(1.4 * DH)).astype(np.float32)
    power = ((t - ntok // 2) / np.float32(WIN // 2)).astype(np.float32)
    sc = base[None, :].astype(np.float64) ** power[:, None].astype(np.float64)
    sc = np.concatenate([sc, sc], 1)
    cos, sin = np.cos(fr), np.sin(fr)
    sin[:, :DH // 2] *= -1
    rot = np.stack([np.stack([cos * sc * 8.0, cos / sc], 1), np.stack([sin * sc * 8.0, sin / sc], 1)], 1)
    c["c_rot"] = rot.reshape(T, P, 2, 2, DH).transpose(1, 0, 2, 3, 4).astype(np.float32)
    return c


def kernel(**inputs):
    import concourse.bacc as _bacc
    from concourse.bass_utils import run_bass_kernel_spmd as _run

    nc = _bacc.Bacc("TRN2", target_bir_lowering=False, num_devices=1)
    a = {n: np.ascontiguousarray(inputs[n]) for n in _DATA}
    a.update(constants(a["L0_attn_x"].shape[1]))
    g = {n: np.asarray(inputs["L0_attn_" + n]) for n in ("W_DQ", "W_UQ", "W_DKV", "W_UKV", "W_QR", "W_KR", "W_O", "q_norm_w", "k_norm_w")}

    def factor(w, heads):
        w = np.tile(w, (1, heads))
        out = np.zeros((128, 128), w.dtype)
        out[:w.shape[0], :w.shape[1]] = w
        return out

    a["m_factors"] = np.stack([factor(g["W_UQ"].T, 16), factor(g["W_DQ"], 16), factor(g["W_UKV"][:8].T, 16), factor(g["W_DKV"], 16),
                               factor(g["W_QR"], 16), factor(g["W_KR"], 16), factor(g["W_UKV"][8:], 1), factor(g["W_O"].T, 16)])
    a["m_qn"] = np.tile(g["q_norm_w"], 16)
    a["m_kn"] = np.tile(g["k_norm_w"], 16)
    arrays, I = {}, {}
    for name, v in a.items():
        v = np.ascontiguousarray(v)
        arrays[name] = v
        I[name] = nc.dram_tensor(name, v.shape, mybir.dt.from_np(v.dtype), kind="ExternalInput").ap()
    out = nc.dram_tensor("out", a["L0_attn_x"].shape, mybir.dt.float32, kind="ExternalOutput").ap()
    macaron_kernel(nc, I, out)
    r = _run(nc, [arrays], core_ids=[0])
    return r.results[0]["out"]
```
